# Optimizing a Trainium2 kernel written in Bass

```python
import numpy as np
import jax
import jax.numpy as jnp

def _softmax(x, axis=-1):
    return jax.nn.softmax(x, axis=axis)

def _gelu(x):
    return jax.nn.gelu(x, approximate=True)

def _silu(x):
    return jax.nn.silu(x)

def _sigmoid(x):
    return jax.nn.sigmoid(x)

def _layernorm(x, axis=-1, eps=1e-05):
    m = jnp.mean(x, axis=axis, keepdims=True)
    v = jnp.var(x, axis=axis, keepdims=True)
    return (x - m) / jnp.sqrt(v + eps)

def _scatter_add(tgt, idx, src, axis=0):
    return tgt.at[idx].add(src)

def _segment_sum(src, seg, n):
    return jax.ops.segment_sum(src, seg, n)
kernel_name = 'mk_decoder_postln_d4_seqx_r8_a91ebd'

def setup_inputs(seed: int=0):
    np.random.seed(seed)
    _w = jnp.asarray

    def _rec_inputs():
        import jax
        import jax.numpy as jnp
        _rk = jax.random.key(seed)
        x = -0.0002928 + 1 * jax.random.normal(jax.random.fold_in(_rk, 1), (32, 128, 128), jnp.float32)
        _lenS = 128 - jax.random.randint(jax.random.fold_in(_rk, 7), (32,), 0, max(1, 128 // 4) + 1, jnp.int32)
        _lenS2 = 128 - jax.random.randint(jax.random.fold_in(_rk, 8), (32,), 0, max(1, 128 // 4) + 1, jnp.int32)
        _ctx_512P = jax.random.normal(jax.random.fold_in(_rk, 11), (32, 16, 64), jnp.float32)
        _ctx_512c = jax.random.dirichlet(jax.random.fold_in(_rk, 511), 0.3 * jnp.ones((16,), jnp.float32), (32, 128))
        _ctx_512t = jnp.einsum('bsk,bkd->bsd', _ctx_512c, _ctx_512P)
        _ctx_512t = _ctx_512t * jax.lax.rsqrt(jnp.mean(jnp.square(_ctx_512t)) + 1e-12) * 0.953939
        ctx_512 = 0.00222621 + 0.99962 * (_ctx_512t + 0.3 * jax.random.normal(jax.random.fold_in(_rk, 611), (32, 128, 64), jnp.float32))
        return (x, ctx_512)
    x, ctx_512 = _rec_inputs()

    def _L0_attn_setup():
        import jax, jax.numpy as jnp
        import numpy as np
        import math
        D_MODEL = 128
        N_HEADS = 16
        D_HEAD = D_MODEL // N_HEADS
        WINDOW = 32
        SCALE = 1.0 / math.sqrt(D_HEAD)

        def _window_mask(seq_len: int) -> jnp.ndarray:
            i = jnp.arange(seq_len)[:, None]
            j = jnp.arange(seq_len)[None, :]
            allowed = (j <= i) & (j > i - WINDOW)
            return jnp.where(allowed, 0.0, -jnp.inf).astype(jnp.float32)
        key = jax.random.key(seed)
        kx, kqkv, kout = jax.random.split(key, 3)
        x = jax.random.normal(kx, (2, 256, D_MODEL), dtype=jnp.float32)
        lim_qkv = math.sqrt(6.0 / (D_MODEL + 3 * D_MODEL))
        W_qkv = jax.random.uniform(kqkv, (D_MODEL, 3 * D_MODEL), dtype=jnp.float32, minval=-lim_qkv, maxval=lim_qkv)
        lim_out = math.sqrt(6.0 / (D_MODEL + D_MODEL))
        W_out = jax.random.uniform(kout, (D_MODEL, D_MODEL), dtype=jnp.float32, minval=-lim_out, maxval=lim_out)
        return {'x': x, 'W_qkv': W_qkv, 'W_out': W_out}
    _L0_attn_all = _L0_attn_setup()
    _L0_attn_in = {k: v for k, v in _L0_attn_all.items() if k in ('W_qkv', 'W_out')}
    del _L0_attn_all

    def _L0_xattn_setup():
        import jax, jax.numpy as jnp
        import numpy as np
        H, D, C1, C2, S, M, B, W = (16, 32, 128, 64, 256, 64, 2, 4)

        def _ln(x, g, b):
            m = jnp.mean(x, -1, keepdims=True)
            v = jnp.var(x, -1, keepdims=True)
            return (x - m) * jax.lax.rsqrt(v + 1e-05) * g + b

        def _mha(x, y, wq, wk, wv, li1_w, li1_b, lnx_g, lnx_b, lny_g, lny_b, ln3_g, ln3_b, li2_w, li2_b, li3_w, li3_b, causal):
            xn = _ln(x, lnx_g, lnx_b)
            yn = _ln(y, lny_g, lny_b)
            q = jnp.einsum('bsc,hcd->bhsd', xn, wq)
            k = jnp.einsum('btc,hcd->bhtd', yn, wk)
            v = jnp.einsum('btc,hcd->bhtd', yn, wv)
            a = jax.nn.softmax(jnp.einsum('bhsd,bhtd->bhst', q, k) * D ** (-0.5), axis=-1)
            if causal:
                s, t = (a.shape[-2], a.shape[-1])
                mask = (jnp.arange(t)[None, :] > jnp.arange(s)[:, None]).astype(a.dtype)
                a = a * mask
            o = jnp.einsum('bhst,bhtd->bhsd', a, v)
            o = o.transpose(0, 2, 1, 3).reshape(x.shape[0], x.shape[1], H * D)
            x_out = x + o @ li1_w + li1_b
            h = jax.nn.gelu(_ln(x_out, ln3_g, ln3_b) @ li2_w + li2_b, approximate=False)
            return x_out + h @ li3_w + li3_b
        key = jax.random.key(seed)
        ks = iter(jax.random.split(key, 64))

        def w(shape, scale=0.02):
            return jax.random.normal(next(ks), shape, jnp.float32) * scale
        inp = {'xx': jax.random.normal(next(ks), (B, S, C1), jnp.float32), 'ee': jax.random.normal(next(ks), (B, M, C2), jnp.float32), 'ln1_g': jnp.ones(C1, jnp.float32), 'ln1_b': jnp.zeros(C1, jnp.float32), 'ln2_g': jnp.ones(C1, jnp.float32), 'ln2_b': jnp.zeros(C1, jnp.float32)}
        for pfx, cy in (('a1', C1), ('a2', C2)):
            inp[pfx + '_wq'] = w((H, C1, D))
            inp[pfx + '_wk'] = w((H, cy, D))
            inp[pfx + '_wv'] = w((H, cy, D))
            inp[pfx + '_li1_w'] = w((H * D, C1))
            inp[pfx + '_li1_b'] = jnp.zeros(C1, jnp.float32)
            inp[pfx + '_lnx_g'] = jnp.ones(C1, jnp.float32)
            inp[pfx + '_lnx_b'] = jnp.zeros(C1, jnp.float32)
            inp[pfx + '_lny_g'] = jnp.ones(cy, jnp.float32)
            inp[pfx + '_lny_b'] = jnp.zeros(cy, jnp.float32)
            inp[pfx + '_ln3_g'] = jnp.ones(C1, jnp.float32)
            inp[pfx + '_ln3_b'] = jnp.zeros(C1, jnp.float32)
            inp[pfx + '_li2_w'] = w((C1, C1 * W))
            inp[pfx + '_li2_b'] = jnp.zeros(C1 * W, jnp.float32)
            inp[pfx + '_li3_w'] = w((C1 * W, C1))
            inp[pfx + '_li3_b'] = jnp.zeros(C1, jnp.float32)
        inp['training'] = 0
        return inp
    _L0_xattn_all = _L0_xattn_setup()
    _L0_xattn_in = {k: v for k, v in _L0_xattn_all.items() if k in ('ln1_g', 'ln1_b', 'ln2_g', 'ln2_b', 'a1_wq', 'a1_wk', 'a1_wv', 'a1_li1_w', 'a1_li1_b', 'a1_lnx_g', 'a1_lnx_b', 'a1_lny_g', 'a1_lny_b', 'a1_ln3_g', 'a1_ln3_b', 'a1_li2_w', 'a1_li2_b', 'a1_li3_w', 'a1_li3_b', 'a2_wq', 'a2_wk', 'a2_wv', 'a2_li1_w', 'a2_li1_b', 'a2_lnx_g', 'a2_lnx_b', 'a2_lny_g', 'a2_lny_b', 'a2_ln3_g', 'a2_ln3_b', 'a2_li2_w', 'a2_li2_b', 'a2_li3_w', 'a2_li3_b')}
    del _L0_xattn_all

    def _L0_ffn_setup():
        import jax, jax.numpy as jnp
        import numpy as np
        HIDDEN_SIZE = 128
        NUM_EXPERTS = 8
        MOE_INTERMEDIATE_SIZE = 176
        NUM_EXPERTS_PER_TOK = 2
        SHARED_EXPERT_INTERMEDIATE_SIZE = 352
        B, T = (2, 128)
        W_SCALE = 0.02
        key = jax.random.key(seed)
        ks = jax.random.split(key, 8)
        H, E, I, SI = (HIDDEN_SIZE, NUM_EXPERTS, MOE_INTERMEDIATE_SIZE, SHARED_EXPERT_INTERMEDIATE_SIZE)
        return {'x': jax.random.normal(ks[0], (B, T, H), jnp.float32), 'gate_w': jax.random.normal(ks[1], (E, H), jnp.float32) * W_SCALE, 'experts_gate_up': jax.random.normal(ks[2], (E, 2 * I, H), jnp.float32) * W_SCALE, 'experts_down': jax.random.normal(ks[3], (E, H, I), jnp.float32) * W_SCALE, 'shared_gate_w': jax.random.normal(ks[4], (SI, H), jnp.float32) * W_SCALE, 'shared_up_w': jax.random.normal(ks[5], (SI, H), jnp.float32) * W_SCALE, 'shared_down_w': jax.random.normal(ks[6], (H, SI), jnp.float32) * W_SCALE, 'shared_expert_gate_w': jax.random.normal(ks[7], (1, H), jnp.float32) * W_SCALE}
    _L0_ffn_all = _L0_ffn_setup()
    _L0_ffn_in = {k: v for k, v in _L0_ffn_all.items() if k in ('gate_w', 'experts_gate_up', 'experts_down', 'shared_gate_w', 'shared_up_w', 'shared_down_w', 'shared_expert_gate_w')}
    del _L0_ffn_all

    def _L1_attn_setup():
        import jax, jax.numpy as jnp
        import numpy as np
        import math
        B, T, C, H = (4, 256, 128, 16)
        EPS = 1e-10

        def layernorm(x):
            mean = jnp.mean(x, axis=-1, keepdims=True)
            xmu = x - mean
            var = jnp.mean(xmu * xmu, axis=-1, keepdims=True)
            return xmu / jnp.sqrt(var + EPS)

        def new_gelu(x):
            c = math.sqrt(2.0 / math.pi)
            return 0.5 * x * (1.0 + jnp.tanh(c * (x + 0.044715 * x * x * x)))

        def attention(x, w_attn, b_attn, w_proj, b_proj):
            b, t, cdim = x.shape
            d = cdim // H
            ca = x @ w_attn.T + b_attn
            q, k, v = jnp.split(ca, 3, axis=2)
            q = q.reshape(b, t, H, d)
            k = k.reshape(b, t, H, d)
            v = v.reshape(b, t, H, d)
            att = jnp.einsum('bthd,bshd->bhts', q, k) * (1.0 / math.sqrt(d))
            mask = jnp.tril(jnp.ones((t, t), dtype=bool))
            att = jnp.where(mask, att, -jnp.inf)
            att = jax.nn.softmax(att, axis=-1)
            y = jnp.einsum('bhts,bshd->bthd', att, v).reshape(b, t, cdim)
            return y @ w_proj.T + b_proj
        key = jax.random.key(seed)
        ks = jax.random.split(key, 9)
        s = 0.02
        return {'x': jax.random.normal(ks[0], (B, T, C), jnp.float32), 'w_attn': jax.random.normal(ks[1], (3 * C, C), jnp.float32) * s, 'b_attn': jax.random.normal(ks[2], (3 * C,), jnp.float32) * s, 'w_proj': jax.random.normal(ks[3], (C, C), jnp.float32) * s, 'b_proj': jax.random.normal(ks[4], (C,), jnp.float32) * s, 'w_fc': jax.random.normal(ks[5], (4 * C, C), jnp.float32) * s, 'b_fc': jax.random.normal(ks[6], (4 * C,), jnp.float32) * s, 'w_mlp_proj': jax.random.normal(ks[7], (C, 4 * C), jnp.float32) * s, 'b_mlp_proj': jax.random.normal(ks[8], (C,), jnp.float32) * s}
    _L1_attn_all = _L1_attn_setup()
    _L1_attn_in = {k: v for k, v in _L1_attn_all.items() if k in ('w_attn', 'b_attn', 'w_proj', 'b_proj', 'w_fc', 'b_fc', 'w_mlp_proj', 'b_mlp_proj')}
    del _L1_attn_all

    def _L1_xattn_setup():
        import jax, jax.numpy as jnp
        import numpy as np
        NUM_HEADS = 16
        HEAD_DIM = 64
        Q_DIM = 128
        KV_DIM = 64
        INNER = NUM_HEADS * HEAD_DIM
        key = jax.random.key(seed)
        ks = jax.random.split(key, 7)
        B, N, M = (32, 128, 256)
        q = jax.random.normal(ks[0], (B, N, Q_DIM), dtype=jnp.float32)
        kv = jax.random.normal(ks[1], (B, M, KV_DIM), dtype=jnp.float32)
        Wq = jax.random.normal(ks[2], (Q_DIM, INNER), dtype=jnp.float32) / np.sqrt(Q_DIM)
        Wk = jax.random.normal(ks[3], (KV_DIM, INNER), dtype=jnp.float32) / np.sqrt(KV_DIM)
        Wv = jax.random.normal(ks[4], (KV_DIM, INNER), dtype=jnp.float32) / np.sqrt(KV_DIM)
        Wo = jax.random.normal(ks[5], (INNER, Q_DIM), dtype=jnp.float32) / np.sqrt(INNER)
        bo = jax.random.normal(ks[6], (Q_DIM,), dtype=jnp.float32) * 0.01
        return {'q': q, 'kv': kv, 'Wq': Wq, 'Wk': Wk, 'Wv': Wv, 'Wo': Wo, 'bo': bo}
    _L1_xattn_all = _L1_xattn_setup()
    _L1_xattn_in = {k: v for k, v in _L1_xattn_all.items() if k in ('Wq', 'Wk', 'Wv', 'Wo', 'bo')}
    del _L1_xattn_all

    def _L1_ffn_setup():
        import jax, jax.numpy as jnp
        import numpy as np
        E, K = (8, 2)
        DM, DE = (128, 352)
        B, S = (1, 256)
        EPS = 1e-06

        def _rmsnorm(x, w):
            var = jnp.mean(jnp.square(x), axis=-1, keepdims=True)
            return x * jax.lax.rsqrt(var + EPS) * w
        key = jax.random.key(seed)
        kx, kg, k1, k2, k3 = jax.random.split(key, 5)

        def kaiming_uniform(k, shape, fan_in):
            bound = 1.0 / np.sqrt(fan_in)
            return jax.random.uniform(k, shape, jnp.float32, -bound, bound)
        return {'x': jax.random.normal(kx, (B, S, DM), jnp.float32), 'gate_w': kaiming_uniform(kg, (E, DM), DM), 'rms_w': jnp.ones((DM,), jnp.float32), 'W1': kaiming_uniform(k1, (E, DE, DM), DE * DM), 'W2': kaiming_uniform(k2, (E, DE, DM), DE * DM), 'W3': kaiming_uniform(k3, (E, DM, DE), DM * DE)}
    _L1_ffn_all = _L1_ffn_setup()
    _L1_ffn_in = {k: v for k, v in _L1_ffn_all.items() if k in ('gate_w', 'rms_w', 'W1', 'W2', 'W3')}
    del _L1_ffn_all

    def _L2_attn_setup():
        import jax, jax.numpy as jnp
        import numpy as np
        B, L, D_MODEL = (4, 256, 128)
        N_HEADS, FEAT, HEAD_DIM = (16, 16, 64)
        CHUNK = 128
        EPS = 1e-12

        def taylor_exp(x):
            f = x.shape[-1]
            r2 = jnp.sqrt(jnp.asarray(2.0, x.dtype))
            rd = jnp.sqrt(jnp.asarray(float(f), x.dtype))
            rrd = jnp.sqrt(rd)
            x2 = (x[..., :, None] * x[..., None, :]).reshape(*x.shape[:-1], f * f) / r2
            ones = jnp.ones_like(x[..., :1])
            return jnp.concatenate([ones, x / rrd, x2 / rd], axis=-1)
        key = jax.random.key(seed)
        k1, k2, k3, k4, k5 = jax.random.split(key, 5)
        s = 0.02
        return {'hidden_states': jax.random.normal(k1, (B, L, D_MODEL), jnp.float32), 'Wq': jax.random.normal(k2, (N_HEADS * FEAT, D_MODEL), jnp.float32) * s, 'Wk': jax.random.normal(k3, (N_HEADS * FEAT, D_MODEL), jnp.float32) * s, 'Wv': jax.random.normal(k4, (N_HEADS * HEAD_DIM, D_MODEL), jnp.float32) * s, 'Wo': jax.random.normal(k5, (D_MODEL, N_HEADS * HEAD_DIM), jnp.float32) * s}
    _L2_attn_all = _L2_attn_setup()
    _L2_attn_in = {k: v for k, v in _L2_attn_all.items() if k in ('Wq', 'Wk', 'Wv', 'Wo')}
    del _L2_attn_all

    def _L2_xattn_setup():
        import jax, jax.numpy as jnp
        import numpy as np
        B, LQ, LK = (8, 256, 256)
        QD, KD, VD = (128, 64, 64)
        key = jax.random.key(seed)
        ks = jax.random.split(key, 9)
        s = 0.02
        return {'query': jax.random.normal(ks[0], (B, LQ, QD), jnp.float32), 'key': jax.random.normal(ks[1], (B, LK, KD), jnp.float32), 'value': jax.random.normal(ks[2], (B, LK, VD), jnp.float32), 'Wq': jax.random.normal(ks[3], (QD, QD), jnp.float32) * s, 'bq': jnp.zeros((QD,), jnp.float32), 'Wk': jax.random.normal(ks[4], (KD, QD), jnp.float32) * s, 'bk': jnp.zeros((QD,), jnp.float32), 'Wv': jax.random.normal(ks[5], (VD, QD), jnp.float32) * s, 'bv': jnp.zeros((QD,), jnp.float32)}
    _L2_xattn_all = _L2_xattn_setup()
    _L2_xattn_in = {k: v for k, v in _L2_xattn_all.items() if k in ('Wq', 'bq', 'Wk', 'bk', 'Wv', 'bv')}
    del _L2_xattn_all

    def _L2_ffn_setup():
        import jax, jax.numpy as jnp
        import numpy as np
        HIDDEN = 128
        INTER = 256
        NUM_EXPERTS = 8
        TOPK = 2
        STD = 0.02
        key = jax.random.key(seed)
        k1, k2, k3, k4 = jax.random.split(key, 4)
        return {'hidden_states': jax.random.normal(k1, (1, 256, HIDDEN), dtype=jnp.float32), 'w1': jax.random.normal(k2, (NUM_EXPERTS, 2 * INTER, HIDDEN), dtype=jnp.float32) * STD, 'w2': jax.random.normal(k3, (NUM_EXPERTS, HIDDEN, INTER), dtype=jnp.float32) * STD, 'router_w': jax.random.normal(k4, (NUM_EXPERTS, HIDDEN), dtype=jnp.float32) * STD}
    _L2_ffn_all = _L2_ffn_setup()
    _L2_ffn_in = {k: v for k, v in _L2_ffn_all.items() if k in ('w1', 'w2', 'router_w')}
    del _L2_ffn_all

    def _L3_attn_setup():
        import jax, jax.numpy as jnp
        import numpy as np
        B, S, E = (4, 512, 128)
        H = 16
        D = E // H
        N_SAMPLE = 128
        key = jax.random.key(seed)
        ks = jax.random.split(key, 7)
        lim = float(np.sqrt(6.0 / (E + E)))
        x = jax.random.normal(ks[0], (B, S, E), dtype=jnp.float32)
        Wq = jax.random.uniform(ks[1], (E, E), jnp.float32, -lim, lim)
        Wk = jax.random.uniform(ks[2], (E, E), jnp.float32, -lim, lim)
        Wv = jax.random.uniform(ks[3], (E, E), jnp.float32, -lim, lim)
        bq = jnp.zeros((E,), jnp.float32)
        bk = jnp.zeros((E,), jnp.float32)
        bv = jnp.zeros((E,), jnp.float32)
        return {'x': x, 'Wq': Wq, 'bq': bq, 'Wk': Wk, 'bk': bk, 'Wv': Wv, 'bv': bv}
    _L3_attn_all = _L3_attn_setup()
    _L3_attn_in = {k: v for k, v in _L3_attn_all.items() if k in ('Wq', 'bq', 'Wk', 'bk', 'Wv', 'bv')}
    del _L3_attn_all

    def _L3_xattn_setup():
        import jax, jax.numpy as jnp
        import numpy as np
        B, LQ, LK = (8, 256, 256)
        QD, KD, VD = (128, 64, 64)
        key = jax.random.key(seed)
        ks = jax.random.split(key, 9)
        s = 0.02
        return {'query': jax.random.normal(ks[0], (B, LQ, QD), jnp.float32), 'key': jax.random.normal(ks[1], (B, LK, KD), jnp.float32), 'value': jax.random.normal(ks[2], (B, LK, VD), jnp.float32), 'Wq': jax.random.normal(ks[3], (QD, QD), jnp.float32) * s, 'bq': jnp.zeros((QD,), jnp.float32), 'Wk': jax.random.normal(ks[4], (KD, QD), jnp.float32) * s, 'bk': jnp.zeros((QD,), jnp.float32), 'Wv': jax.random.normal(ks[5], (VD, QD), jnp.float32) * s, 'bv': jnp.zeros((QD,), jnp.float32)}
    _L3_xattn_all = _L3_xattn_setup()
    _L3_xattn_in = {k: v for k, v in _L3_xattn_all.items() if k in ('Wq', 'bq', 'Wk', 'bk', 'Wv', 'bv')}
    del _L3_xattn_all

    def _L3_ffn_setup():
        import jax, jax.numpy as jnp
        import numpy as np
        B, S, H, E, K = (4, 256, 128, 8, 2)
        key = jax.random.key(seed)
        k0, k1, k2, k3 = jax.random.split(key, 4)
        x = jax.random.normal(k0, (B, S, H), dtype=jnp.float32)
        router_w = jax.random.normal(k1, (E, H), dtype=jnp.float32) * np.float32(1.0 / np.sqrt(H))
        xav1 = np.float32(np.sqrt(2.0 / (2 * H + H)))
        w1 = jax.random.normal(k2, (E, 2 * H, H), dtype=jnp.float32) * xav1
        w2 = jax.random.normal(k3, (E, H, 2 * H), dtype=jnp.float32) * xav1
        return {'x': x, 'router_w': router_w, 'w1': w1, 'w2': w2}
    _L3_ffn_all = _L3_ffn_setup()
    _L3_ffn_in = {k: v for k, v in _L3_ffn_all.items() if k in ('router_w', 'w1', 'w2')}
    del _L3_ffn_all
    return {'x': x, 'ctx_512': ctx_512, 'L0_attn_W_qkv': _L0_attn_in['W_qkv'], 'L0_attn_W_out': _L0_attn_in['W_out'], 'L0_xattn_ln1_g': _L0_xattn_in['ln1_g'], 'L0_xattn_ln1_b': _L0_xattn_in['ln1_b'], 'L0_xattn_ln2_g': _L0_xattn_in['ln2_g'], 'L0_xattn_ln2_b': _L0_xattn_in['ln2_b'], 'L0_xattn_a1_wq': _L0_xattn_in['a1_wq'], 'L0_xattn_a1_wk': _L0_xattn_in['a1_wk'], 'L0_xattn_a1_wv': _L0_xattn_in['a1_wv'], 'L0_xattn_a1_li1_w': _L0_xattn_in['a1_li1_w'], 'L0_xattn_a1_li1_b': _L0_xattn_in['a1_li1_b'], 'L0_xattn_a1_lnx_g': _L0_xattn_in['a1_lnx_g'], 'L0_xattn_a1_lnx_b': _L0_xattn_in['a1_lnx_b'], 'L0_xattn_a1_lny_g': _L0_xattn_in['a1_lny_g'], 'L0_xattn_a1_lny_b': _L0_xattn_in['a1_lny_b'], 'L0_xattn_a1_ln3_g': _L0_xattn_in['a1_ln3_g'], 'L0_xattn_a1_ln3_b': _L0_xattn_in['a1_ln3_b'], 'L0_xattn_a1_li2_w': _L0_xattn_in['a1_li2_w'], 'L0_xattn_a1_li2_b': _L0_xattn_in['a1_li2_b'], 'L0_xattn_a1_li3_w': _L0_xattn_in['a1_li3_w'], 'L0_xattn_a1_li3_b': _L0_xattn_in['a1_li3_b'], 'L0_xattn_a2_wq': _L0_xattn_in['a2_wq'], 'L0_xattn_a2_wk': _L0_xattn_in['a2_wk'], 'L0_xattn_a2_wv': _L0_xattn_in['a2_wv'], 'L0_xattn_a2_li1_w': _L0_xattn_in['a2_li1_w'], 'L0_xattn_a2_li1_b': _L0_xattn_in['a2_li1_b'], 'L0_xattn_a2_lnx_g': _L0_xattn_in['a2_lnx_g'], 'L0_xattn_a2_lnx_b': _L0_xattn_in['a2_lnx_b'], 'L0_xattn_a2_lny_g': _L0_xattn_in['a2_lny_g'], 'L0_xattn_a2_lny_b': _L0_xattn_in['a2_lny_b'], 'L0_xattn_a2_ln3_g': _L0_xattn_in['a2_ln3_g'], 'L0_xattn_a2_ln3_b': _L0_xattn_in['a2_ln3_b'], 'L0_xattn_a2_li2_w': _L0_xattn_in['a2_li2_w'], 'L0_xattn_a2_li2_b': _L0_xattn_in['a2_li2_b'], 'L0_xattn_a2_li3_w': _L0_xattn_in['a2_li3_w'], 'L0_xattn_a2_li3_b': _L0_xattn_in['a2_li3_b'], 'L0_ffn_gate_w': _L0_ffn_in['gate_w'], 'L0_ffn_experts_gate_up': _L0_ffn_in['experts_gate_up'], 'L0_ffn_experts_down': _L0_ffn_in['experts_down'], 'L0_ffn_shared_gate_w': _L0_ffn_in['shared_gate_w'], 'L0_ffn_shared_up_w': _L0_ffn_in['shared_up_w'], 'L0_ffn_shared_down_w': _L0_ffn_in['shared_down_w'], 'L0_ffn_shared_expert_gate_w': _L0_ffn_in['shared_expert_gate_w'], 'L1_attn_w_attn': _L1_attn_in['w_attn'], 'L1_attn_b_attn': _L1_attn_in['b_attn'], 'L1_attn_w_proj': _L1_attn_in['w_proj'], 'L1_attn_b_proj': _L1_attn_in['b_proj'], 'L1_attn_w_fc': _L1_attn_in['w_fc'], 'L1_attn_b_fc': _L1_attn_in['b_fc'], 'L1_attn_w_mlp_proj': _L1_attn_in['w_mlp_proj'], 'L1_attn_b_mlp_proj': _L1_attn_in['b_mlp_proj'], 'L1_xattn_Wq': _L1_xattn_in['Wq'], 'L1_xattn_Wk': _L1_xattn_in['Wk'], 'L1_xattn_Wv': _L1_xattn_in['Wv'], 'L1_xattn_Wo': _L1_xattn_in['Wo'], 'L1_xattn_bo': _L1_xattn_in['bo'], 'L1_ffn_gate_w': _L1_ffn_in['gate_w'], 'L1_ffn_rms_w': _L1_ffn_in['rms_w'], 'L1_ffn_W1': _L1_ffn_in['W1'], 'L1_ffn_W2': _L1_ffn_in['W2'], 'L1_ffn_W3': _L1_ffn_in['W3'], 'L2_attn_Wq': _L2_attn_in['Wq'], 'L2_attn_Wk': _L2_attn_in['Wk'], 'L2_attn_Wv': _L2_attn_in['Wv'], 'L2_attn_Wo': _L2_attn_in['Wo'], 'L2_xattn_Wq': _L2_xattn_in['Wq'], 'L2_xattn_bq': _L2_xattn_in['bq'], 'L2_xattn_Wk': _L2_xattn_in['Wk'], 'L2_xattn_bk': _L2_xattn_in['bk'], 'L2_xattn_Wv': _L2_xattn_in['Wv'], 'L2_xattn_bv': _L2_xattn_in['bv'], 'L2_ffn_w1': _L2_ffn_in['w1'], 'L2_ffn_w2': _L2_ffn_in['w2'], 'L2_ffn_router_w': _L2_ffn_in['router_w'], 'L3_attn_Wq': _L3_attn_in['Wq'], 'L3_attn_bq': _L3_attn_in['bq'], 'L3_attn_Wk': _L3_attn_in['Wk'], 'L3_attn_bk': _L3_attn_in['bk'], 'L3_attn_Wv': _L3_attn_in['Wv'], 'L3_attn_bv': _L3_attn_in['bv'], 'L3_xattn_Wq': _L3_xattn_in['Wq'], 'L3_xattn_bq': _L3_xattn_in['bq'], 'L3_xattn_Wk': _L3_xattn_in['Wk'], 'L3_xattn_bk': _L3_xattn_in['bk'], 'L3_xattn_Wv': _L3_xattn_in['Wv'], 'L3_xattn_bv': _L3_xattn_in['bv'], 'L3_ffn_router_w': _L3_ffn_in['router_w'], 'L3_ffn_w1': _L3_ffn_in['w1'], 'L3_ffn_w2': _L3_ffn_in['w2']}

def reference(x, ctx_512, L0_attn_W_qkv, L0_attn_W_out, L0_xattn_ln1_g, L0_xattn_ln1_b, L0_xattn_ln2_g, L0_xattn_ln2_b, L0_xattn_a1_wq, L0_xattn_a1_wk, L0_xattn_a1_wv, L0_xattn_a1_li1_w, L0_xattn_a1_li1_b, L0_xattn_a1_lnx_g, L0_xattn_a1_lnx_b, L0_xattn_a1_lny_g, L0_xattn_a1_lny_b, L0_xattn_a1_ln3_g, L0_xattn_a1_ln3_b, L0_xattn_a1_li2_w, L0_xattn_a1_li2_b, L0_xattn_a1_li3_w, L0_xattn_a1_li3_b, L0_xattn_a2_wq, L0_xattn_a2_wk, L0_xattn_a2_wv, L0_xattn_a2_li1_w, L0_xattn_a2_li1_b, L0_xattn_a2_lnx_g, L0_xattn_a2_lnx_b, L0_xattn_a2_lny_g, L0_xattn_a2_lny_b, L0_xattn_a2_ln3_g, L0_xattn_a2_ln3_b, L0_xattn_a2_li2_w, L0_xattn_a2_li2_b, L0_xattn_a2_li3_w, L0_xattn_a2_li3_b, L0_ffn_gate_w, L0_ffn_experts_gate_up, L0_ffn_experts_down, L0_ffn_shared_gate_w, L0_ffn_shared_up_w, L0_ffn_shared_down_w, L0_ffn_shared_expert_gate_w, L1_attn_w_attn, L1_attn_b_attn, L1_attn_w_proj, L1_attn_b_proj, L1_attn_w_fc, L1_attn_b_fc, L1_attn_w_mlp_proj, L1_attn_b_mlp_proj, L1_xattn_Wq, L1_xattn_Wk, L1_xattn_Wv, L1_xattn_Wo, L1_xattn_bo, L1_ffn_gate_w, L1_ffn_rms_w, L1_ffn_W1, L1_ffn_W2, L1_ffn_W3, L2_attn_Wq, L2_attn_Wk, L2_attn_Wv, L2_attn_Wo, L2_xattn_Wq, L2_xattn_bq, L2_xattn_Wk, L2_xattn_bk, L2_xattn_Wv, L2_xattn_bv, L2_ffn_w1, L2_ffn_w2, L2_ffn_router_w, L3_attn_Wq, L3_attn_bq, L3_attn_Wk, L3_attn_bk, L3_attn_Wv, L3_attn_bv, L3_xattn_Wq, L3_xattn_bq, L3_xattn_Wk, L3_xattn_bk, L3_xattn_Wv, L3_xattn_bv, L3_ffn_router_w, L3_ffn_w1, L3_ffn_w2):
    import jax
    import jax.numpy as jnp

    def _L0_attn_ref(x, W_qkv, W_out):
        import jax, jax.numpy as jnp
        import numpy as np
        import math
        D_MODEL = 128
        N_HEADS = 16
        D_HEAD = D_MODEL // N_HEADS
        WINDOW = 32
        SCALE = 1.0 / math.sqrt(D_HEAD)

        def _window_mask(seq_len: int) -> jnp.ndarray:
            i = jnp.arange(seq_len)[:, None]
            j = jnp.arange(seq_len)[None, :]
            allowed = (j <= i) & (j > i - WINDOW)
            return jnp.where(allowed, 0.0, -jnp.inf).astype(jnp.float32)
        B, S, _ = x.shape
        qkv = x @ W_qkv
        qkv = qkv.reshape(B, S, 3, N_HEADS, D_HEAD)
        qkv = jnp.transpose(qkv, (2, 0, 3, 1, 4))
        q, k, v = (qkv[0], qkv[1], qkv[2])
        scores = jnp.einsum('bhsd,bhtd->bhst', q, k) * SCALE
        scores = scores + _window_mask(S)[None, None]
        weights = jax.nn.softmax(scores, axis=-1)
        out = jnp.einsum('bhst,bhtd->bhsd', weights, v)
        out = jnp.transpose(out, (0, 2, 1, 3)).reshape(B, S, D_MODEL)
        return out @ W_out

    def _L0_xattn_ref(xx, ee, ln1_g, ln1_b, ln2_g, ln2_b, a1_wq, a1_wk, a1_wv, a1_li1_w, a1_li1_b, a1_lnx_g, a1_lnx_b, a1_lny_g, a1_lny_b, a1_ln3_g, a1_ln3_b, a1_li2_w, a1_li2_b, a1_li3_w, a1_li3_b, a2_wq, a2_wk, a2_wv, a2_li1_w, a2_li1_b, a2_lnx_g, a2_lnx_b, a2_lny_g, a2_lny_b, a2_ln3_g, a2_ln3_b, a2_li2_w, a2_li2_b, a2_li3_w, a2_li3_b, training):
        import jax, jax.numpy as jnp
        import numpy as np
        H, D, C1, C2, S, M, B, W = (16, 32, 128, 64, 256, 64, 2, 4)

        def _ln(x, g, b):
            m = jnp.mean(x, -1, keepdims=True)
            v = jnp.var(x, -1, keepdims=True)
            return (x - m) * jax.lax.rsqrt(v + 1e-05) * g + b

        def _mha(x, y, wq, wk, wv, li1_w, li1_b, lnx_g, lnx_b, lny_g, lny_b, ln3_g, ln3_b, li2_w, li2_b, li3_w, li3_b, causal):
            xn = _ln(x, lnx_g, lnx_b)
            yn = _ln(y, lny_g, lny_b)
            q = jnp.einsum('bsc,hcd->bhsd', xn, wq)
            k = jnp.einsum('btc,hcd->bhtd', yn, wk)
            v = jnp.einsum('btc,hcd->bhtd', yn, wv)
            a = jax.nn.softmax(jnp.einsum('bhsd,bhtd->bhst', q, k) * D ** (-0.5), axis=-1)
            if causal:
                s, t = (a.shape[-2], a.shape[-1])
                mask = (jnp.arange(t)[None, :] > jnp.arange(s)[:, None]).astype(a.dtype)
                a = a * mask
            o = jnp.einsum('bhst,bhtd->bhsd', a, v)
            o = o.transpose(0, 2, 1, 3).reshape(x.shape[0], x.shape[1], H * D)
            x_out = x + o @ li1_w + li1_b
            h = jax.nn.gelu(_ln(x_out, ln3_g, ln3_b) @ li2_w + li2_b, approximate=False)
            return x_out + h @ li3_w + li3_b
        x = _ln(xx, ln1_g, ln1_b)
        x = x + _mha(x, x, a1_wq, a1_wk, a1_wv, a1_li1_w, a1_li1_b, a1_lnx_g, a1_lnx_b, a1_lny_g, a1_lny_b, a1_ln3_g, a1_ln3_b, a1_li2_w, a1_li2_b, a1_li3_w, a1_li3_b, causal=True)
        x = _ln(x, ln2_g, ln2_b)
        return x + _mha(x, ee, a2_wq, a2_wk, a2_wv, a2_li1_w, a2_li1_b, a2_lnx_g, a2_lnx_b, a2_lny_g, a2_lny_b, a2_ln3_g, a2_ln3_b, a2_li2_w, a2_li2_b, a2_li3_w, a2_li3_b, causal=False)

    def _L0_ffn_ref(x, gate_w, experts_gate_up, experts_down, shared_gate_w, shared_up_w, shared_down_w, shared_expert_gate_w):
        import jax, jax.numpy as jnp
        import numpy as np
        HIDDEN_SIZE = 128
        NUM_EXPERTS = 8
        MOE_INTERMEDIATE_SIZE = 176
        NUM_EXPERTS_PER_TOK = 2
        SHARED_EXPERT_INTERMEDIATE_SIZE = 352
        B, T = (2, 128)
        W_SCALE = 0.02
        Bx, Tx, H = x.shape
        E = gate_w.shape[0]
        I = experts_down.shape[2]
        x_flat = x.reshape(Bx * Tx, H)
        logits = x_flat @ gate_w.T
        scores = jax.nn.softmax(logits, axis=-1)
        _, topk_ids = jax.lax.top_k(scores, NUM_EXPERTS_PER_TOK)
        in_topk = jax.nn.one_hot(topk_ids, E, dtype=x.dtype).sum(axis=1)
        w = scores * in_topk
        gu = jnp.einsum('nh,eih->nei', x_flat, experts_gate_up)
        g, u = (gu[..., :I], gu[..., I:])
        h = jax.nn.silu(g) * u
        expert_out = jnp.einsum('nei,ehi->neh', h, experts_down)
        out = jnp.einsum('neh,ne->nh', expert_out, w)
        shared = jax.nn.silu(x_flat @ shared_gate_w.T) * (x_flat @ shared_up_w.T) @ shared_down_w.T
        shared_weight = jax.nn.sigmoid(x_flat @ shared_expert_gate_w.T)
        out = out + shared_weight * shared
        return out.reshape(Bx, Tx, H)

    def _L1_attn_ref(x, w_attn, b_attn, w_proj, b_proj, w_fc, b_fc, w_mlp_proj, b_mlp_proj):
        import jax, jax.numpy as jnp
        import numpy as np
        import math
        B, T, C, H = (4, 256, 128, 16)
        EPS = 1e-10

        def layernorm(x):
            mean = jnp.mean(x, axis=-1, keepdims=True)
            xmu = x - mean
            var = jnp.mean(xmu * xmu, axis=-1, keepdims=True)
            return xmu / jnp.sqrt(var + EPS)

        def new_gelu(x):
            c = math.sqrt(2.0 / math.pi)
            return 0.5 * x * (1.0 + jnp.tanh(c * (x + 0.044715 * x * x * x)))

        def attention(x, w_attn, b_attn, w_proj, b_proj):
            b, t, cdim = x.shape
            d = cdim // H
            ca = x @ w_attn.T + b_attn
            q, k, v = jnp.split(ca, 3, axis=2)
            q = q.reshape(b, t, H, d)
            k = k.reshape(b, t, H, d)
            v = v.reshape(b, t, H, d)
            att = jnp.einsum('bthd,bshd->bhts', q, k) * (1.0 / math.sqrt(d))
            mask = jnp.tril(jnp.ones((t, t), dtype=bool))
            att = jnp.where(mask, att, -jnp.inf)
            att = jax.nn.softmax(att, axis=-1)
            y = jnp.einsum('bhts,bshd->bthd', att, v).reshape(b, t, cdim)
            return y @ w_proj.T + b_proj
        x = x + attention(layernorm(x), w_attn, b_attn, w_proj, b_proj)
        h = new_gelu(layernorm(x) @ w_fc.T + b_fc)
        x = x + (h @ w_mlp_proj.T + b_mlp_proj)
        return x

    def _L1_xattn_ref(q, kv, Wq, Wk, Wv, Wo, bo):
        import jax, jax.numpy as jnp
        import numpy as np
        NUM_HEADS = 16
        HEAD_DIM = 64
        Q_DIM = 128
        KV_DIM = 64
        INNER = NUM_HEADS * HEAD_DIM
        B, N, _ = q.shape
        M = kv.shape[1]
        scale = HEAD_DIM ** (-0.5)
        qh = (q @ Wq).reshape(B, N, NUM_HEADS, HEAD_DIM).transpose(0, 2, 1, 3)
        kh = (kv @ Wk).reshape(B, M, NUM_HEADS, HEAD_DIM).transpose(0, 2, 1, 3)
        vh = (kv @ Wv).reshape(B, M, NUM_HEADS, HEAD_DIM).transpose(0, 2, 1, 3)
        scores = jnp.einsum('bhnd,bhmd->bhnm', qh, kh) * scale
        attn = jax.nn.softmax(scores, axis=-1)
        out = jnp.einsum('bhnm,bhmd->bhnd', attn, vh)
        out = out.transpose(0, 2, 1, 3).reshape(B, N, INNER)
        return out @ Wo + bo

    def _L1_ffn_ref(x, gate_w, rms_w, W1, W2, W3):
        import jax, jax.numpy as jnp
        import numpy as np
        E, K = (8, 2)
        DM, DE = (128, 352)
        B, S = (1, 256)
        EPS = 1e-06

        def _rmsnorm(x, w):
            var = jnp.mean(jnp.square(x), axis=-1, keepdims=True)
            return x * jax.lax.rsqrt(var + EPS) * w
        y = _rmsnorm(x, rms_w)
        logits = jnp.einsum('bsd,ed->bse', y, gate_w)
        vals, idx = jax.lax.top_k(logits, K)
        w = jax.nn.softmax(vals, axis=-1)
        w_full = jnp.einsum('bsk,bske->bse', w, jax.nn.one_hot(idx, E, dtype=x.dtype))
        up = jnp.einsum('bsd,end->bsen', y, W1)
        gate = jnp.einsum('bsd,end->bsen', y, W2)
        h = jax.nn.silu(up) * gate
        out = jnp.einsum('bsen,emn->bsem', h, W3)
        comb = jnp.einsum('bsem,bse->bsm', out, w_full)
        return x + comb

    def _L2_attn_ref(hidden_states, Wq, Wk, Wv, Wo):
        import jax, jax.numpy as jnp
        import numpy as np
        B, L, D_MODEL = (4, 256, 128)
        N_HEADS, FEAT, HEAD_DIM = (16, 16, 64)
        CHUNK = 128
        EPS = 1e-12

        def taylor_exp(x):
            f = x.shape[-1]
            r2 = jnp.sqrt(jnp.asarray(2.0, x.dtype))
            rd = jnp.sqrt(jnp.asarray(float(f), x.dtype))
            rrd = jnp.sqrt(rd)
            x2 = (x[..., :, None] * x[..., None, :]).reshape(*x.shape[:-1], f * f) / r2
            ones = jnp.ones_like(x[..., :1])
            return jnp.concatenate([ones, x / rrd, x2 / rd], axis=-1)
        b, l, _ = hidden_states.shape
        q = (hidden_states @ Wq.T).reshape(b, l, N_HEADS, FEAT).transpose(0, 2, 1, 3)
        k = (hidden_states @ Wk.T).reshape(b, l, N_HEADS, FEAT).transpose(0, 2, 1, 3)
        v = (hidden_states @ Wv.T).reshape(b, l, N_HEADS, HEAD_DIM).transpose(0, 2, 1, 3)
        qf = taylor_exp(q)
        kf = taylor_exp(k)
        De = qf.shape[-1]
        n = l // CHUNK
        qc = jnp.moveaxis(qf.reshape(b, N_HEADS, n, CHUNK, De), 2, 0)
        kc = jnp.moveaxis(kf.reshape(b, N_HEADS, n, CHUNK, De), 2, 0)
        vc = jnp.moveaxis(v.reshape(b, N_HEADS, n, CHUNK, HEAD_DIM), 2, 0)
        mask = jnp.tril(jnp.ones((CHUNK, CHUNK), qf.dtype))

        def step(carry, xs):
            S, z = carry
            qi, ki, vi = xs
            attn = jnp.einsum('bhid,bhjd->bhij', qi, ki) * mask
            num = jnp.einsum('bhij,bhje->bhie', attn, vi) + jnp.einsum('bhid,bhde->bhie', qi, S)
            den = attn.sum(-1) + jnp.einsum('bhid,bhd->bhi', qi, z)
            yi = num / (den[..., None] + EPS)
            S = S + jnp.einsum('bhjd,bhje->bhde', ki, vi)
            z = z + ki.sum(2)
            return ((S, z), yi)
        S0 = jnp.zeros((b, N_HEADS, De, HEAD_DIM), qf.dtype)
        z0 = jnp.zeros((b, N_HEADS, De), qf.dtype)
        _, ys = jax.lax.scan(step, (S0, z0), (qc, kc, vc))
        y = jnp.moveaxis(ys, 0, 2).reshape(b, N_HEADS, l, HEAD_DIM)
        y = y.transpose(0, 2, 1, 3).reshape(b, l, N_HEADS * HEAD_DIM)
        return y @ Wo.T

    def _L2_xattn_ref(query, key, value, Wq, bq, Wk, bk, Wv, bv):
        import jax, jax.numpy as jnp
        import numpy as np
        B, LQ, LK = (8, 256, 256)
        QD, KD, VD = (128, 64, 64)
        q = jnp.einsum('bld,de->ble', query, Wq) + bq
        k = jnp.einsum('bld,de->ble', key, Wk) + bk
        v = jnp.einsum('bld,de->ble', value, Wv) + bv
        scores = jnp.einsum('bqe,bke->bqk', q, k)
        attn = jax.nn.softmax(scores, axis=-1)
        out = jnp.einsum('bqk,bke->bqe', attn, v)
        return out

    def _L2_ffn_ref(hidden_states, w1, w2, router_w):
        import jax, jax.numpy as jnp
        import numpy as np
        HIDDEN = 128
        INTER = 256
        NUM_EXPERTS = 8
        TOPK = 2
        STD = 0.02
        orig_shape = hidden_states.shape
        dtype = hidden_states.dtype
        x = hidden_states.reshape(-1, orig_shape[-1])
        E = w1.shape[0]
        gating = x @ router_w.T
        probs = jax.nn.softmax(gating.astype(jnp.float32), axis=-1)
        topk_w, sel = jax.lax.top_k(probs, TOPK)
        topk_w = topk_w.astype(dtype)
        combine = (jax.nn.one_hot(sel, E, dtype=dtype) * topk_w[..., None]).sum(axis=1)
        h = jnp.einsum('td,eid->tei', x, w1)
        gate = jax.nn.silu(h[..., :INTER])
        y = h[..., INTER:] * gate
        out = jnp.einsum('tei,ehi,te->th', y, w2, combine)
        return out.reshape(orig_shape)

    def _L3_attn_ref(x, Wq, bq, Wk, bk, Wv, bv):
        import jax, jax.numpy as jnp
        import numpy as np
        B, S, E = (4, 512, 128)
        H = 16
        D = E // H
        N_SAMPLE = 128
        Bs, Sl, Ed = x.shape
        q = (x @ Wq.T + bq).reshape(Bs, Sl, H, D).transpose(0, 2, 1, 3)
        k = (x @ Wk.T + bk).reshape(Bs, Sl, H, D).transpose(0, 2, 1, 3)
        v = (x @ Wv.T + bv).reshape(Bs, Sl, H, D).transpose(0, 2, 1, 3)
        pos = jnp.arange(Sl, dtype=x.dtype)
        theta = jnp.pi / 2.0 * pos / Sl
        cos_w = jnp.cos(theta)[None, None, :, None]
        sin_w = jnp.sin(theta)[None, None, :, None]
        qn = jax.nn.relu(q)
        kn = jax.nn.relu(k)
        q_cos, q_sin = (qn * cos_w, qn * sin_w)
        k_cos, k_sin = (kn * cos_w, kn * sin_w)
        scores = jnp.sum(q * k, axis=-1)
        _, idx = jax.lax.top_k(scores, N_SAMPLE)
        kv_cos = jnp.einsum('bhsd,bhse->bhde', k_cos, v)
        kv_sin = jnp.einsum('bhsd,bhse->bhde', k_sin, v)
        qs_cos = jnp.take_along_axis(q_cos, idx[..., None], axis=2)
        qs_sin = jnp.take_along_axis(q_sin, idx[..., None], axis=2)
        sampled = jnp.einsum('bhnd,bhde->bhne', qs_cos, kv_cos) + jnp.einsum('bhnd,bhde->bhne', qs_sin, kv_sin)
        bi = jnp.arange(Bs)[:, None, None]
        hi = jnp.arange(H)[None, :, None]
        values = jnp.zeros((Bs, H, Sl, D), sampled.dtype).at[bi, hi, idx].add(sampled)
        out = values.transpose(0, 2, 1, 3).reshape(Bs, Sl, H * D)
        return out

    def _L3_xattn_ref(query, key, value, Wq, bq, Wk, bk, Wv, bv):
        import jax, jax.numpy as jnp
        import numpy as np
        B, LQ, LK = (8, 256, 256)
        QD, KD, VD = (128, 64, 64)
        q = jnp.einsum('bld,de->ble', query, Wq) + bq
        k = jnp.einsum('bld,de->ble', key, Wk) + bk
        v = jnp.einsum('bld,de->ble', value, Wv) + bv
        scores = jnp.einsum('bqe,bke->bqk', q, k)
        attn = jax.nn.softmax(scores, axis=-1)
        out = jnp.einsum('bqk,bke->bqe', attn, v)
        return out

    def _L3_ffn_ref(x, router_w, w1, w2):
        import jax, jax.numpy as jnp
        import numpy as np
        B, S, H, E, K = (4, 256, 128, 8, 2)
        bsz, seq, hidden = x.shape
        n_experts = w1.shape[0]
        tokens = x.reshape(-1, hidden)
        T = tokens.shape[0]
        logits = tokens @ router_w.T
        topv, topi = jax.lax.top_k(logits, K)
        w = jax.nn.softmax(topv, axis=-1).astype(tokens.dtype)
        gate = jnp.zeros((T, n_experts), tokens.dtype).at[jnp.arange(T)[:, None], topi].add(w)
        out = jnp.zeros_like(tokens)
        for e in range(n_experts):
            h = jax.nn.gelu(tokens @ w1[e].T, approximate=False)
            y = h @ w2[e].T
            out = out + gate[:, e:e + 1] * y
        return out.reshape(bsz, seq, hidden)
    x = _layernorm(x + _L0_attn_ref(x, L0_attn_W_qkv, L0_attn_W_out), axis=-1)
    x = _layernorm(x + _L0_xattn_ref(x, ctx_512, L0_xattn_ln1_g, L0_xattn_ln1_b, L0_xattn_ln2_g, L0_xattn_ln2_b, L0_xattn_a1_wq, L0_xattn_a1_wk, L0_xattn_a1_wv, L0_xattn_a1_li1_w, L0_xattn_a1_li1_b, L0_xattn_a1_lnx_g, L0_xattn_a1_lnx_b, L0_xattn_a1_lny_g, L0_xattn_a1_lny_b, L0_xattn_a1_ln3_g, L0_xattn_a1_ln3_b, L0_xattn_a1_li2_w, L0_xattn_a1_li2_b, L0_xattn_a1_li3_w, L0_xattn_a1_li3_b, L0_xattn_a2_wq, L0_xattn_a2_wk, L0_xattn_a2_wv, L0_xattn_a2_li1_w, L0_xattn_a2_li1_b, L0_xattn_a2_lnx_g, L0_xattn_a2_lnx_b, L0_xattn_a2_lny_g, L0_xattn_a2_lny_b, L0_xattn_a2_ln3_g, L0_xattn_a2_ln3_b, L0_xattn_a2_li2_w, L0_xattn_a2_li2_b, L0_xattn_a2_li3_w, L0_xattn_a2_li3_b, 0), axis=-1)
    x = _layernorm(x + _L0_ffn_ref(x, L0_ffn_gate_w, L0_ffn_experts_gate_up, L0_ffn_experts_down, L0_ffn_shared_gate_w, L0_ffn_shared_up_w, L0_ffn_shared_down_w, L0_ffn_shared_expert_gate_w), axis=-1)
    x = _layernorm(x + _L1_attn_ref(x, L1_attn_w_attn, L1_attn_b_attn, L1_attn_w_proj, L1_attn_b_proj, L1_attn_w_fc, L1_attn_b_fc, L1_attn_w_mlp_proj, L1_attn_b_mlp_proj), axis=-1)
    x = _layernorm(x + _L1_xattn_ref(x, ctx_512, L1_xattn_Wq, L1_xattn_Wk, L1_xattn_Wv, L1_xattn_Wo, L1_xattn_bo), axis=-1)
    x = _layernorm(x + _L1_ffn_ref(x, L1_ffn_gate_w, L1_ffn_rms_w, L1_ffn_W1, L1_ffn_W2, L1_ffn_W3), axis=-1)
    x = _layernorm(x + _L2_attn_ref(x, L2_attn_Wq, L2_attn_Wk, L2_attn_Wv, L2_attn_Wo), axis=-1)
    x = _layernorm(x + _L2_xattn_ref(x, ctx_512, ctx_512, L2_xattn_Wq, L2_xattn_bq, L2_xattn_Wk, L2_xattn_bk, L2_xattn_Wv, L2_xattn_bv), axis=-1)
    x = _layernorm(x + _L2_ffn_ref(x, L2_ffn_w1, L2_ffn_w2, L2_ffn_router_w), axis=-1)
    x = _layernorm(x + _L3_attn_ref(x, L3_attn_Wq, L3_attn_bq, L3_attn_Wk, L3_attn_bk, L3_attn_Wv, L3_attn_bv), axis=-1)
    x = _layernorm(x + _L3_xattn_ref(x, ctx_512, ctx_512, L3_xattn_Wq, L3_xattn_bq, L3_xattn_Wk, L3_xattn_bk, L3_xattn_Wv, L3_xattn_bv), axis=-1)
    x = _layernorm(x + _L3_ffn_ref(x, L3_ffn_router_w, L3_ffn_w1, L3_ffn_w2), axis=-1)
    return x

_drawn_inputs = setup_inputs


def setup_inputs(seed=0):
    import zlib

    import numpy as np

    out = dict(_drawn_inputs(seed))
    spreads = {'L0_xattn_ln1_g': (1.0, 0.2),
     'L0_xattn_ln1_b': (0.0, 0.1),
     'L0_xattn_ln2_g': (1.0, 0.2),
     'L0_xattn_ln2_b': (0.0, 0.1),
     'L0_xattn_a1_li1_b': (0.0, 0.1),
     'L0_xattn_a1_lnx_g': (1.0, 0.6),
     'L0_xattn_a1_lnx_b': (0.0, 0.8),
     'L0_xattn_a1_lny_g': (1.0, 0.6),
     'L0_xattn_a1_lny_b': (0.0, 0.581),
     'L0_xattn_a1_ln3_g': (1.0, 0.6),
     'L0_xattn_a1_ln3_b': (0.0, 0.531),
     'L0_xattn_a1_li2_b': (0.0, 0.1),
     'L0_xattn_a1_li3_b': (0.0, 0.1),
     'L0_xattn_a2_li1_b': (0.0, 0.1),
     'L0_xattn_a2_lnx_g': (1.0, 0.6),
     'L0_xattn_a2_lnx_b': (0.0, 0.8),
     'L0_xattn_a2_lny_g': (1.0, 0.6),
     'L0_xattn_a2_lny_b': (0.0, 0.51),
     'L0_xattn_a2_ln3_g': (1.0, 0.6),
     'L0_xattn_a2_ln3_b': (0.0, 0.479),
     'L0_xattn_a2_li2_b': (0.0, 0.1),
     'L0_xattn_a2_li3_b': (0.0, 0.1),
     'L1_ffn_rms_w': (1.0, 0.6),
     'L2_xattn_bq': (0.0, 0.28),
     'L2_xattn_bk': (0.0, 0.8),
     'L2_xattn_bv': (0.0, 0.1),
     'L3_attn_bq': (0.0, 0.1),
     'L3_attn_bk': (0.0, 0.1),
     'L3_attn_bv': (0.0, 0.1),
     'L3_xattn_bq': (0.0, 0.299),
     'L3_xattn_bk': (0.0, 0.8),
     'L3_xattn_bv': (0.0, 0.1)}
    factors = {'L0_xattn_a1_wq': 8.0,
     'L0_xattn_a1_wk': 8.0,
     'L0_xattn_a2_wq': 8.0,
     'L0_xattn_a2_wk': 8.0,
     'L0_ffn_gate_w': 5.985,
     'L0_ffn_experts_gate_up': 5.051,
     'L0_ffn_experts_down': 5.516,
     'L0_ffn_shared_gate_w': 3.248,
     'L0_ffn_shared_up_w': 3.333,
     'L0_ffn_shared_down_w': 3.133,
     'L0_ffn_shared_expert_gate_w': 7.147,
     'L1_attn_b_attn': 3.06,
     'L1_attn_b_fc': 2.941,
     'L1_ffn_gate_w': 8.0,
     'L1_ffn_W1': 8.0,
     'L1_ffn_W2': 8.0,
     'L1_ffn_W3': 8.0,
     'L2_attn_Wq': 5.605,
     'L2_attn_Wk': 5.979,
     'L2_ffn_w1': 5.226,
     'L2_ffn_w2': 5.658,
     'L2_ffn_router_w': 6.637}
    for name, (base, spread) in spreads.items():
        noise = np.random.default_rng([zlib.crc32(name.encode()), seed]).standard_normal(out[name].shape)
        drawn = base * np.exp(spread * noise) if base else spread * noise
        out[name] = jnp.asarray(drawn.astype(out[name].dtype))
    for name, factor in factors.items():
        out[name] = (out[name] * factor).astype(out[name].dtype)
    return out
```

```python
from contextlib import ExitStack

import numpy as np

import concourse.bass as bass
from concourse import mybir

F32 = mybir.dt.float32
BF16 = mybir.dt.bfloat16
U32 = mybir.dt.uint32
ALU = mybir.AluOpType
ACT = mybir.ActivationFunctionType
AX_X = mybir.AxisListType.X

P = 128
CTX = 64
HEADS = 16
BANK = 512
NEG = -1e30
LN_EPS = 1e-5



def attention(name, **k):
    p = dict(kind="attention", name=name, group=2, qc=4, vc=4, scale=1.0, norm_eps=None, mask=None,
             post_mask=False, taylor=False, ctx=None, affine=False, qkv_bias=False, out_bias=False,
             adds=("x",), store="x")
    p.update(k)
    kv_rows = CTX if p["ctx"] else P
    w = [("wq", P, p["qc"] * P), ("wk", kv_rows, p["qc"] * P), ("wv", kv_rows, p["vc"] * P),
         ("wo", P, p["vc"] * P)]
    if p["affine"]:
        w += [("gx", P, 1), ("bx", P, 1), ("gy", kv_rows, 1), ("by", kv_rows, 1)]
    if p["qkv_bias"]:
        w += [("bq", P, p["qc"]), ("bk", P, p["qc"]), ("bv", P, p["vc"])]
    if p["out_bias"]:
        w += [("bo", P, P)]
    if name == "L0_attn":
        w += [("ln_g", P, P), ("ln_b", P, P)]
    p["weights"] = w
    return p


def experts(name, chunks, **k):
    p = dict(kind="experts", name=name, group=4, chunks=chunks, func=ACT.Gelu, gated=False,
             norm_eps=None, rms_eps=None, affine=False, hidden_bias=False, out_bias=False,
             routing=None, shared=False, adds=("x",), store="x", ctx=None)
    p.update(k)
    sizes = [c for e in chunks for c in e]
    w = [("up", P, sum(sizes) * (2 if p["gated"] else 1)), ("down", P, len(sizes) * P)]
    if p["routing"]:
        w += [("gate", P, 8 + p["shared"])]
    if p["affine"]:
        w += [("gx", P, 1), ("bx", P, 1)]
    if p["rms_eps"]:
        w += [("gx", P, 1)]
    if p["hidden_bias"]:
        w += [("bh", P, len(sizes))]
    if p["out_bias"]:
        w += [("bo", P, P)]
    if p["store"] == "a":
        w += [("ln_g", P, P), ("ln_b", P, P)]
    p["weights"] = w
    return p


def single(name):
    return dict(kind="single", name=name, group=4, ctx="plain", adds=("x",), store="x",
                norm_eps=None, affine=False, out_bias=False,
                weights=[("wq", P, P), ("wk", CTX, P), ("wv", CTX, P), ("bq", P, 1), ("bk", P, 1),
                         ("bv", P, P)])


def cosine(name):
    return dict(kind="cosine", name=name, group=4, ctx=None, adds=("x",), store="x",
                norm_eps=None, affine=False, out_bias=False,
                weights=[("wq", P, P), ("wkv", P, 2 * P), ("bq", P, 1), ("bkv", P, 2 * P)])


THIRDS = [118, 117, 117]
PARTS = [
    attention("L0_attn", scale=8 ** -0.5, mask="window"),
    attention("L0_self", scale=32 ** -0.5, norm_eps=LN_EPS, affine=True, post_mask=True,
              out_bias=True, adds=("a",), store="xo"),
    experts("L0_mlp1", [[P] * 4], norm_eps=LN_EPS, affine=True, hidden_bias=True, out_bias=True,
            adds=("a", "xo"), store="a"),
    attention("L0_cross", scale=32 ** -0.5, norm_eps=LN_EPS, affine=True, ctx="normed",
              out_bias=True, adds=("a",), store="xo"),
    experts("L0_mlp2", [[P] * 4], norm_eps=LN_EPS, affine=True, hidden_bias=True, out_bias=True,
            adds=("a", "xo", "x")),
    experts("L0_ffn", [[88, 88]] * 8 + [THIRDS], func=ACT.Silu, gated=True, routing="all",
            shared=True),
    attention("L1_attn", scale=8 ** -0.5, norm_eps=1e-10, mask="causal", qkv_bias=True,
              out_bias=True, store="xo"),
    experts("L1_mlp", [[P] * 4], func=ACT.Gelu_apprx_tanh, norm_eps=1e-10, hidden_bias=True,
            out_bias=True, adds=("xo", "x")),
    attention("L1_cross", qc=8, vc=8, scale=64 ** -0.5, ctx="plain", out_bias=True),
    experts("L1_ffn", [THIRDS] * 8, func=ACT.Silu, gated=True, routing="top", rms_eps=1e-6,
            adds=("x", "x")),
    attention("L2_attn", vc=8, taylor=True),
    single("L2_cross"),
    experts("L2_ffn", [[P] * 2] * 8, func=ACT.Silu, gated=True, routing="all"),
    cosine("L3_attn"),
    single("L3_cross"),
    experts("L3_ffn", [[P] * 2] * 8, routing="top"),
]
SOURCE = {"L0_self": "a", "L0_mlp1": "xo", "L0_cross": "a", "L0_mlp2": "xo", "L1_mlp": "xo"}

CONSTS = [("ident", P), ("lower", P), ("block4", 4), ("block2", 2), ("block8", P), ("iota", 8),
          ("cos_row", P), ("sin_row", P), ("cos_col", 1), ("sin_col", 1)]
CONSTS_BF = [("ident", P), ("causal", P), ("window", P)]


def columns(fields):
    at, place = 0, {}
    for f in fields:
        place[f[0]] = (at, f[-2] if len(f) == 3 else P, f[-1])
        at += f[-1]
    return place, at



def tail_steps(p):
    n = len(p["adds"]) + p["out_bias"]
    if p["store"] != "xo":
        n += 3
        if p["store"] == "a" or p["name"] == "L0_attn":
            n += 2
        if p["name"] == "L0_attn":
            n += 3
    return n


def signal_counts(p):
    n = dict(z_ready=1, zt_ps=1, zt_ready=1, tail_step=tail_steps(p), tail_done=1)
    if p["store"] != "xo":
        n.update(tail_var=1, tail_rstd=1)
        if p["name"] == "L0_attn":
            n.update(tail_var=2, tail_rstd=2)
    if p["norm_eps"] or p.get("rms_eps"):
        n.update(front_stats=1, front_aggr=1, front_var=1, front_rstd=1)
        if p.get("rms_eps"):
            n.update(front_sq=2)
    if p["ctx"]:
        n.update(ctx_in=16)
    if p["kind"] == "attention":
        u, o = p["qc"] // 2, p["vc"] // 4
        n.update(qk_ps=2 * u, q_ev=u, k_ev=u, kb_ready=2 * u, s_ps=8, s_read=8, p_exp=8, p_sum=4,
                 p_rec=4, p_norm=4, t_ps=8, t_ev=8, pv_ps=2 * o, o_ev=2 * o, v_ps=2 * o,
                 v_ev=2 * o, o_ps=1)
        if p["taylor"]:
            n.update(s_mask=8, p_eps=4)
            del n["p_exp"]
        else:
            n.update(s_max=8)
        if p["post_mask"]:
            n.update(p_mul=4)
    elif p["kind"] == "experts":
        chunks, ne = sum(map(len, p["chunks"])), len(p["chunks"])
        n.update(up_ps=chunks, act_ev=chunks, y_ps=ne)
        if p["gated"]:
            n.update(h_ready=chunks)
        if p["routing"]:
            n.update(gate_ps=1, route=11 + 2 * p["shared"], route_exp=1, acc=ne)
    elif p["kind"] == "single":
        n.update(q_ps=1, k_ps=1, q_ev=1, k_ev=1, v_ps=1, v_ev=1, s_ps=1, s_max=1, s_read=1,
                 p_exp=1, p_sum=1, p_rec=1, p_norm=1, t_ps=1, t_ev=1, pv_ps=1)
    elif p["kind"] == "cosine":
        n.update(kv_ps=2, kv_ev=2, kcs=1, q_ps=1, q_ev=1, qcs=1, o_ps=1, kvb_ps=1, kvb_ev=1)
    return n


class After:

    def __init__(self, base, per_step):
        self.base, self.n = base, per_step

    def __call__(self, i, k):
        return i * self.n + (self.base + k)


def bcast(ap, axis, count):
    ap = ap.unsqueeze(axis)
    shape = list(ap.shape)
    shape[axis] = count
    return ap.to_broadcast(shape)


def run_steps(eng, steps, front, body):
    front(0)
    with eng.Fori(0, steps - 1) as i:
        body(i, True)
    body(steps - 1, False)



def build_program(nc, x, ctx, ctx_t, consts, consts_bf, weights, out, parts, batch):
    with ExitStack() as stack:
        def sb(name, shape, dt=F32):
            return stack.enter_context(nc.sbuf_tensor(name, shape, dt))

        state = {n: sb(f"{n}_state", [P, batch, P]) for n in ("x", "a", "xo")}
        sizes = [columns(p["weights"])[1] for p in parts]
        blocks = [sb(f"weights{b}", [P, max(sizes[b::2] + [1])]) for b in range(2)]
        const_place, const_cols = columns(CONSTS)
        const_bf_place, const_bf_cols = columns(CONSTS_BF)
        const_sb = sb("consts", [P, const_cols])
        const_bf_sb = sb("consts_bf", [P, const_bf_cols], BF16)

        def const(name):
            at, _, n = const_place[name]
            return const_sb[:, at:at + n]

        def const_bf(name):
            at, _, n = const_bf_place[name]
            return const_bf_sb[:, at:at + n]

        ident = const("ident")
        z = sb("z", [P, 4, P])
        z_ctx = sb("z_ctx", [P, 2, CTX])
        ctx_raw = sb("ctx_raw", [P, 2, CTX])
        z_t = sb("z_t", [P, BANK])
        y_t = sb("y_t", [P, BANK])
        stats = sb("stats", [P, 4, 6])
        meanvar = sb("meanvar", [P, 4, 2])
        var_eps = sb("var_eps", [P, 4])
        rstd = sb("rstd", [P, 4])
        res = sb("res", [P, 4, P])
        t_stats = sb("t_stats", [P, 4, 6])
        t_meanvar = sb("t_meanvar", [P, 4, 2])
        t_var_eps = sb("t_var_eps", [P, 4])
        t_rstd = sb("t_rstd", [P, 4])
        eps_col = {e: sb(f"eps{n}", [P, 1]) for n, e in enumerate((LN_EPS, 1e-10, 1e-6))}
        minus_half = sb("minus_half", [P, 1])
        gate_dve = sb("gate_dve", [P, 1])
        gate_pool = sb("gate_pool", [P, 2])
        tail_mark = sb("tail_mark", [P, 1])
        ARENA = 18 * 1024 + 256
        arena = sb("arena", [P, ARENA])

        psum = [stack.enter_context(nc.psum_tensor(f"bank{b}", [P, BANK], F32)) for b in range(8)]

        counts = [signal_counts(p) for p in parts]
        names = sorted({n for c in counts for n in c})
        sem = {n: stack.enter_context(nc.semaphore(n)) for n in names}
        weights_in = [stack.enter_context(nc.semaphore(f"weights_in{b}")) for b in range(2)]
        x_in = stack.enter_context(nc.semaphore("x_in"))
        consts_in = stack.enter_context(nc.semaphore("consts_in"))
        consts_cast = stack.enter_context(nc.semaphore("consts_cast"))
        out_done = stack.enter_context(nc.semaphore("out_done"))
        primed = stack.enter_context(nc.semaphore("primed"))
        bases = {n: int(n != "ctx_in") for n in names}
        afters = []
        for p, c in zip(parts, counts):
            afters.append({n: After(bases[n], k) for n, k in c.items()})
            for n, k in c.items():
                bases[n] += k * (batch // p["group"])

        def weight(l, name):
            at, rows, n = columns(parts[l]["weights"])[0][name]
            return blocks[l % 2][0:rows, at:at + n]

        def dve_gate(eng):
            eng.memset(gate_dve[:, :], 0.0)

        def pool_gate(eng):
            eng.tensor_tensor(gate_pool[:, 0:1], minus_half[:, :], minus_half[:, :], ALU.add)

        def all_tails(l):
            return afters[l]["tail_done"](batch // parts[l]["group"], 0)

        def part_start(eng, l):
            if l:
                eng.wait_ge(sem["tail_done"], all_tails(l - 1))
            else:
                eng.wait_ge(primed, 1)
                eng.wait_ge(consts_in, 32)
                eng.wait_ge(consts_cast, 1)
            eng.wait_ge(weights_in[l % 2], 16 * (l // 2 + 1))

        def group_of(l, i):
            g = parts[l]["group"]
            return bass.ds(i * g, g)

        block = stack.enter_context(nc.Block())

        @block.sync
        def _(eng):
            def load_weights(l):
                at = columns(parts[l]["weights"])[1]
                eng.dma_start(blocks[l % 2][:, 0:at], weights[l]).then_inc(weights_in[l % 2], 16)

            eng.dma_start(const_sb[:, :], consts).then_inc(consts_in, 16)
            eng.dma_start(arena[:, 0:const_bf_cols], consts_bf).then_inc(consts_in, 16)
            load_weights(0)
            eng.dma_start(state["x"][:, :, :], x.rearrange("b s c -> s b c")).then_inc(x_in, 16)
            for l, p in enumerate(parts):
                after, steps, g = afters[l], batch // p["group"], p["group"]
                if l:
                    eng.wait_ge(sem["tail_done"], all_tails(l - 1))
                if l + 1 < len(parts):
                    load_weights(l + 1)
                if p["ctx"]:
                    def load_ctx(j, first=False, p=p, after=after, g=g):
                        if not first:
                            if p["ctx"] == "normed":
                                eng.wait_ge(sem["z_ready"], after["z_ready"](j, 0))
                            else:
                                eng.wait_ge(sem["v_ps"], after["v_ps"](j, 0))
                        if p["ctx"] == "normed":
                            src = ctx[bass.ds(j * g, g), :, :].rearrange("b s c -> s b c")
                            eng.dma_start(ctx_raw[:, :, :], src).then_inc(sem["ctx_in"], 16)
                        else:
                            eng.dma_start(y_t[0:CTX, 0:g * P], ctx_t[:, bass.ds(j * (g * P), g * P)])\
                               .then_inc(sem["ctx_in"], 16)
                    load_ctx(0, True)
                    with eng.Fori(1, steps) as j:
                        load_ctx(j)
            eng.wait_ge(sem["tail_done"], all_tails(len(parts) - 1))
            eng.dma_start(out.rearrange("b s c -> s b c"), state["x"][:, :, :]).then_inc(out_done, 16)
            eng.wait_ge(out_done, 16)


        def dve_front_stats(eng, l, j):
            p, after = parts[l], afters[l]
            if not (p["norm_eps"] or p.get("rms_eps")):
                return
            src = state[SOURCE.get(p["name"], "x")]
            g = p["group"]
            for t in range(g):
                ins = eng.bn_stats(stats[:, t, :], src[:, j * g + t, :])
            if p["ctx"] == "normed":
                eng.wait_ge(sem["ctx_in"], after["ctx_in"](j, 16))
                for t in range(2):
                    ins = eng.bn_stats(stats[:, g + t, :], ctx_raw[:, t, :])
            ins.then_inc(sem["front_stats"], 1)
            n = g + (2 if p["ctx"] == "normed" else 0)
            eng.wait_ge(sem["front_stats"], after["front_stats"](j, 1))
            dve_gate(eng)
            for t in range(n):
                ins = eng.bn_aggr(meanvar[:, t, :], stats[:, t, :])
            ins.then_inc(sem["front_aggr"], 1)
            if p.get("rms_eps"):
                eng.wait_ge(sem["front_aggr"], after["front_aggr"](j, 1))
                eng.tensor_tensor(rstd[:, 0:g], meanvar[:, 0:g, 0], meanvar[:, 0:g, 0], ALU.mult)\
                   .then_inc(sem["front_sq"], 1)
                eng.wait_ge(sem["front_sq"], after["front_sq"](j, 1))
                eng.tensor_tensor(meanvar[:, 0:g, 1], meanvar[:, 0:g, 1], rstd[:, 0:g], ALU.add)\
                   .then_inc(sem["front_sq"], 1)

        def pool_front_rstd(eng, l, j):
            p, after = parts[l], afters[l]
            eps = p["norm_eps"] or p.get("rms_eps")
            if not eps:
                return
            n = p["group"] + (2 if p["ctx"] == "normed" else 0)
            if p.get("rms_eps"):
                eng.wait_ge(sem["front_sq"], after["front_sq"](j, 2))
            else:
                eng.wait_ge(sem["front_aggr"], after["front_aggr"](j, 1))
            eng.tensor_tensor(var_eps[:, 0:n], meanvar[:, 0:n, 1],
                              eps_col[eps][:, :].to_broadcast([P, n]), ALU.add)\
               .then_inc(sem["front_var"], 1)
            eng.wait_ge(sem["front_var"], after["front_var"](j, 1))
            eng.tensor_tensor(rstd[:, 0:n], var_eps[:, 0:n], minus_half[:, :].to_broadcast([P, n]),
                              ALU.pow).then_inc(sem["front_rstd"], 1)

        def dve_front_norm(eng, l, j):
            p, after = parts[l], afters[l]
            src = state[SOURCE.get(p["name"], "x")]
            g = p["group"]
            eng.wait_ge(sem["zt_ps"], after["zt_ps"](j, 0))
            if not (p["norm_eps"] or p.get("rms_eps")):
                dve_gate(eng)
                eng.tensor_copy(z[:, 0:g, :], src[:, group_of(l, j), :]).then_inc(sem["z_ready"], 1)
                return
            eng.wait_ge(sem["front_rstd"], after["front_rstd"](j, 1))
            dve_gate(eng)
            for t in range(g):
                if p.get("rms_eps"):
                    ins = eng.tensor_scalar(z[:, t, :], src[:, j * g + t, :], rstd[:, t:t + 1], None,
                                            ALU.mult)
                else:
                    ins = eng.tensor_scalar(z[:, t, :], src[:, j * g + t, :], meanvar[:, t, 0:1],
                                            rstd[:, t:t + 1], ALU.subtract, ALU.mult)
            if p["ctx"] == "normed":
                for t in range(2):
                    ins = eng.tensor_scalar(z_ctx[:, t, :], ctx_raw[:, t, :], meanvar[:, g + t, 0:1],
                                            rstd[:, g + t:g + t + 1], ALU.subtract, ALU.mult)
            ins.then_inc(sem["z_ready"], 1)

        def pe_transpose_front(eng, l, j, bank):
            p, after = parts[l], afters[l]
            eng.wait_ge(sem["z_ready"], after["z_ready"](j, 1))
            for t in range(p["group"]):
                ins = eng.transpose(psum[bank][:, t * P:(t + 1) * P], z[:, t, :], ident)
            if p["ctx"] == "normed":
                for t in range(2):
                    ins = eng.transpose(psum[bank][0:CTX, (2 + t) * P:(3 + t) * P], z_ctx[:, t, :], ident)
            ins.then_inc(sem["zt_ps"], 1)

        def act_front_out(eng, l, j, bank):
            p, after = parts[l], afters[l]
            n = p["group"] * P
            eng.wait_ge(sem["zt_ps"], after["zt_ps"](j, 1))
            if p.get("rms_eps"):
                eng.activation(z_t[:, 0:n], psum[bank][:, 0:n], ACT.Identity, scale=weight(l, "gx"))\
                   .then_inc(sem["zt_ready"], 1)
            elif not p["affine"]:
                eng.activation(z_t[:, 0:n], psum[bank][:, 0:n], ACT.Copy).then_inc(sem["zt_ready"], 1)
            else:
                ins = eng.activation(z_t[:, 0:n], psum[bank][:, 0:n], ACT.Identity,
                                     bias=weight(l, "bx"), scale=weight(l, "gx"))
                if p["kind"] == "attention":
                    rows, at = (CTX, n) if p["ctx"] else (P, 0)
                    ins = eng.activation(y_t[0:rows, 0:n], psum[bank][0:rows, at:at + n], ACT.Identity,
                                         bias=weight(l, "by"), scale=weight(l, "gy"))
                ins.then_inc(sem["zt_ready"], 1)

        def dve_tail(eng, l, i, source):
            p, after = parts[l], afters[l]
            g, k = p["group"], 0
            steps = len(p["adds"]) + p["out_bias"]
            now = source
            for n in range(steps):
                dst = res[:, 0:g, :] if n < steps - 1 or p["store"] != "xo" else \
                    state["xo"][:, group_of(l, i), :]
                if n < len(p["adds"]):
                    other = state[p["adds"][n]][:, group_of(l, i), :]
                else:
                    other = bcast(weight(l, "bo"), 1, g)
                eng.tensor_tensor(dst, now, other, ALU.add).then_inc(sem["tail_step"], 1)
                k += 1
                eng.wait_ge(sem["tail_step"], after["tail_step"](i, k))
                now = res[:, 0:g, :]
            if p["store"] == "xo":
                eng.memset(tail_mark[:, :], 0.0).then_inc(sem["tail_done"], 1)
                return

            def norm(src, dst, r):
                nonlocal k
                dve_gate(eng)
                for t in range(g):
                    ins = eng.bn_stats(t_stats[:, t, :], src(t))
                ins.then_inc(sem["tail_step"], 1)
                k += 1
                eng.wait_ge(sem["tail_step"], after["tail_step"](i, k))
                dve_gate(eng)
                for t in range(g):
                    ins = eng.bn_aggr(t_meanvar[:, t, :], t_stats[:, t, :])
                ins.then_inc(sem["tail_step"], 1)
                k += 1
                eng.wait_ge(sem["tail_rstd"], after["tail_rstd"](i, r + 1))
                dve_gate(eng)
                for t in range(g):
                    ins = eng.tensor_scalar(dst(t), src(t), t_meanvar[:, t, 0:1], t_rstd[:, t:t + 1],
                                            ALU.subtract, ALU.mult)
                ins.then_inc(sem["tail_step"], 1)
                k += 1
                eng.wait_ge(sem["tail_step"], after["tail_step"](i, k))

            def affine(src, dst):
                nonlocal k
                eng.tensor_tensor(res[:, 0:g, :], src, bcast(weight(l, "ln_g"), 1, g), ALU.mult)\
                   .then_inc(sem["tail_step"], 1)
                k += 1
                eng.wait_ge(sem["tail_step"], after["tail_step"](i, k))
                eng.tensor_tensor(dst, res[:, 0:g, :], bcast(weight(l, "ln_b"), 1, g), ALU.add)\
                   .then_inc(sem["tail_step"], 1)
                k += 1
                eng.wait_ge(sem["tail_step"], after["tail_step"](i, k))

            def in_res(t):
                return res[:, t, :]

            def in_state(t):
                return state["x"][:, i * g + t, :]

            if p["store"] == "a":
                norm(in_res, in_res, 0)
                affine(res[:, 0:g, :], state["a"][:, group_of(l, i), :])
            else:
                norm(in_res, in_state, 0)
            if p["name"] == "L0_attn":
                norm(in_state, in_res, 1)
                affine(res[:, 0:g, :], state["a"][:, group_of(l, i), :])
            assert k == after["tail_step"].n
            eng.memset(tail_mark[:, :], 0.0).then_inc(sem["tail_done"], 1)

        def pool_tail_rstd(eng, l, i):
            p, after = parts[l], afters[l]
            if p["store"] == "xo":
                return
            g = p["group"]
            for r in range(after["tail_rstd"].n):
                eng.wait_ge(sem["tail_step"], after["tail_step"](i, len(p["adds"]) + p["out_bias"] + 2 + 3 * r))
                eng.tensor_tensor(t_var_eps[:, 0:g], t_meanvar[:, 0:g, 1],
                                  eps_col[LN_EPS][:, :].to_broadcast([P, g]), ALU.add)\
                   .then_inc(sem["tail_var"], 1)
                eng.wait_ge(sem["tail_var"], after["tail_var"](i, r + 1))
                eng.tensor_tensor(t_rstd[:, 0:g], t_var_eps[:, 0:g],
                                  minus_half[:, :].to_broadcast([P, g]), ALU.pow)\
                   .then_inc(sem["tail_rstd"], 1)


        class AttentionBuffers:
            def __init__(self, p):
                at = [0]

                def cut(n):
                    at[0] += n
                    assert at[0] <= ARENA
                    return arena[:, at[0] - n:at[0]]

                qc, vc = p["qc"], p["vc"]
                self.q = cut(qc * 2 * P).rearrange("p (c e t) -> p c e t", c=qc, e=2)
                self.k = cut(qc * 2 * P).rearrange("p (c e t) -> p c e t", c=qc, e=2)
                self.kb = cut(2 * HEADS * P).rearrange("p (e c r t) -> p e c r t", e=2, c=qc, t=P)
                self.v = cut(2 * vc * P).rearrange("p (e n) -> p e n", e=2)
                self.probs = cut(2 * HEADS * P).rearrange("p (e h t) -> p e h t", e=2, t=P)
                self.probs_t = cut(HEADS * P).rearrange("p (h t) -> p h t", t=P)
                self.o_t = cut(2 * vc * P).rearrange("p (e c t) -> p e c t", e=2, t=P)
                self.max = cut(2 * HEADS).rearrange("p (e h) -> p e h", e=2)
                self.sum = cut(2 * HEADS).rearrange("p (e h) -> p e h", e=2)
                self.rec = cut(2 * HEADS).rearrange("p (e h) -> p e h", e=2)

        def pe_attention(eng, l):
            p, after, b = parts[l], afters[l], AttentionBuffers(parts[l])
            u, o = p["qc"] // 2, p["vc"] // 4
            per_chunk = HEADS // p["qc"]
            kv_rows = CTX if p["ctx"] else P
            y = y_t if p["ctx"] or p["affine"] else z_t
            hv = P * p["vc"] // HEADS
            wq, wk, wv, wo = (weight(l, n) for n in ("wq", "wk", "wv", "wo"))

            def project_qk(j):
                pe_transpose_front(eng, l, j, 7)
                eng.wait_ge(sem["zt_ready"], after["zt_ready"](j, 1))
                if p["ctx"] == "plain":
                    eng.wait_ge(sem["ctx_in"], after["ctx_in"](j, 16))
                eng.wait_ge(sem["v_ev"], after["v_ev"](j, 0))
                for n in range(u):
                    if n:
                        eng.wait_ge(sem["k_ev"], after["k_ev"](j, n))
                    for c in range(2):
                        ins = eng.matmul(psum[4][:, c * 2 * P:(c + 1) * 2 * P],
                                         wk[:, (2 * n + c) * P:(2 * n + c + 1) * P],
                                         y[0:kv_rows, 0:2 * P], start=True, stop=True)
                    ins.then_inc(sem["qk_ps"], 1)
                    if n:
                        eng.wait_ge(sem["q_ev"], after["q_ev"](j, n))
                    for c in range(2):
                        ins = eng.matmul(psum[5][:, c * 2 * P:(c + 1) * 2 * P],
                                         wq[:, (2 * n + c) * P:(2 * n + c + 1) * P],
                                         z_t[:, 0:2 * P], start=True, stop=True)
                    ins.then_inc(sem["qk_ps"], 1)

            def project_v(j):
                for n in range(2 * o):
                    e, half = n // o, n % o
                    if n >= 2:
                        eng.wait_ge(sem["v_ev"], after["v_ev"](j, n - 1))
                    eng.matmul(psum[4 + n % 2][:, :], y[0:kv_rows, e * P:(e + 1) * P],
                               wv[:, half * BANK:(half + 1) * BANK], start=True, stop=True)\
                       .then_inc(sem["v_ps"], 1)

            def front(j):
                project_qk(j)
                eng.wait_ge(sem["k_ev"], after["k_ev"](j, u))
                eng.wait_ge(sem["q_ev"], after["q_ev"](j, u))
                project_v(j)

            def scores(i, e, g):
                n = g * (p["qc"] // 4) // 2
                if e == 0:
                    eng.wait_ge(sem["s_read"], after["s_read"](i, 0))
                else:
                    eng.wait_ge(sem["s_read"], after["s_read"](i, g + 1))
                eng.wait_ge(sem["q_ev"], after["q_ev"](i, n + 1))
                eng.wait_ge(sem["kb_ready"], after["kb_ready"](i, 2 * n + e + 1))
                if p["mask"]:
                    eng.matmul(psum[g][:, :], const_bf("ident"), bcast(const_bf(p["mask"]), 1, 4),
                               start=True, stop=False)
                for c in range(p["qc"] // 4):
                    chunk, w = g * (p["qc"] // 4) + c, per_chunk * P
                    ins = eng.matmul(psum[g][:, c * w:(c + 1) * w], b.q[:, chunk, e, :],
                                     b.kb[:, e, chunk, :, :], start=not p["mask"], stop=True)
                ins.then_inc(sem["s_ps"], 1)

            def transposes(i, e, g):
                n = 4 * e + g
                eng.wait_ge(sem["p_norm"], after["p_norm"](i, 2 * e + g // 2 + 1))
                if n >= 2:
                    eng.wait_ge(sem["t_ev"], after["t_ev"](i, n - 1))
                for h in range(4):
                    ins = eng.transpose(psum[4 + n % 2][:, h * P:(h + 1) * P],
                                        b.probs[:, e, 4 * g + h, :], ident)
                ins.then_inc(sem["t_ps"], 1)

            def values(i, e, g):
                eng.wait_ge(sem["t_ev"], after["t_ev"](i, 4 * e + g + 1))
                n = e * o + g * o // 4
                first = g % (4 // o) == 0
                if first and n == 0:
                    eng.wait_ge(sem["tail_done"], after["tail_done"](i, 0))
                elif first and n >= 2:
                    eng.wait_ge(sem["o_ev"], after["o_ev"](i, n - 1))
                for h in range(4 * g, 4 * g + 4):
                    row, chunk = h * hv % P, h * hv // P
                    ins = eng.matmul(psum[6 + n % 2][row:row + hv, chunk % 4 * P:(chunk % 4 + 1) * P],
                                     b.v[:, e, h * hv:(h + 1) * hv], b.probs_t[:, h, :],
                                     start=True, stop=True)
                if g % (4 // o) == 4 // o - 1:
                    ins.then_inc(sem["pv_ps"], 1)

            def output(i):
                eng.wait_ge(sem["o_ev"], after["o_ev"](i, 2 * o))
                for e in range(2):
                    for c in range(p["vc"]):
                        ins = eng.matmul(psum[6][:, e * P:(e + 1) * P], b.o_t[:, e, c, :],
                                         wo[:, c * P:(c + 1) * P], start=(c == 0),
                                         stop=(c == p["vc"] - 1))
                ins.then_inc(sem["o_ps"], 1)

            def body(i, more):
                for e in range(2):
                    for g in range(4):
                        scores(i, e, g)
                if more:
                    project_qk(i + 1)
                    eng.wait_ge(sem["k_ev"], after["k_ev"](i + 1, u))
                    eng.wait_ge(sem["q_ev"], after["q_ev"](i + 1, u))
                else:
                    eng.wait_ge(sem["v_ev"], after["v_ev"](i, 2 * o))
                for e in range(2):
                    transposes(i, e, 0)
                    for g in range(4):
                        if g < 3:
                            transposes(i, e, g + 1)
                        values(i, e, g)
                if more:
                    eng.wait_ge(sem["t_ev"], after["t_ev"](i, 8))
                    project_v(i + 1)
                output(i)

            run_steps(eng, batch // 2, front, body)

        def act_attention(eng, l):
            p, after, b = parts[l], afters[l], AttentionBuffers(parts[l])
            u, o = p["qc"] // 2, p["vc"] // 4

            def q_out(j, n):
                eng.wait_ge(sem["qk_ps"], after["qk_ps"](j, 2 * n + 2))
                src = psum[5][:, :].rearrange("p (c e t) -> p c e t", c=2, e=2)
                if p["qkv_bias"]:
                    bq = weight(l, "bq")
                    for c in range(2):
                        ins = eng.activation(b.q[:, 2 * n + c, :, :], src[:, c, :, :], ACT.Identity,
                                             bias=bq[:, 2 * n + c:2 * n + c + 1])
                else:
                    ins = eng.activation(b.q[:, 2 * n:2 * n + 2, :, :], src, ACT.Copy)
                ins.then_inc(sem["q_ev"], 1)

            def v_out(j):
                for n in range(2 * o):
                    e, half = n // o, n % o
                    eng.wait_ge(sem["v_ps"], after["v_ps"](j, n + 1))
                    eng.activation(b.v[:, e, half * BANK:(half + 1) * BANK], psum[4 + n % 2][:, :],
                                   ACT.Copy).then_inc(sem["v_ev"], 1)

            def front(j):
                act_front_out(eng, l, j, 7)
                for n in range(u):
                    q_out(j, n)
                v_out(j)

            def exps(i, e, g):
                dst = b.probs[:, e, 4 * g:4 * g + 4, :]
                if p["taylor"]:
                    eng.wait_ge(sem["s_ps"], after["s_ps"](i, 4 * e + g + 1))
                    eng.activation(dst, psum[g][:, :].rearrange("p (h t) -> p h t", h=4), ACT.Square,
                                   bias=1.0, scale=0.25).then_inc(sem["s_read"], 1)
                else:
                    eng.wait_ge(sem["s_read"], after["s_read"](i, 4 * e + g + 1))
                    eng.activation(dst, dst, ACT.Exp, scale=p["scale"]).then_inc(sem["p_exp"], 1)

            def body(i, more):
                for g in range(4):
                    exps(i, 0, g)
                exps(i, 1, 0)
                if more:
                    act_front_out(eng, l, i + 1, 7)
                exps(i, 1, 1)
                if more:
                    for n in range(u // 2):
                        q_out(i + 1, n)
                exps(i, 1, 2)
                if more:
                    for n in range(u // 2, u):
                        q_out(i + 1, n)
                exps(i, 1, 3)
                for n in range(8):
                    eng.wait_ge(sem["t_ps"], after["t_ps"](i, n + 1))
                    g = n % 4
                    eng.activation(b.probs_t[:, 4 * g:4 * g + 4, :],
                                   psum[4 + n % 2][:, :].rearrange("p (h t) -> p h t", h=4), ACT.Copy)\
                       .then_inc(sem["t_ev"], 1)
                if more:
                    v_out(i + 1)

            run_steps(eng, batch // 2, front, body)

        def dve_attention(eng, l):
            p, after, b = parts[l], afters[l], AttentionBuffers(parts[l])
            u, o = p["qc"] // 2, p["vc"] // 4

            def k_out(j, n):
                eng.wait_ge(sem["qk_ps"], after["qk_ps"](j, 2 * n + 1))
                eng.wait_ge(sem["kb_ready"], after["kb_ready"](j, 0))
                dst = b.k[:, 2 * n:2 * n + 2, :, :].rearrange("p c e t -> p c (e t)")
                src = psum[4][:, :].rearrange("p (c n) -> p c n", c=2)
                if p["qkv_bias"]:
                    ins = eng.tensor_tensor(dst, src, bcast(weight(l, "bk")[:, 2 * n:2 * n + 2], 2, 2 * P),
                                            ALU.add)
                else:
                    ins = eng.tensor_copy(dst, src)
                ins.then_inc(sem["k_ev"], 1)

            def front(j):
                dve_front_stats(eng, l, j)
                dve_front_norm(eng, l, j)
                for n in range(u):
                    k_out(j, n)

            def shift(i, e, g):
                n = 4 * e + g
                eng.wait_ge(sem["s_ps"], after["s_ps"](i, n + 1))
                src = psum[g][:, :].rearrange("p (h t) -> p h t", h=4)
                m = b.max[:, e, 4 * g:4 * g + 4]
                eng.tensor_reduce(m, src, AX_X, ALU.max).then_inc(sem["s_max"], 1)
                eng.wait_ge(sem["s_max"], after["s_max"](i, n + 1))
                eng.tensor_tensor(b.probs[:, e, 4 * g:4 * g + 4, :], src, bcast(m, 2, P), ALU.subtract)\
                   .then_inc(sem["s_read"], 1)

            def taylor_mask(i, e, g):
                n = 4 * e + g
                eng.wait_ge(sem["s_read"], after["s_read"](i, n + 1))
                dst = b.probs[:, e, 4 * g:4 * g + 4, :]
                eng.scalar_tensor_tensor(out=dst, in0=dst, scalar=1.0, in1=bcast(const("lower"), 1, 4),
                                         op0=ALU.add, op1=ALU.mult).then_inc(sem["s_mask"], 1)

            first_pass = taylor_mask if p["taylor"] else shift

            def sums(i, e, half):
                n = 2 * e + half
                hs = slice(8 * half, 8 * half + 8)
                if p["taylor"]:
                    eng.wait_ge(sem["s_mask"], after["s_mask"](i, 4 * e + 2 * half + 2))
                else:
                    eng.wait_ge(sem["p_exp"], after["p_exp"](i, 4 * e + 2 * half + 2))
                eng.tensor_reduce(b.sum[:, e, hs], b.probs[:, e, hs, :], AX_X, ALU.add)\
                   .then_inc(sem["p_sum"], 1)
                eng.wait_ge(sem["p_sum"], after["p_sum"](i, n + 1))
                if p["taylor"]:
                    eng.tensor_scalar(b.max[:, e, hs], b.sum[:, e, hs], 2e-12, None, ALU.add)\
                       .then_inc(sem["p_eps"], 1)
                    eng.wait_ge(sem["p_eps"], after["p_eps"](i, n + 1))
                    eng.reciprocal(b.rec[:, e, hs], b.max[:, e, hs]).then_inc(sem["p_rec"], 1)
                else:
                    eng.reciprocal(b.rec[:, e, hs], b.sum[:, e, hs]).then_inc(sem["p_rec"], 1)

            def outputs(i):
                for n in range(2 * o):
                    e, half = n // o, n % o
                    eng.wait_ge(sem["pv_ps"], after["pv_ps"](i, n + 1))
                    dst = b.o_t[:, e, 4 * half:4 * half + 4, :]
                    src = psum[6 + n % 2][:, :].rearrange("p (c t) -> p c t", c=4)
                    if p["qkv_bias"]:
                        ins = eng.tensor_tensor(dst, src, bcast(weight(l, "bv"), 2, P), ALU.add)
                    else:
                        ins = eng.tensor_copy(dst, src)
                    ins.then_inc(sem["o_ev"], 1)

            def body(i, more):
                if more:
                    dve_front_stats(eng, l, i + 1)
                first_pass(i, 0, 0)
                first_pass(i, 0, 1)
                if more:
                    dve_front_norm(eng, l, i + 1)
                first_pass(i, 0, 2)
                first_pass(i, 0, 3)
                first_pass(i, 1, 0)
                sums(i, 0, 0)
                first_pass(i, 1, 1)
                sums(i, 0, 1)
                if more:
                    for n in range(u // 2):
                        k_out(i + 1, n)
                first_pass(i, 1, 2)
                if more:
                    for n in range(u // 2, u):
                        k_out(i + 1, n)
                first_pass(i, 1, 3)
                sums(i, 1, 0)
                sums(i, 1, 1)
                outputs(i)
                eng.wait_ge(sem["o_ps"], after["o_ps"](i, 1))
                dve_tail(eng, l, i, psum[6][:, 0:2 * P].rearrange("p (e c) -> p e c", e=2))

            run_steps(eng, batch // 2, front, body)

        def pool_attention(eng, l):
            p, after, b = parts[l], afters[l], AttentionBuffers(parts[l])
            u, r = p["qc"] // 2, HEADS // p["qc"]
            rows = const(f"block{r}")

            def spread_k(j):
                for n in range(u):
                    for e in range(2):
                        eng.wait_ge(sem["k_ev"], after["k_ev"](j, n + 1))
                        for c in range(2 * n, 2 * n + 2):
                            ins = eng.tensor_tensor(b.kb[:, e, c, :, :], bcast(b.k[:, c, e, :], 1, r),
                                                    bcast(rows, 2, P), ALU.mult)
                        ins.then_inc(sem["kb_ready"], 1)

            def front(j):
                pool_front_rstd(eng, l, j)
                spread_k(j)

            def normalise(i, e, half):
                n = 2 * e + half
                hs = slice(8 * half, 8 * half + 8)
                probs = b.probs[:, e, hs, :]
                eng.wait_ge(sem["p_rec"], after["p_rec"](i, n + 1))
                done = sem["p_mul"] if p["post_mask"] else sem["p_norm"]
                eng.tensor_tensor(probs, probs, bcast(b.rec[:, e, hs], 2, P), ALU.mult)\
                   .then_inc(done, 1)
                if p["post_mask"]:
                    eng.wait_ge(sem["p_mul"], after["p_mul"](i, n + 1))
                    pool_gate(eng)
                    eng.affine_select(out=probs, in_=probs, compare_op=ALU.is_gt, fill=0.0, base=0,
                                      pattern=[[0, 8], [1, P]], channel_multiplier=-1)\
                       .then_inc(sem["p_norm"], 1)

            def body(i, more):
                if more:
                    pool_front_rstd(eng, l, i + 1)
                for e in range(2):
                    for half in range(2):
                        normalise(i, e, half)
                if more:
                    spread_k(i + 1)
                pool_tail_rstd(eng, l, i)

            run_steps(eng, batch // 2, front, body)


        class ExpertBuffers:
            def __init__(self):
                at = [0]

                def cut(n):
                    at[0] += n
                    return arena[:, at[0] - n:at[0]]

                self.gate = cut(2 * BANK).rearrange("p (b n) -> p b n", b=2)
                self.h = cut(2 * 4 * BANK).rearrange("p (b c n) -> p b c n", b=2, c=4)
                self.acc = cut(4 * P).rearrange("p (t c) -> p t c", t=4)
                self.logits = cut(4 * 9).rearrange("p (t e) -> p t e", t=4)
                self.shifted = cut(4 * 9).rearrange("p (t e) -> p t e", t=4)
                self.exps = cut(4 * 9).rearrange("p (t e) -> p t e", t=4)
                self.top = cut(4 * 8).rearrange("p (t e) -> p t e", t=4)
                self.top_at = cut(4 * 8).rearrange("p (t e) -> p t e", t=4).bitcast(U32)
                self.index = cut(4 * 2).rearrange("p (t e) -> p t e", t=4)
                self.hot = cut(2 * 4 * 8).rearrange("p (k t e) -> p k t e", k=2, t=4)
                self.chosen = cut(4 * 8).rearrange("p (t e) -> p t e", t=4)
                self.picked = cut(4 * 8).rearrange("p (t e) -> p t e", t=4)
                self.den = cut(4 * 2).rearrange("p (t e) -> p t e", t=4)
                self.rden = cut(4 * 2).rearrange("p (t e) -> p t e", t=4)
                self.w = cut(4 * 9).rearrange("p (t e) -> p t e", t=4)

        def expert_chunks(p):
            out_, n, at = [], 0, 0
            for e, sizes_ in enumerate(p["chunks"]):
                for c, size in enumerate(sizes_):
                    out_.append((e, c, n, size, at))
                    n += 1
                    at += size * (2 if p["gated"] else 1)
            return out_

        def pe_experts(eng, l):
            p, after, b = parts[l], afters[l], ExpertBuffers()
            chunks, ne = expert_chunks(p), len(p["chunks"])
            up_w, down_w = weight(l, "up"), weight(l, "down")

            def front(j):
                pe_transpose_front(eng, l, j, 4)

            def wait_hidden(i, n):
                if p["gated"]:
                    eng.wait_ge(sem["h_ready"], after["h_ready"](i, n))
                else:
                    eng.wait_ge(sem["act_ev"], after["act_ev"](i, n))

            def up(i, e):
                for ex, _, n, size, at in chunks:
                    if ex != e:
                        continue
                    if p["gated"]:
                        wait_hidden(i, max(n - 1, 0))
                        for k in range(2):
                            ins = eng.matmul(psum[2 * (n % 2) + k][0:size, :],
                                             up_w[:, at + k * size:at + (k + 1) * size], z_t[:, :],
                                             start=True, stop=True)
                    else:
                        wait_hidden(i, max(n - 3, 0))
                        ins = eng.matmul(psum[n % 4][0:size, :], up_w[:, at:at + size], z_t[:, :],
                                         start=True, stop=True)
                    ins.then_inc(sem["up_ps"], 1)

            def down(i, e):
                mine = [c for c in chunks if c[0] == e]
                if p["routing"]:
                    eng.wait_ge(sem["acc"], after["acc"](i, max(e - 1, 0)))
                else:
                    eng.wait_ge(sem["tail_done"], after["tail_done"](i, 0))
                wait_hidden(i, mine[-1][2] + 1)
                for t in range(4):
                    for _, c, n, size, _ in mine:
                        ins = eng.matmul(psum[6 + e % 2][:, t * P:(t + 1) * P],
                                         b.h[0:size, e % 2, c, t * P:(t + 1) * P],
                                         down_w[0:size, n * P:(n + 1) * P], start=(c == 0),
                                         stop=(c == len(mine) - 1))
                ins.then_inc(sem["y_ps"], 1)

            def body(i, more):
                eng.wait_ge(sem["zt_ready"], after["zt_ready"](i, 1))
                if p["routing"]:
                    eng.wait_ge(sem["route"], after["route"](i, 0))
                    ng = 8 + p["shared"]
                    for t in range(4):
                        ins = eng.matmul(psum[5][:, t * ng:(t + 1) * ng], z_t[:, t * P:(t + 1) * P],
                                         weight(l, "gate"), start=True, stop=True)
                    ins.then_inc(sem["gate_ps"], 1)
                for e in range(ne):
                    up(i, e)
                    if e:
                        down(i, e - 1)
                if more:
                    front(i + 1)
                down(i, ne - 1)

            run_steps(eng, batch // 4, front, body)

        def act_experts(eng, l):
            p, after, b = parts[l], afters[l], ExpertBuffers()
            chunks, ne = expert_chunks(p), len(p["chunks"])

            def front(j):
                act_front_out(eng, l, j, 4)

            def hidden(i, e):
                for ex, c, n, size, _ in chunks:
                    if ex != e:
                        continue
                    eng.wait_ge(sem["up_ps"], after["up_ps"](i, n + 1))
                    if p["gated"]:
                        dst, src = b.gate[0:size, n % 2, :], psum[2 * (n % 2)][0:size, :]
                    else:
                        dst, src = b.h[0:size, e % 2, c, :], psum[n % 4][0:size, :]
                    if p["hidden_bias"]:
                        ins = eng.activation(dst, src, p["func"], bias=weight(l, "bh")[:, n:n + 1])
                    else:
                        ins = eng.activation(dst, src, p["func"])
                    ins.then_inc(sem["act_ev"], 1)

            def body(i, more):
                for e in range(ne):
                    hidden(i, e)
                    if e == 0 and p["routing"]:
                        eng.wait_ge(sem["route"], after["route"](i, 4))
                        ins = eng.activation(b.exps[:, :, 0:8], b.shifted[:, :, 0:8], ACT.Exp)
                        if p["shared"]:
                            ins = eng.activation(b.exps[:, :, 8:9], b.logits[:, :, 8:9], ACT.Exp,
                                                 scale=-1.0)
                        ins.then_inc(sem["route_exp"], 1)
                if more:
                    front(i + 1)

            run_steps(eng, batch // 4, front, body)

        def dve_experts(eng, l):
            p, after, b = parts[l], afters[l], ExpertBuffers()
            chunks, ne = expert_chunks(p), len(p["chunks"])
            ng = 8 + p["shared"]

            def front(j):
                dve_front_stats(eng, l, j)
                dve_front_norm(eng, l, j)

            def route_before(i):
                eng.wait_ge(sem["gate_ps"], after["gate_ps"](i, 1))
                eng.tensor_copy(b.logits[:, :, 0:ng], psum[5][:, 0:4 * ng].rearrange("p (t e) -> p t e", t=4))\
                   .then_inc(sem["route"], 1)
                eng.wait_ge(sem["route"], after["route"](i, 1))
                dve_gate(eng)
                for t in range(4):
                    ins = eng.max(b.top[:, t, :], b.logits[:, t, 0:8])
                ins.then_inc(sem["route"], 1)
                eng.wait_ge(sem["route"], after["route"](i, 2))
                dve_gate(eng)
                for t in range(4):
                    ins = eng.max_index(b.top_at[:, t, :], b.top[:, t, :], b.logits[:, t, 0:8])
                ins.then_inc(sem["route"], 1)
                eng.tensor_tensor(b.shifted[:, :, 0:8], b.logits[:, :, 0:8],
                                  b.top[:, :, 0:1].to_broadcast([P, 4, 8]), ALU.subtract)\
                   .then_inc(sem["route"], 1)
                eng.wait_ge(sem["route"], after["route"](i, 3))
                eng.tensor_copy(b.index[:, :, :], b.top_at[:, :, 0:2]).then_inc(sem["route"], 1)
                eng.wait_ge(sem["route"], after["route"](i, 5))
                for k in range(2):
                    ins = eng.tensor_tensor(b.hot[:, k, :, :], bcast(const("iota"), 1, 4),
                                            b.index[:, :, k:k + 1].to_broadcast([P, 4, 8]),
                                            ALU.is_equal)
                ins.then_inc(sem["route"], 1)
                eng.wait_ge(sem["route"], after["route"](i, 6))
                eng.tensor_tensor(b.chosen[:, :, :], b.hot[:, 0, :, :], b.hot[:, 1, :, :], ALU.add)\
                   .then_inc(sem["route"], 1)

            def route_after(i):
                k = 7
                eng.wait_ge(sem["route_exp"], after["route_exp"](i, 1))
                eng.wait_ge(sem["route"], after["route"](i, k))
                eng.tensor_tensor(b.picked[:, :, :], b.exps[:, :, 0:8], b.chosen[:, :, :], ALU.mult)\
                   .then_inc(sem["route"], 1)
                k += 1
                eng.wait_ge(sem["route"], after["route"](i, k))
                over = b.picked if p["routing"] == "top" else b.exps
                eng.tensor_reduce(b.den[:, :, 0], over[:, :, 0:8], AX_X, ALU.add).then_inc(sem["route"], 1)
                k += 1
                eng.wait_ge(sem["route"], after["route"](i, k))
                if p["shared"]:
                    eng.tensor_scalar(b.den[:, :, 1], b.exps[:, :, 8], 1.0, None, ALU.add)\
                       .then_inc(sem["route"], 1)
                    k += 1
                    eng.wait_ge(sem["route"], after["route"](i, k))
                nd = 1 + p["shared"]
                eng.reciprocal(b.rden[:, :, 0:nd], b.den[:, :, 0:nd]).then_inc(sem["route"], 1)
                k += 1
                eng.wait_ge(sem["route"], after["route"](i, k))
                eng.tensor_tensor(b.w[:, :, 0:8], b.picked[:, :, :],
                                  b.rden[:, :, 0:1].to_broadcast([P, 4, 8]), ALU.mult).then_inc(sem["route"], 1)
                k += 1
                if p["shared"]:
                    eng.tensor_copy(b.w[:, :, 8], b.rden[:, :, 1]).then_inc(sem["route"], 1)
                    k += 1
                eng.wait_ge(sem["route"], after["route"](i, k))
                dve_gate(eng)
                assert k == after["route"].n

            def hidden(i, e):
                for ex, c, n, size, _ in chunks:
                    if ex == e:
                        eng.wait_ge(sem["act_ev"], after["act_ev"](i, n + 1))
                        eng.tensor_tensor(b.h[0:size, e % 2, c, :], b.gate[0:size, n % 2, :],
                                          psum[2 * (n % 2) + 1][0:size, :], ALU.mult)\
                           .then_inc(sem["h_ready"], 1)

            def accumulate(i, e):
                eng.wait_ge(sem["y_ps"], after["y_ps"](i, e + 1))
                if e:
                    eng.wait_ge(sem["acc"], after["acc"](i, e))
                for t in range(4):
                    y, w = psum[6 + e % 2][:, t * P:(t + 1) * P], b.w[:, t, e:e + 1]
                    if e == 0:
                        ins = eng.tensor_scalar(b.acc[:, t, :], y, w, None, ALU.mult)
                    else:
                        ins = eng.scalar_tensor_tensor(out=b.acc[:, t, :], in0=y, scalar=w,
                                                       in1=b.acc[:, t, :], op0=ALU.mult, op1=ALU.add)
                ins.then_inc(sem["acc"], 1)

            def body(i, more):
                if p["routing"]:
                    route_before(i)
                elif more:
                    front(i + 1)
                for e in range(ne):
                    if p["gated"]:
                        hidden(i, e)
                    if not p["routing"]:
                        continue
                    if e == 1:
                        route_after(i)
                    if e:
                        accumulate(i, e - 1)
                    if more and e == 2:
                        dve_front_stats(eng, l, i + 1)
                    if more and e == 3:
                        dve_front_norm(eng, l, i + 1)
                if p["routing"]:
                    accumulate(i, ne - 1)
                    eng.wait_ge(sem["acc"], after["acc"](i, ne))
                    source = b.acc[:, :, :]
                else:
                    eng.wait_ge(sem["y_ps"], after["y_ps"](i, 1))
                    source = psum[6][:, :].rearrange("p (t c) -> p t c", t=4)
                dve_tail(eng, l, i, source)

            run_steps(eng, batch // 4, front, body)

        def pool_norms(eng, l):
            def front(j):
                pool_front_rstd(eng, l, j)

            def body(i, more):
                if more:
                    front(i + 1)
                pool_tail_rstd(eng, l, i)

            if parts[l]["norm_eps"] or parts[l].get("rms_eps"):
                run_steps(eng, batch // 4, front, body)
            else:
                with eng.Fori(0, batch // 4) as i:
                    pool_tail_rstd(eng, l, i)


        class SingleBuffers:
            def __init__(self):
                self.q, self.k, self.v, self.probs, self.probs_t = (
                    arena[:, n * BANK:(n + 1) * BANK].rearrange("p (e t) -> p e t", e=4)
                    for n in range(5))
                self.max, self.sum, self.rec = (
                    arena[:, 5 * BANK + 4 * n:5 * BANK + 4 * n + 4] for n in range(3))

        def quads(bank):
            return psum[bank][:, :].rearrange("p (e t) -> p e t", e=4)

        def pe_single(eng, l):
            after, b = afters[l], SingleBuffers()

            def project_qk(j):
                pe_transpose_front(eng, l, j, 4)
                eng.wait_ge(sem["zt_ready"], after["zt_ready"](j, 1))
                eng.wait_ge(sem["q_ev"], after["q_ev"](j, 0))
                eng.matmul(psum[0][:, :], weight(l, "wq"), z_t[:, :], start=True, stop=True)\
                   .then_inc(sem["q_ps"], 1)
                eng.wait_ge(sem["ctx_in"], after["ctx_in"](j, 16))
                eng.wait_ge(sem["k_ev"], after["k_ev"](j, 0))
                eng.matmul(psum[1][:, :], weight(l, "wk"), y_t[0:CTX, :], start=True, stop=True)\
                   .then_inc(sem["k_ps"], 1)

            def project_v(j):
                eng.wait_ge(sem["v_ev"], after["v_ev"](j, 0))
                for e in range(4):
                    ins = eng.matmul(psum[2][:, e * P:(e + 1) * P], y_t[0:CTX, e * P:(e + 1) * P],
                                     weight(l, "wv"), start=True, stop=True)
                ins.then_inc(sem["v_ps"], 1)

            def front(j):
                project_qk(j)
                project_v(j)

            def body(i, more):
                eng.wait_ge(sem["q_ev"], after["q_ev"](i, 1))
                eng.wait_ge(sem["k_ev"], after["k_ev"](i, 1))
                eng.wait_ge(sem["s_read"], after["s_read"](i, 0))
                for e in range(4):
                    ins = eng.matmul(psum[3][:, e * P:(e + 1) * P], b.q[:, e, :], b.k[:, e, :],
                                     start=True, stop=True)
                ins.then_inc(sem["s_ps"], 1)
                if more:
                    project_qk(i + 1)
                eng.wait_ge(sem["p_norm"], after["p_norm"](i, 1))
                for e in range(4):
                    ins = eng.transpose(psum[5][:, e * P:(e + 1) * P], b.probs[:, e, :], ident)
                ins.then_inc(sem["t_ps"], 1)
                eng.wait_ge(sem["t_ev"], after["t_ev"](i, 1))
                eng.wait_ge(sem["v_ev"], after["v_ev"](i, 1))
                eng.wait_ge(sem["tail_done"], after["tail_done"](i, 0))
                for e in range(4):
                    ins = eng.matmul(psum[6][:, e * P:(e + 1) * P], b.probs_t[:, e, :], b.v[:, e, :],
                                     start=True, stop=True)
                ins.then_inc(sem["pv_ps"], 1)
                if more:
                    project_v(i + 1)

            run_steps(eng, batch // 4, front, body)

        def act_single(eng, l):
            after, b = afters[l], SingleBuffers()

            def front(j):
                act_front_out(eng, l, j, 4)
                eng.wait_ge(sem["q_ps"], after["q_ps"](j, 1))
                eng.activation(b.q, quads(0), ACT.Identity, bias=weight(l, "bq")).then_inc(sem["q_ev"], 1)

            def body(i, more):
                eng.wait_ge(sem["s_read"], after["s_read"](i, 1))
                eng.activation(b.probs, b.probs, ACT.Exp).then_inc(sem["p_exp"], 1)
                if more:
                    front(i + 1)
                eng.wait_ge(sem["t_ps"], after["t_ps"](i, 1))
                eng.activation(b.probs_t, quads(5), ACT.Copy).then_inc(sem["t_ev"], 1)

            run_steps(eng, batch // 4, front, body)

        def dve_single(eng, l):
            after, b = afters[l], SingleBuffers()

            def k_out(j):
                eng.wait_ge(sem["k_ps"], after["k_ps"](j, 1))
                eng.tensor_scalar(b.k, quads(1), weight(l, "bk"), None, ALU.add)\
                   .then_inc(sem["k_ev"], 1)

            def v_out(j):
                eng.wait_ge(sem["v_ps"], after["v_ps"](j, 1))
                eng.tensor_tensor(b.v, quads(2), bcast(weight(l, "bv"), 1, 4), ALU.add)\
                   .then_inc(sem["v_ev"], 1)

            def front(j):
                dve_front_norm(eng, l, j)
                k_out(j)
                v_out(j)

            def body(i, more):
                if more:
                    dve_front_norm(eng, l, i + 1)
                eng.wait_ge(sem["s_ps"], after["s_ps"](i, 1))
                eng.tensor_reduce(b.max, quads(3), AX_X, ALU.max).then_inc(sem["s_max"], 1)
                eng.wait_ge(sem["s_max"], after["s_max"](i, 1))
                eng.tensor_tensor(b.probs, quads(3), bcast(b.max, 2, P), ALU.subtract)\
                   .then_inc(sem["s_read"], 1)
                eng.wait_ge(sem["p_exp"], after["p_exp"](i, 1))
                eng.tensor_reduce(b.sum, b.probs, AX_X, ALU.add).then_inc(sem["p_sum"], 1)
                eng.wait_ge(sem["p_sum"], after["p_sum"](i, 1))
                eng.reciprocal(b.rec, b.sum).then_inc(sem["p_rec"], 1)
                eng.wait_ge(sem["p_rec"], after["p_rec"](i, 1))
                eng.tensor_tensor(b.probs, b.probs, bcast(b.rec, 2, P), ALU.mult)\
                   .then_inc(sem["p_norm"], 1)
                if more:
                    k_out(i + 1)
                eng.wait_ge(sem["pv_ps"], after["pv_ps"](i, 1))
                dve_tail(eng, l, i, quads(6))
                if more:
                    v_out(i + 1)

            run_steps(eng, batch // 4, front, body)


        class CosineBuffers:
            def __init__(self):
                def cut(n, m):
                    return arena[:, n * BANK:(n + m) * BANK]

                self.kv = cut(0, 2).rearrange("p (e n) -> p e n", e=4)
                self.q, self.q_cos, self.q_sin, self.k_cos, self.k_sin, self.kv_cos, self.kv_sin = (
                    cut(n, 1).rearrange("p (e t) -> p e t", e=4) for n in range(2, 9))

        def pe_cosine(eng, l):
            after, b = afters[l], CosineBuffers()

            def front(j):
                eng.wait_ge(sem["zt_ready"], after["zt_ready"](j, 1))
                eng.wait_ge(sem["kv_ev"], after["kv_ev"](j, 0))
                for pair in range(2):
                    for e in range(2 * pair, 2 * pair + 2):
                        ins = eng.matmul(psum[pair][:, e % 2 * 2 * P:(e % 2 + 1) * 2 * P],
                                         z_t[:, e * P:(e + 1) * P], weight(l, "wkv"), start=True,
                                         stop=True)
                    ins.then_inc(sem["kv_ps"], 1)
                eng.wait_ge(sem["q_ev"], after["q_ev"](j, 0))
                eng.matmul(psum[2][:, :], weight(l, "wq"), z_t[:, :], start=True, stop=True)\
                   .then_inc(sem["q_ps"], 1)

            def first(j):
                pe_transpose_front(eng, l, j, 4)
                front(j)

            def body(i, more):
                eng.wait_ge(sem["kcs"], after["kcs"](i, 1))
                eng.wait_ge(sem["kv_ev"], after["kv_ev"](i, 2))
                eng.wait_ge(sem["kvb_ev"], after["kvb_ev"](i, 0))
                for bank, k in ((3, b.k_cos), (5, b.k_sin)):
                    for e in range(4):
                        ins = eng.matmul(psum[bank][:, e * P:(e + 1) * P], k[:, e, :],
                                         b.kv[:, e, P:2 * P], start=True, stop=True)
                ins.then_inc(sem["kvb_ps"], 1)
                if more:
                    pe_transpose_front(eng, l, i + 1, 4)
                eng.wait_ge(sem["kvb_ev"], after["kvb_ev"](i, 1))
                eng.wait_ge(sem["qcs"], after["qcs"](i, 1))
                eng.wait_ge(sem["tail_done"], after["tail_done"](i, 0))
                for e in range(4):
                    eng.matmul(psum[6][:, e * P:(e + 1) * P], b.q_cos[:, e, :], b.kv_cos[:, e, :],
                               start=True, stop=False)
                    ins = eng.matmul(psum[6][:, e * P:(e + 1) * P], b.q_sin[:, e, :],
                                     b.kv_sin[:, e, :], start=False, stop=True)
                ins.then_inc(sem["o_ps"], 1)
                if more:
                    front(i + 1)

            run_steps(eng, batch // 4, first, body)

        def act_cosine(eng, l):
            after, b = afters[l], CosineBuffers()

            def q_out(j):
                eng.wait_ge(sem["q_ps"], after["q_ps"](j, 1))
                eng.wait_ge(sem["qcs"], after["qcs"](j, 0))
                eng.activation(b.q, quads(2), ACT.Relu, bias=weight(l, "bq")).then_inc(sem["q_ev"], 1)

            def front(j):
                act_front_out(eng, l, j, 4)
                q_out(j)

            def body(i, more):
                if more:
                    front(i + 1)

            run_steps(eng, batch // 4, front, body)

        def dve_cosine(eng, l):
            after, b = afters[l], CosineBuffers()

            def kv_out(j):
                bias = weight(l, "bkv")
                for pair in range(2):
                    eng.wait_ge(sem["kv_ps"], after["kv_ps"](j, pair + 1))
                    eng.tensor_tensor(b.kv[:, 2 * pair:2 * pair + 2, :],
                                      psum[pair][:, :].rearrange("p (e n) -> p e n", e=2),
                                      bcast(bias, 1, 2), ALU.add).then_inc(sem["kv_ev"], 1)
                eng.wait_ge(sem["kv_ev"], after["kv_ev"](j, 2))
                eng.tensor_scalar(b.k_cos, b.kv[:, :, 0:P], 0.0, const("cos_col"), ALU.max, ALU.mult)
                eng.tensor_scalar(b.k_sin, b.kv[:, :, 0:P], 0.0, const("sin_col"), ALU.max, ALU.mult)\
                   .then_inc(sem["kcs"], 1)

            def q_weights(j):
                eng.wait_ge(sem["q_ev"], after["q_ev"](j, 1))
                eng.tensor_tensor(b.q_cos, b.q, bcast(const("cos_row"), 1, 4), ALU.mult)
                eng.tensor_tensor(b.q_sin, b.q, bcast(const("sin_row"), 1, 4), ALU.mult)\
                   .then_inc(sem["qcs"], 1)

            def front(j):
                dve_front_norm(eng, l, j)
                kv_out(j)
                q_weights(j)

            def body(i, more):
                if more:
                    dve_front_norm(eng, l, i + 1)
                eng.wait_ge(sem["kvb_ps"], after["kvb_ps"](i, 1))
                blocks_ = bcast(const("block8"), 1, 4)
                eng.tensor_tensor(b.kv_cos, quads(3), blocks_, ALU.mult)
                eng.tensor_tensor(b.kv_sin, quads(5), blocks_, ALU.mult).then_inc(sem["kvb_ev"], 1)
                eng.wait_ge(sem["o_ps"], after["o_ps"](i, 1))
                if more:
                    kv_out(i + 1)
                    q_weights(i + 1)
                dve_tail(eng, l, i, quads(6))

            run_steps(eng, batch // 4, front, body)

        @block.tensor
        def _(eng):
            for l, p in enumerate(parts):
                part_start(eng, l)
                {"attention": pe_attention, "experts": pe_experts, "single": pe_single,
                 "cosine": pe_cosine}[p["kind"]](eng, l)

        @block.scalar
        def _(eng):
            for l, p in enumerate(parts):
                part_start(eng, l)
                {"attention": act_attention, "experts": act_experts, "single": act_single,
                 "cosine": act_cosine}[p["kind"]](eng, l)

        @block.vector
        def _(eng):
            eng.wait_ge(consts_in, 32)
            eng.tensor_copy(const_bf_sb[:, :], arena[:, 0:const_bf_cols]).then_inc(consts_cast, 1)
            eng.wait_ge(x_in, 16)
            for l, p in enumerate(parts):
                part_start(eng, l)
                {"attention": dve_attention, "experts": dve_experts, "single": dve_single,
                 "cosine": dve_cosine}[p["kind"]](eng, l)

        @block.gpsimd
        def _(eng):
            for n, signal in sem.items():
                if n != "ctx_in":
                    eng.sem_inc(signal, 1)
            for e, col in eps_col.items():
                eng.memset(col[:, :], e)
            eng.memset(minus_half[:, :], -0.5).then_inc(primed, 1)
            for l, p in enumerate(parts):
                part_start(eng, l)
                (pool_attention if p["kind"] == "attention" else pool_norms)(eng, l)



def const_arrays():
    row, col = np.arange(P)[:, None], np.arange(P)[None, :]
    theta = (np.float32(np.pi / 2) * np.arange(P, dtype=np.float32) / np.float32(P)).astype(np.float32)
    cos, sin = np.cos(theta).astype(np.float32), np.sin(theta).astype(np.float32)
    f = {"ident": row == col, "lower": col <= row, "block4": row // 32 == np.arange(4),
         "block2": row // 64 == np.arange(2), "block8": row // 8 == col // 8,
         "iota": np.broadcast_to(np.arange(8), (P, 8)),
         "cos_row": np.broadcast_to(cos, (P, P)), "sin_row": np.broadcast_to(sin, (P, P)),
         "cos_col": cos[:, None], "sin_col": sin[:, None]}
    causal = np.where(col <= row, 0.0, NEG)
    window = np.where((col <= row) & (col > row - 32), 0.0, NEG)
    g = {"ident": row == col, "causal": causal, "window": window}
    return (np.concatenate([np.asarray(f[n], np.float32) for n, _ in CONSTS], 1),
            np.concatenate([np.asarray(g[n], np.float32) for n, _ in CONSTS_BF], 1))


def weight_arrays(name, a):
    def heads(w, d, to=32):
        w = w.reshape(w.shape[0], HEADS, d)
        return np.pad(w, ((0, 0), (0, 0), (0, to - d))).reshape(w.shape[0], HEADS * to)

    def rows(w):
        return w.reshape(-1, P, w.shape[1]).transpose(1, 0, 2).reshape(P, -1)

    def padded_rows(w, d):
        w = w.reshape(HEADS, d, -1)
        return rows(np.pad(w, ((0, 0), (0, 32 - d), (0, 0))).reshape(HEADS * 32, -1))

    def per_row(v):
        return v.reshape(-1, P).T

    def wide(v):
        return np.broadcast_to(v[None, :], (P, v.size))

    def col(v):
        return v[:, None]

    def projected(w):
        return w.transpose(1, 0, 2).reshape(w.shape[1], -1)

    def moe(gate_up, down, chunks):
        ups, downs = [], []
        for (g, u), d, sizes in zip(gate_up, down, chunks):
            at = 0
            for c in sizes:
                ups += [g[at:at + c].T] + ([u[at:at + c].T] if u is not None else [])
                downs.append(np.pad(d[:, at:at + c].T, ((0, P - c), (0, 0))))
                at += c
        return dict(up=np.concatenate(ups, 1), down=np.concatenate(downs, 1))

    chunks = {p["name"]: p.get("chunks") for p in PARTS}[name]
    if name == "L0_attn":
        q, k, v = np.split(a["L0_attn_W_qkv"], 3, axis=1)
        return dict(wq=heads(q, 8), wk=heads(k, 8), wv=heads(v, 8), wo=padded_rows(a["L0_attn_W_out"], 8),
                    ln_g=wide(a["L0_xattn_ln1_g"]), ln_b=wide(a["L0_xattn_ln1_b"]))
    if name in ("L0_self", "L0_cross"):
        t = "L0_xattn_a1_" if name == "L0_self" else "L0_xattn_a2_"
        w = dict(wq=projected(a[t + "wq"]), wk=projected(a[t + "wk"]), wv=projected(a[t + "wv"]),
                 wo=rows(a[t + "li1_w"]), bo=wide(a[t + "li1_b"]), gx=col(a[t + "lnx_g"]),
                 bx=col(a[t + "lnx_b"]), gy=col(a[t + "lny_g"]), by=col(a[t + "lny_b"]))
        return w
    if name in ("L0_mlp1", "L0_mlp2"):
        t = "L0_xattn_a1_" if name == "L0_mlp1" else "L0_xattn_a2_"
        w = dict(up=a[t + "li2_w"], down=rows(a[t + "li3_w"]), bh=per_row(a[t + "li2_b"]),
                 bo=wide(a[t + "li3_b"]), gx=col(a[t + "ln3_g"]), bx=col(a[t + "ln3_b"]))
        if name == "L0_mlp1":
            w.update(ln_g=wide(a["L0_xattn_ln2_g"]), ln_b=wide(a["L0_xattn_ln2_b"]))
        return w
    if name == "L0_ffn":
        gu, inner = a["L0_ffn_experts_gate_up"], a["L0_ffn_experts_gate_up"].shape[1] // 2
        w = moe([(e[:inner], e[inner:]) for e in gu] + [(a["L0_ffn_shared_gate_w"], a["L0_ffn_shared_up_w"])],
                list(a["L0_ffn_experts_down"]) + [a["L0_ffn_shared_down_w"]], chunks)
        w["gate"] = np.concatenate([a["L0_ffn_gate_w"], a["L0_ffn_shared_expert_gate_w"]], 0).T
        return w
    if name == "L1_attn":
        q, k, v = np.split(a["L1_attn_w_attn"].T, 3, axis=1)
        bq, bk, bv = (per_row(heads(v_[None, :], 8)[0]) for v_ in np.split(a["L1_attn_b_attn"], 3))
        return dict(wq=heads(q, 8), wk=heads(k, 8), wv=heads(v, 8), wo=padded_rows(a["L1_attn_w_proj"].T, 8),
                    bq=bq, bk=bk, bv=bv, bo=wide(a["L1_attn_b_proj"]))
    if name == "L1_mlp":
        return dict(up=a["L1_attn_w_fc"].T, down=rows(a["L1_attn_w_mlp_proj"].T),
                    bh=per_row(a["L1_attn_b_fc"]), bo=wide(a["L1_attn_b_mlp_proj"]))
    if name == "L1_cross":
        return dict(wq=a["L1_xattn_Wq"], wk=a["L1_xattn_Wk"], wv=a["L1_xattn_Wv"], wo=rows(a["L1_xattn_Wo"]),
                    bo=wide(a["L1_xattn_bo"]))
    if name == "L1_ffn":
        w = moe(list(zip(a["L1_ffn_W1"], a["L1_ffn_W2"])), a["L1_ffn_W3"], chunks)
        return dict(w, gate=a["L1_ffn_gate_w"].T, gx=col(a["L1_ffn_rms_w"]))
    if name == "L2_attn":
        return dict(wq=heads(a["L2_attn_Wq"].T, 16), wk=heads(a["L2_attn_Wk"].T, 16),
                    wv=a["L2_attn_Wv"].T, wo=rows(a["L2_attn_Wo"].T))
    if name in ("L2_cross", "L3_cross"):
        t = name[:2] + "_xattn_"
        return dict(wq=a[t + "Wq"], wk=a[t + "Wk"], wv=a[t + "Wv"], bq=col(a[t + "bq"]),
                    bk=col(a[t + "bk"]), bv=wide(a[t + "bv"]))
    if name == "L2_ffn":
        inner = a["L2_ffn_w1"].shape[1] // 2
        w = moe([(e[:inner], e[inner:]) for e in a["L2_ffn_w1"]], a["L2_ffn_w2"], chunks)
        return dict(w, gate=a["L2_ffn_router_w"].T)
    if name == "L3_attn":
        return dict(wq=a["L3_attn_Wq"].T,
                    wkv=np.concatenate([a["L3_attn_Wk"].T, a["L3_attn_Wv"].T], 1),
                    bq=col(a["L3_attn_bq"]),
                    bkv=wide(np.concatenate([a["L3_attn_bk"], a["L3_attn_bv"]])))
    if name == "L3_ffn":
        w = moe([(e, None) for e in a["L3_ffn_w1"]], a["L3_ffn_w2"], chunks)
        return dict(w, gate=a["L3_ffn_router_w"].T)
    raise ValueError(name)


def weight_block(p, a):
    w = weight_arrays(p["name"], a)
    fields = []
    for name, r, c in p["weights"]:
        assert w[name].shape == (r, c), (p["name"], name, w[name].shape, r, c)
        fields.append(np.pad(w[name], ((0, P - r), (0, 0))))
    return np.ascontiguousarray(np.concatenate(fields, 1))


def kernel(**inputs):
    import concourse.bacc as bacc
    from concourse.bass_utils import run_bass_kernel_spmd

    a = {k: np.asarray(v) for k, v in inputs.items()}
    x, ctx = a["x"], a["ctx_512"]
    batch = x.shape[0]
    consts, consts_bf = const_arrays()
    arrays = {"in_x": np.ascontiguousarray(x), "in_ctx": np.ascontiguousarray(ctx),
              "in_ctx_t": np.ascontiguousarray(ctx.transpose(2, 0, 1).reshape(CTX, -1)),
              "in_consts": consts, "in_consts_bf": consts_bf}
    for p in PARTS:
        arrays[f"in_w_{p['name']}"] = weight_block(p, a)

    nc = bacc.Bacc("TRN2", target_bir_lowering=False, num_devices=1)
    dram = {n: nc.dram_tensor(n, v.shape, mybir.dt.from_np(v.dtype), kind="ExternalInput").ap()
            for n, v in arrays.items()}
    out = nc.dram_tensor("out", x.shape, F32, kind="ExternalOutput").ap()
    build_program(nc, dram["in_x"], dram["in_ctx"], dram["in_ctx_t"], dram["in_consts"],
                  dram["in_consts_bf"], [dram[f"in_w_{p['name']}"] for p in PARTS], out, PARTS, batch)
    return run_bass_kernel_spmd(nc, [arrays], core_ids=[0]).results[0]["out"]
```

```python
import itertools
from contextlib import ExitStack

import numpy as np

import concourse.bass as bass
from concourse import mybir

F32 = mybir.dt.float32
BF16 = mybir.dt.bfloat16
U32 = mybir.dt.uint32
ALU = mybir.AluOpType
ACT = mybir.ActivationFunctionType
AX_X = mybir.AxisListType.X

P = 128
CTX = 64
HEADS = 16
BANK = 512
NEG = -1e30
LN_EPS = 1e-5
GATES = 16



def attention(name, **k):
    p = dict(kind="attention", name=name, group=2, qc=4, vc=4, scale=1.0, norm_eps=None, mask=None,
             post_mask=False, taylor=False, ctx=None, affine=False, qkv_bias=False, out_bias=False,
             adds=("x",), store="x")
    p.update(k)
    kv_rows = CTX if p["ctx"] else P
    w = [("wq", P, p["qc"] * P), ("wk", kv_rows, p["qc"] * P), ("wv", kv_rows, p["vc"] * P),
         ("wo", P, p["vc"] * P)]
    if p["affine"]:
        w += [("gx", P, 1), ("bx", P, 1), ("gy", kv_rows, 1), ("by", kv_rows, 1)]
    if p["qkv_bias"]:
        w += [("bq", P, p["qc"]), ("bk", P, p["qc"]), ("bv", P, p["vc"])]
    if p["out_bias"]:
        w += [("bo", P, P)]
    if name == "L0_attn":
        w += [("ln_g", P, P), ("ln_b", P, P)]
    p["weights"] = w
    return p


def experts(name, chunks, **k):
    p = dict(kind="experts", name=name, group=4, chunks=chunks, func=ACT.Gelu, gated=False,
             norm_eps=None, rms_eps=None, affine=False, hidden_bias=False, out_bias=False,
             routing=None, shared=False, adds=("x",), store="x", ctx=None)
    p.update(k)
    sizes = [c for e in chunks for c in e]
    w = [("up", P, sum(sizes) * (2 if p["gated"] else 1)), ("down", P, len(sizes) * P)]
    if p["routing"]:
        w += [("gate", P, 8 + p["shared"])]
    if p["affine"]:
        w += [("gx", P, 1), ("bx", P, 1)]
    if p["rms_eps"]:
        w += [("gx", P, 1)]
    if p["hidden_bias"]:
        w += [("bh", P, len(sizes))]
    if p["out_bias"]:
        w += [("bo", P, P)]
    if p["store"] == "a":
        w += [("ln_g", P, P), ("ln_b", P, P)]
    p["weights"] = w
    return p


def single(name):
    return dict(kind="single", name=name, group=4, ctx="plain", adds=("x",), store="x",
                norm_eps=None, affine=False, out_bias=False,
                weights=[("wq", P, P), ("wk", CTX, P), ("wv", CTX, P), ("bq", P, 1), ("bk", P, 1),
                         ("bv", P, P)])


def cosine(name):
    return dict(kind="cosine", name=name, group=4, ctx=None, adds=("x",), store="x",
                norm_eps=None, affine=False, out_bias=False,
                weights=[("wq", P, P), ("wkv", P, 2 * P), ("bq", P, 1), ("bkv", P, 2 * P)])


THIRDS = [118, 117, 117]
PARTS = [
    attention("L0_attn", qc=1, scale=8 ** -0.5, mask="window"),
    attention("L0_self", scale=32 ** -0.5, norm_eps=LN_EPS, affine=True, post_mask=True,
              out_bias=True, adds=("a",), store="xo"),
    experts("L0_mlp1", [[P] * 4], norm_eps=LN_EPS, affine=True, hidden_bias=True, out_bias=True,
            adds=("a", "xo"), store="a"),
    attention("L0_cross", scale=32 ** -0.5, norm_eps=LN_EPS, affine=True, ctx="normed",
              out_bias=True, adds=("a",), store="xo"),
    experts("L0_mlp2", [[P] * 4], norm_eps=LN_EPS, affine=True, hidden_bias=True, out_bias=True,
            adds=("a", "xo", "x")),
    experts("L0_ffn", [[88, 88]] * 8 + [THIRDS], func=ACT.Silu, gated=True, routing="all",
            shared=True),
    attention("L1_attn", qc=1, scale=8 ** -0.5, norm_eps=1e-10, mask="causal", qkv_bias=True,
              out_bias=True, store="xo"),
    experts("L1_mlp", [[P] * 4], func=ACT.Gelu_apprx_tanh, norm_eps=1e-10, hidden_bias=True,
            out_bias=True, adds=("xo", "x")),
    attention("L1_cross", qc=8, vc=8, scale=64 ** -0.5, ctx="plain", out_bias=True),
    experts("L1_ffn", [THIRDS] * 8, func=ACT.Silu, gated=True, routing="top", rms_eps=1e-6,
            adds=("x", "x")),
    attention("L2_attn", qc=2, vc=8, taylor=True),
    single("L2_cross"),
    experts("L2_ffn", [[P] * 2] * 8, func=ACT.Silu, gated=True, routing="all"),
    cosine("L3_attn"),
    single("L3_cross"),
    experts("L3_ffn", [[P] * 2] * 8, routing="top"),
]
SOURCE = {"L0_self": "a", "L0_mlp1": "xo", "L0_cross": "a", "L0_mlp2": "xo", "L1_mlp": "xo"}

CONSTS = [("ident", P), ("lower", P), ("heads16", 16), ("heads8", 8), ("heads4", 4), ("heads2", 2),
          ("diagonal", P), ("iota", 8),
          ("cos_row", P), ("sin_row", P), ("cos_col", 1), ("sin_col", 1)]
CONSTS_BF = [("ident", P), ("causal", P), ("window", P)]


def columns(fields):
    at, place = 0, {}
    for f in fields:
        place[f[0]] = (at, f[-2] if len(f) == 3 else P, f[-1])
        at += f[-1]
    return place, at



def tail_steps(p):
    n = len(p["adds"]) + p["out_bias"] - 1
    if p["store"] != "xo":
        n += 3
        if p["store"] == "a" or p["name"] == "L0_attn":
            n += 2
        if p["name"] == "L0_attn":
            n += 3
    return n


def units(p):
    return max(p["qc"] // 2, 1)


def signal_counts(p):
    n = dict(z_ready=1, zt_ps=1, zt_ready=1, tail_read=1, tail_step=tail_steps(p), tail_done=1)
    if p["store"] != "xo":
        n.update(tail_var=1, tail_rstd=1)
        if p["name"] == "L0_attn":
            n.update(tail_var=2, tail_rstd=2)
    if p["norm_eps"] or p.get("rms_eps"):
        n.update(front_stats=1, front_aggr=1, front_var=1, front_rstd=1)
        if p.get("rms_eps"):
            n.update(front_sq=2)
    if p["ctx"]:
        n.update(ctx_in=16)
    if p["kind"] == "attention":
        u, o = units(p), p["vc"] // 4
        n.update(qk_ps=2 * u, qk_ev=2 * u, kb_ready=2 * u, s_ps=8, s_read=8, p_exp=8, p_sum=4,
                 p_rec=4, p_norm=4, t_ps=8, t_ev=8, pv_ps=2 * o, o_ev=2 * o, v_ps=2 * o,
                 v_ev=2 * o, o_ps=1)
        if p["taylor"]:
            n.update(s_mask=8, p_eps=4)
            del n["p_exp"]
        else:
            n.update(s_max=8)
        if p["post_mask"]:
            n.update(p_mul=4)
    elif p["kind"] == "experts":
        chunks, ne = sum(map(len, p["chunks"])), len(p["chunks"])
        n.update(up_ps=chunks, act_ev=chunks, y_ps=ne)
        if p["gated"]:
            n.update(h_ready=chunks)
        if p["routing"]:
            n.update(gate_ps=1, route=11 + 2 * p["shared"], route_exp=1, acc=ne)
    elif p["kind"] == "single":
        n.update(q_ps=1, k_ps=1, q_ev=1, k_ev=1, v_ps=1, v_ev=1, s_ps=1, s_max=1, s_read=1,
                 p_exp=1, p_sum=1, p_rec=1, p_norm=1, t_ps=1, t_ev=1, pv_ps=1)
    elif p["kind"] == "cosine":
        n.update(kv_ps=2, kv_ev=2, kcs=1, q_ps=1, q_ev=1, qcs=1, o_ps=1, kvb_ps=1, kvb_ev=1)
    return n


class After:

    def __init__(self, base, per_step):
        self.base, self.n = base, per_step

    def __call__(self, i, k):
        return i * self.n + (self.base + k)


def bcast(ap, axis, count):
    ap = ap.unsqueeze(axis)
    shape = list(ap.shape)
    shape[axis] = count
    return ap.to_broadcast(shape)


def run_tailed(eng, steps, front, body, tail):
    front(0)
    body(0, False, True)
    with eng.Fori(1, steps - 1) as i:
        body(i, True, True)
    body(steps - 1, True, False)
    tail(steps - 1)


def run_steps(eng, steps, front, body):
    front(0)
    with eng.Fori(0, steps - 1) as i:
        body(i, True)
    body(steps - 1, False)



def build_program(nc, x, ctx, ctx_t, consts, consts_bf, weights, out, parts, batch):
    with ExitStack() as stack:
        def sb(name, shape, dt=F32):
            return stack.enter_context(nc.sbuf_tensor(name, shape, dt))

        state = {n: sb(f"{n}_state", [P, batch, P]) for n in ("x", "a", "xo")}
        sizes = [columns(p["weights"])[1] for p in parts]
        blocks = [sb(f"weights{b}", [P, max(sizes[b::2] + [1])]) for b in range(2)]
        const_place, const_cols = columns(CONSTS)
        const_bf_place, const_bf_cols = columns(CONSTS_BF)
        const_sb = sb("consts", [P, const_cols])
        const_bf_sb = sb("consts_bf", [P, const_bf_cols], BF16)

        def const(name):
            at, _, n = const_place[name]
            return const_sb[:, at:at + n]

        def const_bf(name):
            at, _, n = const_bf_place[name]
            return const_bf_sb[:, at:at + n]

        ident = const("ident")
        z = sb("z", [P, 4, P])
        z_ctx = sb("z_ctx", [P, 2, CTX])
        ctx_raw = sb("ctx_raw", [P, 2, CTX])
        z_t = sb("z_t", [P, BANK])
        y_t = sb("y_t", [P, BANK])
        stats = sb("stats", [P, 4, 6])
        meanvar = sb("meanvar", [P, 4, 2])
        var_eps = sb("var_eps", [P, 4])
        rstd = sb("rstd", [P, 4])
        res = sb("res", [P, 4, P])
        t_stats = sb("t_stats", [P, 4, 6])
        t_meanvar = sb("t_meanvar", [P, 4, 2])
        t_var_eps = sb("t_var_eps", [P, 4])
        t_rstd = sb("t_rstd", [P, 4])
        eps_col = {e: sb(f"eps{n}", [P, 1]) for n, e in enumerate((LN_EPS, 1e-10, 1e-6))}
        minus_half = sb("minus_half", [P, 1])
        gate_dve = sb("gate_dve", [P, GATES])
        gate_at = itertools.cycle(range(GATES))
        gate_pool = sb("gate_pool", [P, 2])
        tail_mark = sb("tail_mark", [P, 1])
        ARENA = 18 * 1024 + 256
        arena = sb("arena", [P, ARENA])

        psum = [stack.enter_context(nc.psum_tensor(f"bank{b}", [P, BANK], F32)) for b in range(8)]

        counts = [signal_counts(p) for p in parts]
        names = sorted({n for c in counts for n in c})
        sem = {n: stack.enter_context(nc.semaphore(n)) for n in names}
        weights_in = [stack.enter_context(nc.semaphore(f"weights_in{b}")) for b in range(2)]
        x_in = stack.enter_context(nc.semaphore("x_in"))
        consts_in = stack.enter_context(nc.semaphore("consts_in"))
        consts_cast = stack.enter_context(nc.semaphore("consts_cast"))
        out_done = stack.enter_context(nc.semaphore("out_done"))
        primed = stack.enter_context(nc.semaphore("primed"))
        bases = {n: int(n != "ctx_in") for n in names}
        afters = []
        for p, c in zip(parts, counts):
            afters.append({n: After(bases[n], k) for n, k in c.items()})
            for n, k in c.items():
                bases[n] += k * (batch // p["group"])

        def weight(l, name):
            at, rows, n = columns(parts[l]["weights"])[0][name]
            return blocks[l % 2][0:rows, at:at + n]

        def dve_gate(eng):
            at = next(gate_at)
            eng.memset(gate_dve[:, at:at + 1], 0.0)

        def pool_gate(eng):
            eng.tensor_tensor(gate_pool[:, 0:1], minus_half[:, :], minus_half[:, :], ALU.add)

        def all_tails(l):
            return afters[l]["tail_done"](batch // parts[l]["group"], 0)

        def part_start(eng, l):
            if l:
                eng.wait_ge(sem["tail_done"], all_tails(l - 1))
            else:
                eng.wait_ge(primed, 1)
                eng.wait_ge(consts_in, 32)
                eng.wait_ge(consts_cast, 1)
            eng.wait_ge(weights_in[l % 2], 16 * (l // 2 + 1))

        def group_of(l, i):
            g = parts[l]["group"]
            return bass.ds(i * g, g)

        block = stack.enter_context(nc.Block())

        @block.sync
        def _(eng):
            def load_weights(l):
                at = columns(parts[l]["weights"])[1]
                eng.dma_start(blocks[l % 2][:, 0:at], weights[l]).then_inc(weights_in[l % 2], 16)

            eng.dma_start(const_sb[:, :], consts).then_inc(consts_in, 16)
            eng.dma_start(arena[:, 0:const_bf_cols], consts_bf).then_inc(consts_in, 16)
            load_weights(0)
            eng.dma_start(state["x"][:, :, :], x.rearrange("b s c -> s b c")).then_inc(x_in, 16)
            for l, p in enumerate(parts):
                after, steps, g = afters[l], batch // p["group"], p["group"]
                if l:
                    eng.wait_ge(sem["tail_done"], all_tails(l - 1))
                if l + 1 < len(parts):
                    load_weights(l + 1)
                if p["ctx"]:
                    def load_ctx(j, first=False, p=p, after=after, g=g):
                        if not first:
                            if p["ctx"] == "normed":
                                eng.wait_ge(sem["z_ready"], after["z_ready"](j, 0))
                            else:
                                eng.wait_ge(sem["v_ps"], after["v_ps"](j, 0))
                        if p["ctx"] == "normed":
                            src = ctx[bass.ds(j * g, g), :, :].rearrange("b s c -> s b c")
                            eng.dma_start(ctx_raw[:, :, :], src).then_inc(sem["ctx_in"], 16)
                        else:
                            eng.dma_start(y_t[0:CTX, 0:g * P], ctx_t[:, bass.ds(j * (g * P), g * P)])\
                               .then_inc(sem["ctx_in"], 16)
                    load_ctx(0, True)
                    with eng.Fori(1, steps) as j:
                        load_ctx(j)
            eng.wait_ge(sem["tail_done"], all_tails(len(parts) - 1))
            eng.dma_start(out.rearrange("b s c -> s b c"), state["x"][:, :, :]).then_inc(out_done, 16)
            eng.wait_ge(out_done, 16)


        def dve_front_stats(eng, l, j):
            p, after = parts[l], afters[l]
            if not (p["norm_eps"] or p.get("rms_eps")):
                return
            src = state[SOURCE.get(p["name"], "x")]
            g = p["group"]
            for t in range(g):
                ins = eng.bn_stats(stats[:, t, :], src[:, j * g + t, :])
            if p["ctx"] == "normed":
                eng.wait_ge(sem["ctx_in"], after["ctx_in"](j, 16))
                for t in range(2):
                    ins = eng.bn_stats(stats[:, g + t, :], ctx_raw[:, t, :])
            ins.then_inc(sem["front_stats"], 1)
            n = g + (2 if p["ctx"] == "normed" else 0)
            eng.wait_ge(sem["front_stats"], after["front_stats"](j, 1))
            dve_gate(eng)
            for t in range(n):
                ins = eng.bn_aggr(meanvar[:, t, :], stats[:, t, :])
            ins.then_inc(sem["front_aggr"], 1)
            if p.get("rms_eps"):
                eng.wait_ge(sem["front_aggr"], after["front_aggr"](j, 1))
                eng.tensor_tensor(rstd[:, 0:g], meanvar[:, 0:g, 0], meanvar[:, 0:g, 0], ALU.mult)\
                   .then_inc(sem["front_sq"], 1)
                eng.wait_ge(sem["front_sq"], after["front_sq"](j, 1))
                eng.tensor_tensor(meanvar[:, 0:g, 1], meanvar[:, 0:g, 1], rstd[:, 0:g], ALU.add)\
                   .then_inc(sem["front_sq"], 1)

        def pool_front_rstd(eng, l, j):
            p, after = parts[l], afters[l]
            eps = p["norm_eps"] or p.get("rms_eps")
            if not eps:
                return
            n = p["group"] + (2 if p["ctx"] == "normed" else 0)
            if p.get("rms_eps"):
                eng.wait_ge(sem["front_sq"], after["front_sq"](j, 2))
            else:
                eng.wait_ge(sem["front_aggr"], after["front_aggr"](j, 1))
            eng.tensor_tensor(var_eps[:, 0:n], meanvar[:, 0:n, 1],
                              eps_col[eps][:, :].to_broadcast([P, n]), ALU.add)\
               .then_inc(sem["front_var"], 1)
            eng.wait_ge(sem["front_var"], after["front_var"](j, 1))
            eng.tensor_tensor(rstd[:, 0:n], var_eps[:, 0:n], minus_half[:, :].to_broadcast([P, n]),
                              ALU.pow).then_inc(sem["front_rstd"], 1)

        def dve_front_norm(eng, l, j):
            p, after = parts[l], afters[l]
            src = state[SOURCE.get(p["name"], "x")]
            g = p["group"]
            eng.wait_ge(sem["zt_ps"], after["zt_ps"](j, 0))
            if not (p["norm_eps"] or p.get("rms_eps")):
                dve_gate(eng)
                eng.tensor_copy(z[:, 0:g, :], src[:, group_of(l, j), :]).then_inc(sem["z_ready"], 1)
                return
            eng.wait_ge(sem["front_rstd"], after["front_rstd"](j, 1))
            dve_gate(eng)
            for t in range(g):
                if p.get("rms_eps"):
                    ins = eng.tensor_scalar(z[:, t, :], src[:, j * g + t, :], rstd[:, t:t + 1], None,
                                            ALU.mult)
                else:
                    ins = eng.tensor_scalar(z[:, t, :], src[:, j * g + t, :], meanvar[:, t, 0:1],
                                            rstd[:, t:t + 1], ALU.subtract, ALU.mult)
            if p["ctx"] == "normed":
                for t in range(2):
                    ins = eng.tensor_scalar(z_ctx[:, t, :], ctx_raw[:, t, :], meanvar[:, g + t, 0:1],
                                            rstd[:, g + t:g + t + 1], ALU.subtract, ALU.mult)
            ins.then_inc(sem["z_ready"], 1)

        def pe_transpose_front(eng, l, j, bank):
            p, after = parts[l], afters[l]
            eng.wait_ge(sem["z_ready"], after["z_ready"](j, 1))
            for t in range(p["group"]):
                ins = eng.transpose(psum[bank][:, t * P:(t + 1) * P], z[:, t, :], ident)
            if p["ctx"] == "normed":
                for t in range(2):
                    ins = eng.transpose(psum[bank][0:CTX, (2 + t) * P:(3 + t) * P], z_ctx[:, t, :], ident)
            ins.then_inc(sem["zt_ps"], 1)

        def act_front_out(eng, l, j, bank):
            p, after = parts[l], afters[l]
            n = p["group"] * P
            eng.wait_ge(sem["zt_ps"], after["zt_ps"](j, 1))
            if p.get("rms_eps"):
                eng.activation(z_t[:, 0:n], psum[bank][:, 0:n], ACT.Identity, scale=weight(l, "gx"))\
                   .then_inc(sem["zt_ready"], 1)
            elif not p["affine"]:
                eng.activation(z_t[:, 0:n], psum[bank][:, 0:n], ACT.Copy).then_inc(sem["zt_ready"], 1)
            else:
                ins = eng.activation(z_t[:, 0:n], psum[bank][:, 0:n], ACT.Identity,
                                     bias=weight(l, "bx"), scale=weight(l, "gx"))
                if p["kind"] == "attention":
                    rows, at = (CTX, n) if p["ctx"] else (P, 0)
                    ins = eng.activation(y_t[0:rows, 0:n], psum[bank][0:rows, at:at + n], ACT.Identity,
                                         bias=weight(l, "by"), scale=weight(l, "gy"))
                ins.then_inc(sem["zt_ready"], 1)


        def norm_step(l, r):
            return len(parts[l]["adds"]) + parts[l]["out_bias"] - 1 + 3 * r

        def dve_tail_add(eng, l, i, source):
            p, after = parts[l], afters[l]
            g, steps, now = p["group"], len(p["adds"]) + p["out_bias"], source
            for n in range(steps):
                dst = res[:, 0:g, :] if n < steps - 1 or p["store"] != "xo" else \
                    state["xo"][:, group_of(l, i), :]
                if n < len(p["adds"]):
                    other = state[p["adds"][n]][:, group_of(l, i), :]
                else:
                    other = bcast(weight(l, "bo"), 1, g)
                if n == 1:
                    eng.wait_ge(sem["tail_read"], after["tail_read"](i, 1))
                elif n:
                    eng.wait_ge(sem["tail_step"], after["tail_step"](i, n - 1))
                ins = eng.tensor_tensor(dst, now, other, ALU.add)
                ins.then_inc(sem["tail_step"] if n else sem["tail_read"], 1)
                now = res[:, 0:g, :]
            if p["store"] == "xo":
                if steps > 1:
                    eng.wait_ge(sem["tail_step"], after["tail_step"](i, steps - 1))
                else:
                    eng.wait_ge(sem["tail_read"], after["tail_read"](i, 1))
                eng.memset(tail_mark[:, :], 0.0).then_inc(sem["tail_done"], 1)

        def tail_source(l, i, r, t):
            return state["x"][:, i * parts[l]["group"] + t, :] if r else res[:, t, :]

        def dve_tail_stats(eng, l, i, r=0):
            p, after = parts[l], afters[l]
            if p["store"] == "xo":
                return
            k = norm_step(l, r)
            if k:
                eng.wait_ge(sem["tail_step"], after["tail_step"](i, k))
            else:
                eng.wait_ge(sem["tail_read"], after["tail_read"](i, 1))
            dve_gate(eng)
            for t in range(p["group"]):
                ins = eng.bn_stats(t_stats[:, t, :], tail_source(l, i, r, t))
            ins.then_inc(sem["tail_step"], 1)
            eng.wait_ge(sem["tail_step"], after["tail_step"](i, k + 1))
            dve_gate(eng)
            for t in range(p["group"]):
                ins = eng.bn_aggr(t_meanvar[:, t, :], t_stats[:, t, :])
            ins.then_inc(sem["tail_step"], 1)

        def pool_tail_rstd(eng, l, i, r=0):
            p, after = parts[l], afters[l]
            if p["store"] == "xo":
                return
            g = p["group"]
            eng.wait_ge(sem["tail_step"], after["tail_step"](i, norm_step(l, r) + 2))
            eng.tensor_tensor(t_var_eps[:, 0:g], t_meanvar[:, 0:g, 1],
                              eps_col[LN_EPS][:, :].to_broadcast([P, g]), ALU.add)\
               .then_inc(sem["tail_var"], 1)
            eng.wait_ge(sem["tail_var"], after["tail_var"](i, r + 1))
            eng.tensor_tensor(t_rstd[:, 0:g], t_var_eps[:, 0:g],
                              minus_half[:, :].to_broadcast([P, g]), ALU.pow)\
               .then_inc(sem["tail_rstd"], 1)

        def dve_tail_norm(eng, l, i, r=0):
            p, after = parts[l], afters[l]
            if p["store"] == "xo":
                return
            g, k = p["group"], norm_step(l, r) + 2
            in_place = r or p["store"] == "a"
            eng.wait_ge(sem["tail_rstd"], after["tail_rstd"](i, r + 1))
            dve_gate(eng)
            for t in range(g):
                dst = res[:, t, :] if in_place else state["x"][:, i * g + t, :]
                ins = eng.tensor_scalar(dst, tail_source(l, i, r, t), t_meanvar[:, t, 0:1],
                                        t_rstd[:, t:t + 1], ALU.subtract, ALU.mult)
            ins.then_inc(sem["tail_step"], 1)
            k += 1
            if in_place:
                eng.wait_ge(sem["tail_step"], after["tail_step"](i, k))
                eng.tensor_tensor(res[:, 0:g, :], res[:, 0:g, :], bcast(weight(l, "ln_g"), 1, g),
                                  ALU.mult).then_inc(sem["tail_step"], 1)
                k += 1
                eng.wait_ge(sem["tail_step"], after["tail_step"](i, k))
                eng.tensor_tensor(state["a"][:, group_of(l, i), :], res[:, 0:g, :],
                                  bcast(weight(l, "ln_b"), 1, g), ALU.add)\
                   .then_inc(sem["tail_step"], 1)
                k += 1
            if k == after["tail_step"].n:
                eng.wait_ge(sem["tail_step"], after["tail_step"](i, k))
                eng.memset(tail_mark[:, :], 0.0).then_inc(sem["tail_done"], 1)

        def pool_whole_tail(eng, l, i):
            for r in range(1 + (parts[l]["name"] == "L0_attn")):
                pool_tail_rstd(eng, l, i, r)

        QK_BANKS = (4, 5, 6, 7)
        T_BANKS = (4, 5, 0, 1, 0, 1, 4, 5)

        class AttentionBuffers:
            def __init__(self, p):
                at = [0]

                def cut(n):
                    at[0] += n
                    assert at[0] <= ARENA
                    return arena[:, at[0] - n:at[0]]

                qc, vc = p["qc"], p["vc"]
                self.q = cut(qc * 2 * P).rearrange("p (c e t) -> p c e t", c=qc, e=2)
                self.k = cut(qc * 2 * P).rearrange("p (c e t) -> p c e t", c=qc, e=2)
                self.kb = cut(2 * HEADS * P).rearrange("p (e c r t) -> p e c r t", e=2, c=qc, t=P)
                self.v = cut(2 * vc * P).rearrange("p (e n) -> p e n", e=2)
                self.probs = cut(2 * HEADS * P).rearrange("p (e h t) -> p e h t", e=2, t=P)
                self.probs_t = cut(HEADS * P).rearrange("p (h t) -> p h t", t=P)
                self.o_t = cut(2 * vc * P).rearrange("p (e c t) -> p e c t", e=2, t=P)
                self.max = cut(2 * HEADS).rearrange("p (e h) -> p e h", e=2)
                self.sum = cut(2 * HEADS).rearrange("p (e h) -> p e h", e=2)
                self.rec = cut(2 * HEADS).rearrange("p (e h) -> p e h", e=2)

        def pe_attention(eng, l):
            p, after, b = parts[l], afters[l], AttentionBuffers(parts[l])
            u, o, cpu = units(p), p["vc"] // 4, min(p["qc"], 2)
            per_chunk = HEADS // p["qc"]
            kv_rows = CTX if p["ctx"] else P
            y = y_t if p["ctx"] or p["affine"] else z_t
            hv = P * p["vc"] // HEADS
            wq, wk, wv, wo = (weight(l, n) for n in ("wq", "wk", "wv", "wo"))

            def project_qk(j):
                pe_transpose_front(eng, l, j, 7)
                eng.wait_ge(sem["zt_ready"], after["zt_ready"](j, 1))
                if p["ctx"] == "plain":
                    eng.wait_ge(sem["ctx_in"], after["ctx_in"](j, 16))
                eng.wait_ge(sem["v_ev"], after["v_ev"](j, 0))
                for n in range(u):
                    for k, (w, src) in enumerate(((wk, y[0:kv_rows, 0:2 * P]), (wq, z_t[:, 0:2 * P]))):
                        if n >= 2:
                            eng.wait_ge(sem["qk_ev"], after["qk_ev"](j, 2 * n + k - 3))
                        bank = psum[QK_BANKS[(2 * n + k) % 4]]
                        for c in range(cpu):
                            at = (cpu * n + c) * P
                            ins = eng.matmul(bank[:, c * 2 * P:(c + 1) * 2 * P], w[:, at:at + P], src,
                                             start=True, stop=True)
                        ins.then_inc(sem["qk_ps"], 1)

            def project_v(j, e):
                for half in range(o):
                    eng.matmul(psum[4 + half][:, :], y[0:kv_rows, e * P:(e + 1) * P],
                               wv[:, half * BANK:(half + 1) * BANK], start=True, stop=True)\
                       .then_inc(sem["v_ps"], 1)

            def front(j):
                project_qk(j)
                eng.wait_ge(sem["qk_ev"], after["qk_ev"](j, 2 * u))
                project_v(j, 0)
                eng.wait_ge(sem["v_ev"], after["v_ev"](j, o))
                project_v(j, 1)

            def scores(i, e, g):
                if e == 0 and g == 0:
                    eng.wait_ge(sem["s_read"], after["s_read"](i, 0))
                    eng.wait_ge(sem["t_ev"], after["t_ev"](i, 0))
                if e == 0 and g == 3:
                    eng.wait_ge(sem["tail_read"], after["tail_read"](i, 0))
                if e == 1:
                    eng.wait_ge(sem["s_read"], after["s_read"](i, g + 1))
                n = g * p["qc"] // 4 // cpu
                eng.wait_ge(sem["qk_ev"], after["qk_ev"](i, 2 * n + 2))
                eng.wait_ge(sem["kb_ready"], after["kb_ready"](i, e * u + n + 1))
                if p["mask"]:
                    eng.matmul(psum[g][:, :], const_bf("ident"), bcast(const_bf(p["mask"]), 1, 4),
                               start=True, stop=False)
                together = min(per_chunk, 4)
                for c in range(4 // together):
                    h = 4 * g + c * together
                    first = h % per_chunk
                    ins = eng.matmul(psum[g][:, c * together * P:(c + 1) * together * P],
                                     b.q[:, h // per_chunk, e, :],
                                     b.kb[:, e, h // per_chunk, first:first + together, :],
                                     start=not p["mask"], stop=True)
                ins.then_inc(sem["s_ps"], 1)

            def transposes(i, e, g, more):
                n = 4 * e + g
                eng.wait_ge(sem["p_norm"], after["p_norm"](i, 2 * e + g // 2 + 1))
                if T_BANKS[n] < 2:
                    eng.wait_ge(sem["s_read"], after["s_read"](i, 8))
                if e == 1:
                    eng.wait_ge(sem["t_ev"], after["t_ev"](i, 4))
                    if more and T_BANKS[n] >= 4:
                        eng.wait_ge(sem["v_ev"], after["v_ev"](i + 1, o))
                for h in range(4):
                    ins = eng.transpose(psum[T_BANKS[n]][:, h * P:(h + 1) * P],
                                        b.probs[:, e, 4 * g + h, :], ident)
                ins.then_inc(sem["t_ps"], 1)

            def values(i, e, g):
                eng.wait_ge(sem["t_ev"], after["t_ev"](i, 4 * e + g + 1))
                n = e * o + g * o // 4
                if n >= 2 and g % (4 // o) == 0:
                    eng.wait_ge(sem["o_ev"], after["o_ev"](i, n - 1))
                for h in range(4 * g, 4 * g + 4):
                    row, chunk = h * hv % P, h * hv // P
                    ins = eng.matmul(psum[6 + n % 2][row:row + hv, chunk % 4 * P:(chunk % 4 + 1) * P],
                                     b.v[:, e, h * hv:(h + 1) * hv], b.probs_t[:, h, :],
                                     start=True, stop=True)
                if g % (4 // o) == 4 // o - 1:
                    ins.then_inc(sem["pv_ps"], 1)

            def output(i, e):
                eng.wait_ge(sem["o_ev"], after["o_ev"](i, (e + 1) * o))
                eng.wait_ge(sem["s_read"], after["s_read"](i, 8))
                for c in range(p["vc"]):
                    ins = eng.matmul(psum[3][:, e * P:(e + 1) * P], b.o_t[:, e, c, :],
                                     wo[:, c * P:(c + 1) * P], start=(c == 0),
                                     stop=(c == p["vc"] - 1))
                if e:
                    ins.then_inc(sem["o_ps"], 1)

            def body(i, more):
                for e in range(2):
                    for g in range(4):
                        scores(i, e, g)
                if more:
                    project_qk(i + 1)
                    eng.wait_ge(sem["qk_ev"], after["qk_ev"](i + 1, 2 * u))
                else:
                    eng.wait_ge(sem["v_ev"], after["v_ev"](i, 2 * o))
                for e in range(2):
                    transposes(i, e, 0, more)
                    transposes(i, e, 1, more)
                    for g in range(4):
                        if g < 2:
                            transposes(i, e, g + 2, more)
                        values(i, e, g)
                    if more:
                        if e:
                            eng.wait_ge(sem["t_ev"], after["t_ev"](i, 8))
                        project_v(i + 1, e)
                    output(i, e)

            run_steps(eng, batch // 2, front, body)

        def act_attention(eng, l):
            p, after, b = parts[l], afters[l], AttentionBuffers(parts[l])
            u, o, cpu = units(p), p["vc"] // 4, min(p["qc"], 2)

            def qk_out(j, n):
                for k, (whole, bias) in enumerate(((b.k, "bk"), (b.q, "bq"))):
                    eng.wait_ge(sem["qk_ps"], after["qk_ps"](j, 2 * n + k + 1))
                    src = psum[QK_BANKS[(2 * n + k) % 4]][:, 0:cpu * 2 * P]
                    src = src.rearrange("p (c e t) -> p c e t", c=cpu, e=2)
                    if k == 0:
                        eng.wait_ge(sem["kb_ready"], after["kb_ready"](j, 0))
                    if p["qkv_bias"]:
                        for c in range(cpu):
                            ch = cpu * n + c
                            ins = eng.activation(whole[:, ch, :, :], src[:, c, :, :], ACT.Identity,
                                                 bias=weight(l, bias)[:, ch:ch + 1])
                    else:
                        ins = eng.activation(whole[:, cpu * n:cpu * n + cpu, :, :], src, ACT.Copy)
                    ins.then_inc(sem["qk_ev"], 1)

            def v_out(j, e):
                for half in range(o):
                    eng.wait_ge(sem["v_ps"], after["v_ps"](j, e * o + half + 1))
                    eng.activation(b.v[:, e, half * BANK:(half + 1) * BANK], psum[4 + half][:, :],
                                   ACT.Copy).then_inc(sem["v_ev"], 1)

            def front(j):
                act_front_out(eng, l, j, 7)
                for n in range(u):
                    qk_out(j, n)
                v_out(j, 0)
                v_out(j, 1)

            def outputs(i, e):
                for half in range(o):
                    n = e * o + half
                    eng.wait_ge(sem["pv_ps"], after["pv_ps"](i, n + 1))
                    dst = b.o_t[:, e, 4 * half:4 * half + 4, :]
                    src = psum[6 + n % 2][:, :].rearrange("p (c t) -> p c t", c=4)
                    if p["qkv_bias"]:
                        for c in range(4):
                            ins = eng.activation(dst[:, c, :], src[:, c, :], ACT.Identity,
                                                 bias=weight(l, "bv")[:, c:c + 1])
                    else:
                        ins = eng.activation(dst, src, ACT.Copy)
                    ins.then_inc(sem["o_ev"], 1)

            def exps(i, e, g):
                dst = b.probs[:, e, 4 * g:4 * g + 4, :]
                if p["taylor"]:
                    eng.wait_ge(sem["s_ps"], after["s_ps"](i, 4 * e + g + 1))
                    eng.activation(dst, psum[g][:, :].rearrange("p (h t) -> p h t", h=4), ACT.Square,
                                   bias=1.0, scale=0.25).then_inc(sem["s_read"], 1)
                else:
                    eng.wait_ge(sem["s_read"], after["s_read"](i, 4 * e + g + 1))
                    eng.activation(dst, dst, ACT.Exp, scale=p["scale"]).then_inc(sem["p_exp"], 1)

            def body(i, more):
                for g in range(4):
                    exps(i, 0, g)
                exps(i, 1, 0)
                if more:
                    act_front_out(eng, l, i + 1, 7)
                exps(i, 1, 1)
                if more:
                    for n in range((u + 1) // 2):
                        qk_out(i + 1, n)
                exps(i, 1, 2)
                if more:
                    for n in range((u + 1) // 2, u):
                        qk_out(i + 1, n)
                exps(i, 1, 3)
                for e in range(2):
                    for g in range(4):
                        n = 4 * e + g
                        eng.wait_ge(sem["t_ps"], after["t_ps"](i, n + 1))
                        eng.activation(b.probs_t[:, 4 * g:4 * g + 4, :],
                                       psum[T_BANKS[n]][:, :].rearrange("p (h t) -> p h t", h=4),
                                       ACT.Copy).then_inc(sem["t_ev"], 1)
                    outputs(i, e)
                    if more:
                        v_out(i + 1, e)

            run_steps(eng, batch // 2, front, body)

        def dve_attention(eng, l):
            p, after, b = parts[l], afters[l], AttentionBuffers(parts[l])

            def front(j):
                dve_front_stats(eng, l, j)
                dve_front_norm(eng, l, j)

            def shift(i, e, g):
                n = 4 * e + g
                eng.wait_ge(sem["s_ps"], after["s_ps"](i, n + 1))
                src = psum[g][:, :].rearrange("p (h t) -> p h t", h=4)
                m = b.max[:, e, 4 * g:4 * g + 4]
                eng.tensor_reduce(m, src, AX_X, ALU.max).then_inc(sem["s_max"], 1)
                eng.wait_ge(sem["s_max"], after["s_max"](i, n + 1))
                eng.tensor_tensor(b.probs[:, e, 4 * g:4 * g + 4, :], src, bcast(m, 2, P), ALU.subtract)\
                   .then_inc(sem["s_read"], 1)

            def taylor_mask(i, e, g):
                n = 4 * e + g
                eng.wait_ge(sem["s_read"], after["s_read"](i, n + 1))
                dst = b.probs[:, e, 4 * g:4 * g + 4, :]
                eng.scalar_tensor_tensor(out=dst, in0=dst, scalar=1.0, in1=bcast(const("lower"), 1, 4),
                                         op0=ALU.add, op1=ALU.mult).then_inc(sem["s_mask"], 1)

            first_pass = taylor_mask if p["taylor"] else shift

            def sums(i, e, half):
                n = 2 * e + half
                hs = slice(8 * half, 8 * half + 8)
                if p["taylor"]:
                    eng.wait_ge(sem["s_mask"], after["s_mask"](i, 4 * e + 2 * half + 2))
                else:
                    eng.wait_ge(sem["p_exp"], after["p_exp"](i, 4 * e + 2 * half + 2))
                eng.tensor_reduce(b.sum[:, e, hs], b.probs[:, e, hs, :], AX_X, ALU.add)\
                   .then_inc(sem["p_sum"], 1)
                eng.wait_ge(sem["p_sum"], after["p_sum"](i, n + 1))
                if p["taylor"]:
                    eng.tensor_scalar(b.max[:, e, hs], b.sum[:, e, hs], 2e-12, None, ALU.add)\
                       .then_inc(sem["p_eps"], 1)
                    eng.wait_ge(sem["p_eps"], after["p_eps"](i, n + 1))
                    eng.reciprocal(b.rec[:, e, hs], b.max[:, e, hs]).then_inc(sem["p_rec"], 1)
                else:
                    eng.reciprocal(b.rec[:, e, hs], b.sum[:, e, hs]).then_inc(sem["p_rec"], 1)

            twice = p["name"] == "L0_attn"

            def tail_add(i):
                eng.wait_ge(sem["o_ps"], after["o_ps"](i, 1))
                dve_tail_add(eng, l, i, psum[3][:, 0:2 * P].rearrange("p (e c) -> p e c", e=2))

            def tail(i):
                tail_add(i)
                dve_tail_stats(eng, l, i)
                dve_tail_norm(eng, l, i)
                if twice:
                    dve_tail_stats(eng, l, i, 1)
                    dve_tail_norm(eng, l, i, 1)

            def body(i, before, more):
                first_pass(i, 0, 0)
                if before:
                    tail_add(i - 1)
                if more:
                    dve_front_stats(eng, l, i + 1)
                first_pass(i, 0, 1)
                if more:
                    dve_front_norm(eng, l, i + 1)
                if before:
                    dve_tail_stats(eng, l, i - 1)
                first_pass(i, 0, 2)
                first_pass(i, 0, 3)
                if before:
                    dve_tail_norm(eng, l, i - 1)
                first_pass(i, 1, 0)
                if before and twice:
                    dve_tail_stats(eng, l, i - 1, 1)
                sums(i, 0, 0)
                first_pass(i, 1, 1)
                sums(i, 0, 1)
                if before and twice:
                    dve_tail_norm(eng, l, i - 1, 1)
                first_pass(i, 1, 2)
                sums(i, 1, 0)
                first_pass(i, 1, 3)
                sums(i, 1, 1)

            run_tailed(eng, batch // 2, front, body, tail)

        def pool_attention(eng, l):
            p, after, b = parts[l], afters[l], AttentionBuffers(parts[l])
            u, r, cpu = units(p), HEADS // p["qc"], min(p["qc"], 2)
            rows = const(f"heads{r}")

            def spread_k(j):
                for e in range(2):
                    for n in range(u):
                        eng.wait_ge(sem["qk_ev"], after["qk_ev"](j, 2 * n + 1))
                        for c in range(cpu * n, cpu * n + cpu):
                            ins = eng.tensor_tensor(b.kb[:, e, c, :, :], bcast(b.k[:, c, e, :], 1, r),
                                                    bcast(rows, 2, P), ALU.mult)
                        ins.then_inc(sem["kb_ready"], 1)

            def front(j):
                pool_front_rstd(eng, l, j)
                spread_k(j)

            def normalise(i, e, half):
                n = 2 * e + half
                hs = slice(8 * half, 8 * half + 8)
                probs = b.probs[:, e, hs, :]
                eng.wait_ge(sem["p_rec"], after["p_rec"](i, n + 1))
                done = sem["p_mul"] if p["post_mask"] else sem["p_norm"]
                eng.tensor_tensor(probs, probs, bcast(b.rec[:, e, hs], 2, P), ALU.mult)\
                   .then_inc(done, 1)
                if p["post_mask"]:
                    eng.wait_ge(sem["p_mul"], after["p_mul"](i, n + 1))
                    pool_gate(eng)
                    eng.affine_select(out=probs, in_=probs, compare_op=ALU.is_gt, fill=0.0, base=0,
                                      pattern=[[0, 8], [1, P]], channel_multiplier=-1)\
                       .then_inc(sem["p_norm"], 1)

            def body(i, before, more):
                if more:
                    pool_front_rstd(eng, l, i + 1)
                if before:
                    pool_whole_tail(eng, l, i - 1)
                for e in range(2):
                    for half in range(2):
                        normalise(i, e, half)
                if more:
                    spread_k(i + 1)

            def tail(i):
                pool_whole_tail(eng, l, i)

            run_tailed(eng, batch // 2, front, body, tail)


        class ExpertBuffers:
            def __init__(self):
                at = [0]

                def cut(n):
                    at[0] += n
                    return arena[:, at[0] - n:at[0]]

                self.gate = cut(2 * BANK).rearrange("p (b n) -> p b n", b=2)
                self.h = cut(2 * 4 * BANK).rearrange("p (b c n) -> p b c n", b=2, c=4)
                self.acc = cut(4 * P).rearrange("p (t c) -> p t c", t=4)
                self.logits = cut(4 * 9).rearrange("p (t e) -> p t e", t=4)
                self.shifted = cut(4 * 9).rearrange("p (t e) -> p t e", t=4)
                self.exps = cut(4 * 9).rearrange("p (t e) -> p t e", t=4)
                self.top = cut(4 * 8).rearrange("p (t e) -> p t e", t=4)
                self.top_at = cut(4 * 8).rearrange("p (t e) -> p t e", t=4).bitcast(U32)
                self.index = cut(4 * 2).rearrange("p (t e) -> p t e", t=4)
                self.hot = cut(2 * 4 * 8).rearrange("p (k t e) -> p k t e", k=2, t=4)
                self.chosen = cut(4 * 8).rearrange("p (t e) -> p t e", t=4)
                self.picked = cut(4 * 8).rearrange("p (t e) -> p t e", t=4)
                self.den = cut(4 * 2).rearrange("p (t e) -> p t e", t=4)
                self.rden = cut(4 * 2).rearrange("p (t e) -> p t e", t=4)
                self.w = cut(4 * 9).rearrange("p (t e) -> p t e", t=4)

        def expert_chunks(p):
            out_, n, at = [], 0, 0
            for e, sizes_ in enumerate(p["chunks"]):
                for c, size in enumerate(sizes_):
                    out_.append((e, c, n, size, at))
                    n += 1
                    at += size * (2 if p["gated"] else 1)
            return out_

        def pe_experts(eng, l):
            p, after, b = parts[l], afters[l], ExpertBuffers()
            chunks, ne = expert_chunks(p), len(p["chunks"])
            up_w, down_w = weight(l, "up"), weight(l, "down")

            def front(j):
                pe_transpose_front(eng, l, j, 4)

            def wait_hidden(i, n):
                if p["gated"]:
                    eng.wait_ge(sem["h_ready"], after["h_ready"](i, n))
                else:
                    eng.wait_ge(sem["act_ev"], after["act_ev"](i, n))

            def up(i, e):
                for ex, _, n, size, at in chunks:
                    if ex != e:
                        continue
                    if p["gated"]:
                        wait_hidden(i, max(n - 1, 0))
                        for k in range(2):
                            ins = eng.matmul(psum[2 * (n % 2) + k][0:size, :],
                                             up_w[:, at + k * size:at + (k + 1) * size], z_t[:, :],
                                             start=True, stop=True)
                    else:
                        wait_hidden(i, max(n - 3, 0))
                        ins = eng.matmul(psum[n % 4][0:size, :], up_w[:, at:at + size], z_t[:, :],
                                         start=True, stop=True)
                    ins.then_inc(sem["up_ps"], 1)

            def down(i, e):
                mine = [c for c in chunks if c[0] == e]
                if p["routing"]:
                    eng.wait_ge(sem["acc"], after["acc"](i, max(e - 1, 0)))
                else:
                    eng.wait_ge(sem["tail_read"], after["tail_read"](i, 0))
                wait_hidden(i, mine[-1][2] + 1)
                for t in range(4):
                    for _, c, n, size, _ in mine:
                        ins = eng.matmul(psum[6 + e % 2][:, t * P:(t + 1) * P],
                                         b.h[0:size, e % 2, c, t * P:(t + 1) * P],
                                         down_w[0:size, n * P:(n + 1) * P], start=(c == 0),
                                         stop=(c == len(mine) - 1))
                ins.then_inc(sem["y_ps"], 1)

            def body(i, more):
                eng.wait_ge(sem["zt_ready"], after["zt_ready"](i, 1))
                if p["routing"]:
                    eng.wait_ge(sem["route"], after["route"](i, 0))
                    ng = 8 + p["shared"]
                    for t in range(4):
                        ins = eng.matmul(psum[5][:, t * ng:(t + 1) * ng], z_t[:, t * P:(t + 1) * P],
                                         weight(l, "gate"), start=True, stop=True)
                    ins.then_inc(sem["gate_ps"], 1)
                for e in range(ne):
                    up(i, e)
                    if e:
                        down(i, e - 1)
                if more:
                    front(i + 1)
                down(i, ne - 1)

            run_steps(eng, batch // 4, front, body)

        def act_experts(eng, l):
            p, after, b = parts[l], afters[l], ExpertBuffers()
            chunks, ne = expert_chunks(p), len(p["chunks"])

            def front(j):
                act_front_out(eng, l, j, 4)

            def hidden(i, e):
                for ex, c, n, size, _ in chunks:
                    if ex != e:
                        continue
                    eng.wait_ge(sem["up_ps"], after["up_ps"](i, n + 1))
                    if p["gated"]:
                        dst, src = b.gate[0:size, n % 2, :], psum[2 * (n % 2)][0:size, :]
                    else:
                        dst, src = b.h[0:size, e % 2, c, :], psum[n % 4][0:size, :]
                    if p["hidden_bias"]:
                        ins = eng.activation(dst, src, p["func"], bias=weight(l, "bh")[:, n:n + 1])
                    else:
                        ins = eng.activation(dst, src, p["func"])
                    ins.then_inc(sem["act_ev"], 1)

            def body(i, more):
                for e in range(ne):
                    hidden(i, e)
                    if e == 1 and p["routing"]:
                        eng.wait_ge(sem["route"], after["route"](i, 4))
                        ins = eng.activation(b.exps[:, :, 0:8], b.shifted[:, :, 0:8], ACT.Exp)
                        if p["shared"]:
                            ins = eng.activation(b.exps[:, :, 8:9], b.logits[:, :, 8:9], ACT.Exp,
                                                 scale=-1.0)
                        ins.then_inc(sem["route_exp"], 1)
                if more:
                    front(i + 1)

            run_steps(eng, batch // 4, front, body)

        def dve_experts(eng, l):
            p, after, b = parts[l], afters[l], ExpertBuffers()
            chunks, ne = expert_chunks(p), len(p["chunks"])
            ng = 8 + p["shared"]

            def front(j):
                dve_front_stats(eng, l, j)
                dve_front_norm(eng, l, j)

            def route_before(i):
                eng.wait_ge(sem["gate_ps"], after["gate_ps"](i, 1))
                eng.tensor_copy(b.logits[:, :, 0:ng], psum[5][:, 0:4 * ng].rearrange("p (t e) -> p t e", t=4))\
                   .then_inc(sem["route"], 1)
                eng.wait_ge(sem["route"], after["route"](i, 1))
                dve_gate(eng)
                for t in range(4):
                    ins = eng.max(b.top[:, t, :], b.logits[:, t, 0:8])
                ins.then_inc(sem["route"], 1)
                eng.wait_ge(sem["route"], after["route"](i, 2))
                dve_gate(eng)
                for t in range(4):
                    ins = eng.max_index(b.top_at[:, t, :], b.top[:, t, :], b.logits[:, t, 0:8])
                ins.then_inc(sem["route"], 1)
                eng.tensor_tensor(b.shifted[:, :, 0:8], b.logits[:, :, 0:8],
                                  b.top[:, :, 0:1].to_broadcast([P, 4, 8]), ALU.subtract)\
                   .then_inc(sem["route"], 1)
                eng.wait_ge(sem["route"], after["route"](i, 3))
                eng.tensor_copy(b.index[:, :, :], b.top_at[:, :, 0:2]).then_inc(sem["route"], 1)
                eng.wait_ge(sem["route"], after["route"](i, 5))
                for k in range(2):
                    ins = eng.tensor_tensor(b.hot[:, k, :, :], bcast(const("iota"), 1, 4),
                                            b.index[:, :, k:k + 1].to_broadcast([P, 4, 8]),
                                            ALU.is_equal)
                ins.then_inc(sem["route"], 1)
                eng.wait_ge(sem["route"], after["route"](i, 6))
                eng.tensor_tensor(b.chosen[:, :, :], b.hot[:, 0, :, :], b.hot[:, 1, :, :], ALU.add)\
                   .then_inc(sem["route"], 1)

            def route_after(i):
                k = 7
                eng.wait_ge(sem["route_exp"], after["route_exp"](i, 1))
                eng.wait_ge(sem["route"], after["route"](i, k))
                eng.tensor_tensor(b.picked[:, :, :], b.exps[:, :, 0:8], b.chosen[:, :, :], ALU.mult)\
                   .then_inc(sem["route"], 1)
                k += 1
                eng.wait_ge(sem["route"], after["route"](i, k))
                over = b.picked if p["routing"] == "top" else b.exps
                eng.tensor_reduce(b.den[:, :, 0], over[:, :, 0:8], AX_X, ALU.add).then_inc(sem["route"], 1)
                k += 1
                eng.wait_ge(sem["route"], after["route"](i, k))
                if p["shared"]:
                    eng.tensor_scalar(b.den[:, :, 1], b.exps[:, :, 8], 1.0, None, ALU.add)\
                       .then_inc(sem["route"], 1)
                    k += 1
                    eng.wait_ge(sem["route"], after["route"](i, k))
                nd = 1 + p["shared"]
                eng.reciprocal(b.rden[:, :, 0:nd], b.den[:, :, 0:nd]).then_inc(sem["route"], 1)
                k += 1
                eng.wait_ge(sem["route"], after["route"](i, k))
                eng.tensor_tensor(b.w[:, :, 0:8], b.picked[:, :, :],
                                  b.rden[:, :, 0:1].to_broadcast([P, 4, 8]), ALU.mult).then_inc(sem["route"], 1)
                k += 1
                if p["shared"]:
                    eng.tensor_copy(b.w[:, :, 8], b.rden[:, :, 1]).then_inc(sem["route"], 1)
                    k += 1
                eng.wait_ge(sem["route"], after["route"](i, k))
                dve_gate(eng)
                assert k == after["route"].n

            def hidden(i, e):
                for ex, c, n, size, _ in chunks:
                    if ex == e:
                        eng.wait_ge(sem["act_ev"], after["act_ev"](i, n + 1))
                        eng.tensor_tensor(b.h[0:size, e % 2, c, :], b.gate[0:size, n % 2, :],
                                          psum[2 * (n % 2) + 1][0:size, :], ALU.mult)\
                           .then_inc(sem["h_ready"], 1)

            def accumulate(i, e):
                eng.wait_ge(sem["y_ps"], after["y_ps"](i, e + 1))
                if e:
                    eng.wait_ge(sem["acc"], after["acc"](i, e))
                for t in range(4):
                    y, w = psum[6 + e % 2][:, t * P:(t + 1) * P], b.w[:, t, e:e + 1]
                    if e == 0:
                        ins = eng.tensor_scalar(b.acc[:, t, :], y, w, None, ALU.mult)
                    else:
                        ins = eng.scalar_tensor_tensor(out=b.acc[:, t, :], in0=y, scalar=w,
                                                       in1=b.acc[:, t, :], op0=ALU.mult, op1=ALU.add)
                ins.then_inc(sem["acc"], 1)

            def tail_add(i):
                if p["routing"]:
                    eng.wait_ge(sem["acc"], after["acc"](i, ne))
                    dve_tail_add(eng, l, i, b.acc[:, :, :])
                else:
                    eng.wait_ge(sem["y_ps"], after["y_ps"](i, 1))
                    dve_tail_add(eng, l, i, psum[6][:, :].rearrange("p (t c) -> p t c", t=4))

            def tail(i):
                tail_add(i)
                dve_tail_stats(eng, l, i)
                dve_tail_norm(eng, l, i)

            def mlp_body(i, before, more):
                if before:
                    tail_add(i - 1)
                if more:
                    dve_front_stats(eng, l, i + 1)
                if before:
                    dve_tail_stats(eng, l, i - 1)
                if more:
                    dve_front_norm(eng, l, i + 1)
                if before:
                    dve_tail_norm(eng, l, i - 1)

            def routed_body(i, before, more):
                route_before(i)
                for e in range(ne):
                    if p["gated"]:
                        hidden(i, e)
                    if e == 1 and before:
                        tail_add(i - 1)
                        dve_tail_stats(eng, l, i - 1)
                    if e == 2:
                        route_after(i)
                        accumulate(i, 0)
                        if before:
                            dve_tail_norm(eng, l, i - 1)
                    if e >= 2:
                        accumulate(i, e - 1)
                    if more and e == 3:
                        dve_front_stats(eng, l, i + 1)
                    if more and e == 4:
                        dve_front_norm(eng, l, i + 1)
                accumulate(i, ne - 1)

            run_tailed(eng, batch // 4, front, routed_body if p["routing"] else mlp_body, tail)

        def pool_norms(eng, l):
            def front(j):
                pool_front_rstd(eng, l, j)

            def tail(i):
                pool_tail_rstd(eng, l, i)

            def body(i, before, more):
                if more and not parts[l].get("routing"):
                    front(i + 1)
                if before:
                    tail(i - 1)
                if more and parts[l].get("routing"):
                    front(i + 1)

            run_tailed(eng, batch // 4, front, body, tail)


        class SingleBuffers:
            def __init__(self):
                self.q, self.k, self.v, self.probs, self.probs_t = (
                    arena[:, n * BANK:(n + 1) * BANK].rearrange("p (e t) -> p e t", e=4)
                    for n in range(5))
                self.max, self.sum, self.rec = (
                    arena[:, 5 * BANK + 4 * n:5 * BANK + 4 * n + 4] for n in range(3))

        def quads(bank):
            return psum[bank][:, :].rearrange("p (e t) -> p e t", e=4)

        def pe_single(eng, l):
            after, b = afters[l], SingleBuffers()

            def project_qk(j):
                pe_transpose_front(eng, l, j, 4)
                eng.wait_ge(sem["zt_ready"], after["zt_ready"](j, 1))
                eng.wait_ge(sem["q_ev"], after["q_ev"](j, 0))
                eng.matmul(psum[0][:, :], weight(l, "wq"), z_t[:, :], start=True, stop=True)\
                   .then_inc(sem["q_ps"], 1)
                eng.wait_ge(sem["ctx_in"], after["ctx_in"](j, 16))
                eng.wait_ge(sem["k_ev"], after["k_ev"](j, 0))
                eng.matmul(psum[1][:, :], weight(l, "wk"), y_t[0:CTX, :], start=True, stop=True)\
                   .then_inc(sem["k_ps"], 1)

            def project_v(j):
                eng.wait_ge(sem["v_ev"], after["v_ev"](j, 0))
                for e in range(4):
                    ins = eng.matmul(psum[2][:, e * P:(e + 1) * P], y_t[0:CTX, e * P:(e + 1) * P],
                                     weight(l, "wv"), start=True, stop=True)
                ins.then_inc(sem["v_ps"], 1)

            def front(j):
                project_qk(j)
                project_v(j)

            def body(i, more):
                eng.wait_ge(sem["q_ev"], after["q_ev"](i, 1))
                eng.wait_ge(sem["k_ev"], after["k_ev"](i, 1))
                eng.wait_ge(sem["s_read"], after["s_read"](i, 0))
                for e in range(4):
                    ins = eng.matmul(psum[3][:, e * P:(e + 1) * P], b.q[:, e, :], b.k[:, e, :],
                                     start=True, stop=True)
                ins.then_inc(sem["s_ps"], 1)
                if more:
                    project_qk(i + 1)
                eng.wait_ge(sem["p_norm"], after["p_norm"](i, 1))
                for e in range(4):
                    ins = eng.transpose(psum[5][:, e * P:(e + 1) * P], b.probs[:, e, :], ident)
                ins.then_inc(sem["t_ps"], 1)
                eng.wait_ge(sem["t_ev"], after["t_ev"](i, 1))
                eng.wait_ge(sem["v_ev"], after["v_ev"](i, 1))
                eng.wait_ge(sem["tail_read"], after["tail_read"](i, 0))
                for e in range(4):
                    ins = eng.matmul(psum[6][:, e * P:(e + 1) * P], b.probs_t[:, e, :], b.v[:, e, :],
                                     start=True, stop=True)
                ins.then_inc(sem["pv_ps"], 1)
                if more:
                    project_v(i + 1)

            run_steps(eng, batch // 4, front, body)

        def act_single(eng, l):
            after, b = afters[l], SingleBuffers()

            def front(j):
                act_front_out(eng, l, j, 4)
                eng.wait_ge(sem["q_ps"], after["q_ps"](j, 1))
                eng.activation(b.q, quads(0), ACT.Identity, bias=weight(l, "bq")).then_inc(sem["q_ev"], 1)

            def body(i, more):
                eng.wait_ge(sem["s_read"], after["s_read"](i, 1))
                eng.activation(b.probs, b.probs, ACT.Exp).then_inc(sem["p_exp"], 1)
                if more:
                    front(i + 1)
                eng.wait_ge(sem["t_ps"], after["t_ps"](i, 1))
                eng.activation(b.probs_t, quads(5), ACT.Copy).then_inc(sem["t_ev"], 1)

            run_steps(eng, batch // 4, front, body)

        def dve_single(eng, l):
            after, b = afters[l], SingleBuffers()

            def k_out(j):
                eng.wait_ge(sem["k_ps"], after["k_ps"](j, 1))
                eng.tensor_scalar(b.k, quads(1), weight(l, "bk"), None, ALU.add)\
                   .then_inc(sem["k_ev"], 1)

            def v_out(j):
                eng.wait_ge(sem["v_ps"], after["v_ps"](j, 1))
                eng.tensor_tensor(b.v, quads(2), bcast(weight(l, "bv"), 1, 4), ALU.add)\
                   .then_inc(sem["v_ev"], 1)

            def front(j):
                dve_front_norm(eng, l, j)
                k_out(j)
                v_out(j)

            def tail_add(i):
                eng.wait_ge(sem["pv_ps"], after["pv_ps"](i, 1))
                dve_tail_add(eng, l, i, quads(6))

            def tail(i):
                tail_add(i)
                dve_tail_stats(eng, l, i)
                dve_tail_norm(eng, l, i)

            def body(i, before, more):
                if more:
                    dve_front_norm(eng, l, i + 1)
                eng.wait_ge(sem["s_ps"], after["s_ps"](i, 1))
                eng.tensor_reduce(b.max, quads(3), AX_X, ALU.max).then_inc(sem["s_max"], 1)
                eng.wait_ge(sem["s_max"], after["s_max"](i, 1))
                eng.tensor_tensor(b.probs, quads(3), bcast(b.max, 2, P), ALU.subtract)\
                   .then_inc(sem["s_read"], 1)
                if before:
                    tail_add(i - 1)
                    dve_tail_stats(eng, l, i - 1)
                    v_out(i)
                eng.wait_ge(sem["p_exp"], after["p_exp"](i, 1))
                eng.tensor_reduce(b.sum, b.probs, AX_X, ALU.add).then_inc(sem["p_sum"], 1)
                eng.wait_ge(sem["p_sum"], after["p_sum"](i, 1))
                eng.reciprocal(b.rec, b.sum).then_inc(sem["p_rec"], 1)
                eng.wait_ge(sem["p_rec"], after["p_rec"](i, 1))
                eng.tensor_tensor(b.probs, b.probs, bcast(b.rec, 2, P), ALU.mult)\
                   .then_inc(sem["p_norm"], 1)
                if more:
                    k_out(i + 1)
                if before:
                    dve_tail_norm(eng, l, i - 1)

            run_tailed(eng, batch // 4, front, body, tail)


        class CosineBuffers:
            def __init__(self):
                def cut(n, m):
                    return arena[:, n * BANK:(n + m) * BANK]

                self.kv = cut(0, 2).rearrange("p (e n) -> p e n", e=4)
                self.q, self.q_cos, self.q_sin, self.k_cos, self.k_sin, self.kv_cos, self.kv_sin = (
                    cut(n, 1).rearrange("p (e t) -> p e t", e=4) for n in range(2, 9))

        def pe_cosine(eng, l):
            after, b = afters[l], CosineBuffers()

            def front(j):
                eng.wait_ge(sem["zt_ready"], after["zt_ready"](j, 1))
                eng.wait_ge(sem["kv_ev"], after["kv_ev"](j, 0))
                for pair in range(2):
                    for e in range(2 * pair, 2 * pair + 2):
                        ins = eng.matmul(psum[pair][:, e % 2 * 2 * P:(e % 2 + 1) * 2 * P],
                                         z_t[:, e * P:(e + 1) * P], weight(l, "wkv"), start=True,
                                         stop=True)
                    ins.then_inc(sem["kv_ps"], 1)
                eng.wait_ge(sem["q_ev"], after["q_ev"](j, 0))
                eng.matmul(psum[2][:, :], weight(l, "wq"), z_t[:, :], start=True, stop=True)\
                   .then_inc(sem["q_ps"], 1)

            def first(j):
                pe_transpose_front(eng, l, j, 4)
                front(j)

            def body(i, more):
                eng.wait_ge(sem["kcs"], after["kcs"](i, 1))
                eng.wait_ge(sem["kv_ev"], after["kv_ev"](i, 2))
                eng.wait_ge(sem["kvb_ev"], after["kvb_ev"](i, 0))
                for bank, k in ((3, b.k_cos), (5, b.k_sin)):
                    for e in range(4):
                        ins = eng.matmul(psum[bank][:, e * P:(e + 1) * P], k[:, e, :],
                                         b.kv[:, e, P:2 * P], start=True, stop=True)
                ins.then_inc(sem["kvb_ps"], 1)
                if more:
                    pe_transpose_front(eng, l, i + 1, 4)
                eng.wait_ge(sem["kvb_ev"], after["kvb_ev"](i, 1))
                eng.wait_ge(sem["qcs"], after["qcs"](i, 1))
                eng.wait_ge(sem["tail_read"], after["tail_read"](i, 0))
                for e in range(4):
                    eng.matmul(psum[6][:, e * P:(e + 1) * P], b.q_cos[:, e, :], b.kv_cos[:, e, :],
                               start=True, stop=False)
                    ins = eng.matmul(psum[6][:, e * P:(e + 1) * P], b.q_sin[:, e, :],
                                     b.kv_sin[:, e, :], start=False, stop=True)
                ins.then_inc(sem["o_ps"], 1)
                if more:
                    front(i + 1)

            run_steps(eng, batch // 4, first, body)

        def act_cosine(eng, l):
            after, b = afters[l], CosineBuffers()

            def q_out(j):
                eng.wait_ge(sem["q_ps"], after["q_ps"](j, 1))
                eng.wait_ge(sem["qcs"], after["qcs"](j, 0))
                eng.activation(b.q, quads(2), ACT.Relu, bias=weight(l, "bq")).then_inc(sem["q_ev"], 1)

            def front(j):
                act_front_out(eng, l, j, 4)
                q_out(j)

            def body(i, more):
                if more:
                    front(i + 1)

            run_steps(eng, batch // 4, front, body)

        def dve_cosine(eng, l):
            after, b = afters[l], CosineBuffers()

            def kv_out(j):
                bias = weight(l, "bkv")
                for pair in range(2):
                    eng.wait_ge(sem["kv_ps"], after["kv_ps"](j, pair + 1))
                    eng.tensor_tensor(b.kv[:, 2 * pair:2 * pair + 2, :],
                                      psum[pair][:, :].rearrange("p (e n) -> p e n", e=2),
                                      bcast(bias, 1, 2), ALU.add).then_inc(sem["kv_ev"], 1)
                eng.wait_ge(sem["kv_ev"], after["kv_ev"](j, 2))
                eng.tensor_scalar(b.k_cos, b.kv[:, :, 0:P], 0.0, const("cos_col"), ALU.max, ALU.mult)
                eng.tensor_scalar(b.k_sin, b.kv[:, :, 0:P], 0.0, const("sin_col"), ALU.max, ALU.mult)\
                   .then_inc(sem["kcs"], 1)

            def q_weights(j):
                eng.wait_ge(sem["q_ev"], after["q_ev"](j, 1))
                eng.tensor_tensor(b.q_cos, b.q, bcast(const("cos_row"), 1, 4), ALU.mult)
                eng.tensor_tensor(b.q_sin, b.q, bcast(const("sin_row"), 1, 4), ALU.mult)\
                   .then_inc(sem["qcs"], 1)

            def front(j):
                dve_front_norm(eng, l, j)
                kv_out(j)
                q_weights(j)

            def tail_add(i):
                eng.wait_ge(sem["o_ps"], after["o_ps"](i, 1))
                dve_tail_add(eng, l, i, quads(6))

            def tail(i):
                tail_add(i)
                dve_tail_stats(eng, l, i)
                dve_tail_norm(eng, l, i)

            def body(i, before, more):
                if before:
                    tail_add(i - 1)
                if more:
                    dve_front_norm(eng, l, i + 1)
                eng.wait_ge(sem["kvb_ps"], after["kvb_ps"](i, 1))
                blocks_ = bcast(const("diagonal"), 1, 4)
                eng.tensor_tensor(b.kv_cos, quads(3), blocks_, ALU.mult)
                eng.tensor_tensor(b.kv_sin, quads(5), blocks_, ALU.mult).then_inc(sem["kvb_ev"], 1)
                if before:
                    dve_tail_stats(eng, l, i - 1)
                if more:
                    kv_out(i + 1)
                    q_weights(i + 1)
                if before:
                    dve_tail_norm(eng, l, i - 1)

            run_tailed(eng, batch // 4, front, body, tail)

        @block.tensor
        def _(eng):
            for l, p in enumerate(parts):
                part_start(eng, l)
                {"attention": pe_attention, "experts": pe_experts, "single": pe_single,
                 "cosine": pe_cosine}[p["kind"]](eng, l)

        @block.scalar
        def _(eng):
            for l, p in enumerate(parts):
                part_start(eng, l)
                {"attention": act_attention, "experts": act_experts, "single": act_single,
                 "cosine": act_cosine}[p["kind"]](eng, l)

        @block.vector
        def _(eng):
            eng.wait_ge(consts_in, 32)
            eng.tensor_copy(const_bf_sb[:, :], arena[:, 0:const_bf_cols]).then_inc(consts_cast, 1)
            eng.wait_ge(x_in, 16)
            for l, p in enumerate(parts):
                part_start(eng, l)
                {"attention": dve_attention, "experts": dve_experts, "single": dve_single,
                 "cosine": dve_cosine}[p["kind"]](eng, l)

        @block.gpsimd
        def _(eng):
            for n, signal in sem.items():
                if n != "ctx_in":
                    eng.sem_inc(signal, 1)
            for e, col in eps_col.items():
                eng.memset(col[:, :], e)
            eng.memset(minus_half[:, :], -0.5).then_inc(primed, 1)
            for l, p in enumerate(parts):
                part_start(eng, l)
                (pool_attention if p["kind"] == "attention" else pool_norms)(eng, l)



def const_arrays():
    row, col = np.arange(P)[:, None], np.arange(P)[None, :]
    theta = (np.float32(np.pi / 2) * np.arange(P, dtype=np.float32) / np.float32(P)).astype(np.float32)
    cos, sin = np.cos(theta).astype(np.float32), np.sin(theta).astype(np.float32)
    f = {"ident": row == col, "lower": col <= row, "heads16": row // 8 == np.arange(16),
         "heads8": row // 16 == np.arange(8), "heads4": row // 32 == np.arange(4),
         "heads2": row // 64 == np.arange(2), "diagonal": row // 8 == col // 8,
         "iota": np.broadcast_to(np.arange(8), (P, 8)),
         "cos_row": np.broadcast_to(cos, (P, P)), "sin_row": np.broadcast_to(sin, (P, P)),
         "cos_col": cos[:, None], "sin_col": sin[:, None]}
    causal = np.where(col <= row, 0.0, NEG)
    window = np.where((col <= row) & (col > row - 32), 0.0, NEG)
    g = {"ident": row == col, "causal": causal, "window": window}
    return (np.concatenate([np.asarray(f[n], np.float32) for n, _ in CONSTS], 1),
            np.concatenate([np.asarray(g[n], np.float32) for n, _ in CONSTS_BF], 1))


def weight_arrays(name, a):
    def heads(w, d, to=32):
        w = w.reshape(w.shape[0], HEADS, d)
        return np.pad(w, ((0, 0), (0, 0), (0, to - d))).reshape(w.shape[0], HEADS * to)

    def rows(w):
        return w.reshape(-1, P, w.shape[1]).transpose(1, 0, 2).reshape(P, -1)

    def padded_rows(w, d):
        w = w.reshape(HEADS, d, -1)
        return rows(np.pad(w, ((0, 0), (0, 32 - d), (0, 0))).reshape(HEADS * 32, -1))

    def per_row(v):
        return v.reshape(-1, P).T

    def wide(v):
        return np.broadcast_to(v[None, :], (P, v.size))

    def col(v):
        return v[:, None]

    def projected(w):
        return w.transpose(1, 0, 2).reshape(w.shape[1], -1)

    def moe(gate_up, down, chunks):
        ups, downs = [], []
        for (g, u), d, sizes in zip(gate_up, down, chunks):
            at = 0
            for c in sizes:
                ups += [g[at:at + c].T] + ([u[at:at + c].T] if u is not None else [])
                downs.append(np.pad(d[:, at:at + c].T, ((0, P - c), (0, 0))))
                at += c
        return dict(up=np.concatenate(ups, 1), down=np.concatenate(downs, 1))

    chunks = {p["name"]: p.get("chunks") for p in PARTS}[name]
    if name == "L0_attn":
        q, k, v = np.split(a["L0_attn_W_qkv"], 3, axis=1)
        return dict(wq=q, wk=k, wv=heads(v, 8), wo=padded_rows(a["L0_attn_W_out"], 8),
                    ln_g=wide(a["L0_xattn_ln1_g"]), ln_b=wide(a["L0_xattn_ln1_b"]))
    if name in ("L0_self", "L0_cross"):
        t = "L0_xattn_a1_" if name == "L0_self" else "L0_xattn_a2_"
        w = dict(wq=projected(a[t + "wq"]), wk=projected(a[t + "wk"]), wv=projected(a[t + "wv"]),
                 wo=rows(a[t + "li1_w"]), bo=wide(a[t + "li1_b"]), gx=col(a[t + "lnx_g"]),
                 bx=col(a[t + "lnx_b"]), gy=col(a[t + "lny_g"]), by=col(a[t + "lny_b"]))
        return w
    if name in ("L0_mlp1", "L0_mlp2"):
        t = "L0_xattn_a1_" if name == "L0_mlp1" else "L0_xattn_a2_"
        w = dict(up=a[t + "li2_w"], down=rows(a[t + "li3_w"]), bh=per_row(a[t + "li2_b"]),
                 bo=wide(a[t + "li3_b"]), gx=col(a[t + "ln3_g"]), bx=col(a[t + "ln3_b"]))
        if name == "L0_mlp1":
            w.update(ln_g=wide(a["L0_xattn_ln2_g"]), ln_b=wide(a["L0_xattn_ln2_b"]))
        return w
    if name == "L0_ffn":
        gu, inner = a["L0_ffn_experts_gate_up"], a["L0_ffn_experts_gate_up"].shape[1] // 2
        w = moe([(e[:inner], e[inner:]) for e in gu] + [(a["L0_ffn_shared_gate_w"], a["L0_ffn_shared_up_w"])],
                list(a["L0_ffn_experts_down"]) + [a["L0_ffn_shared_down_w"]], chunks)
        w["gate"] = np.concatenate([a["L0_ffn_gate_w"], a["L0_ffn_shared_expert_gate_w"]], 0).T
        return w
    if name == "L1_attn":
        q, k, v = np.split(a["L1_attn_w_attn"].T, 3, axis=1)
        bq, bk, bv = np.split(a["L1_attn_b_attn"], 3)
        return dict(wq=q, wk=k, wv=heads(v, 8), wo=padded_rows(a["L1_attn_w_proj"].T, 8), bq=col(bq),
                    bk=col(bk), bv=per_row(heads(bv[None, :], 8)[0]), bo=wide(a["L1_attn_b_proj"]))
    if name == "L1_mlp":
        return dict(up=a["L1_attn_w_fc"].T, down=rows(a["L1_attn_w_mlp_proj"].T),
                    bh=per_row(a["L1_attn_b_fc"]), bo=wide(a["L1_attn_b_mlp_proj"]))
    if name == "L1_cross":
        return dict(wq=a["L1_xattn_Wq"], wk=a["L1_xattn_Wk"], wv=a["L1_xattn_Wv"], wo=rows(a["L1_xattn_Wo"]),
                    bo=wide(a["L1_xattn_bo"]))
    if name == "L1_ffn":
        w = moe(list(zip(a["L1_ffn_W1"], a["L1_ffn_W2"])), a["L1_ffn_W3"], chunks)
        return dict(w, gate=a["L1_ffn_gate_w"].T, gx=col(a["L1_ffn_rms_w"]))
    if name == "L2_attn":
        return dict(wq=a["L2_attn_Wq"].T, wk=a["L2_attn_Wk"].T,
                    wv=a["L2_attn_Wv"].T, wo=rows(a["L2_attn_Wo"].T))
    if name in ("L2_cross", "L3_cross"):
        t = name[:2] + "_xattn_"
        return dict(wq=a[t + "Wq"], wk=a[t + "Wk"], wv=a[t + "Wv"], bq=col(a[t + "bq"]),
                    bk=col(a[t + "bk"]), bv=wide(a[t + "bv"]))
    if name == "L2_ffn":
        inner = a["L2_ffn_w1"].shape[1] // 2
        w = moe([(e[:inner], e[inner:]) for e in a["L2_ffn_w1"]], a["L2_ffn_w2"], chunks)
        return dict(w, gate=a["L2_ffn_router_w"].T)
    if name == "L3_attn":
        return dict(wq=a["L3_attn_Wq"].T,
                    wkv=np.concatenate([a["L3_attn_Wk"].T, a["L3_attn_Wv"].T], 1),
                    bq=col(a["L3_attn_bq"]),
                    bkv=wide(np.concatenate([a["L3_attn_bk"], a["L3_attn_bv"]])))
    if name == "L3_ffn":
        w = moe([(e, None) for e in a["L3_ffn_w1"]], a["L3_ffn_w2"], chunks)
        return dict(w, gate=a["L3_ffn_router_w"].T)
    raise ValueError(name)


def weight_block(p, a):
    w = weight_arrays(p["name"], a)
    fields = []
    for name, r, c in p["weights"]:
        assert w[name].shape == (r, c), (p["name"], name, w[name].shape, r, c)
        fields.append(np.pad(w[name], ((0, P - r), (0, 0))))
    return np.ascontiguousarray(np.concatenate(fields, 1))


def kernel(**inputs):
    import concourse.bacc as bacc
    from concourse.bass_utils import run_bass_kernel_spmd

    a = {k: np.asarray(v) for k, v in inputs.items()}
    x, ctx = a["x"], a["ctx_512"]
    batch = x.shape[0]
    consts, consts_bf = const_arrays()
    arrays = {"in_x": np.ascontiguousarray(x), "in_ctx": np.ascontiguousarray(ctx),
              "in_ctx_t": np.ascontiguousarray(ctx.transpose(2, 0, 1).reshape(CTX, -1)),
              "in_consts": consts, "in_consts_bf": consts_bf}
    for p in PARTS:
        arrays[f"in_w_{p['name']}"] = weight_block(p, a)

    nc = bacc.Bacc("TRN2", target_bir_lowering=False, num_devices=1)
    dram = {n: nc.dram_tensor(n, v.shape, mybir.dt.from_np(v.dtype), kind="ExternalInput").ap()
            for n, v in arrays.items()}
    out = nc.dram_tensor("out", x.shape, F32, kind="ExternalOutput").ap()
    build_program(nc, dram["in_x"], dram["in_ctx"], dram["in_ctx_t"], dram["in_consts"],
                  dram["in_consts_bf"], [dram[f"in_w_{p['name']}"] for p in PARTS], out, PARTS, batch)
    return run_bass_kernel_spmd(nc, [arrays], core_ids=[0]).results[0]["out"]
```

```python
import itertools
from contextlib import ExitStack

import numpy as np

import concourse.bass as bass
from concourse import mybir

F32 = mybir.dt.float32
BF16 = mybir.dt.bfloat16
U32 = mybir.dt.uint32
ALU = mybir.AluOpType
ACT = mybir.ActivationFunctionType
AX_X = mybir.AxisListType.X

P = 128
CTX = 64
HEADS = 16
BANK = 512
NEG = -1e30
LN_EPS = 1e-5
GATES = 16



def attention(name, **k):
    p = dict(kind="attention", name=name, group=2, qc=4, vc=4, scale=1.0, norm_eps=None,
             post_mask=False, taylor=False, ctx=None, affine=False, out_bias=False,
             adds=("x",), store="x")
    p.update(k)
    kv_rows = CTX if p["ctx"] else P
    w = [("wq", P, p["qc"] * P), ("wk", kv_rows, p["qc"] * P), ("wv", kv_rows, p["vc"] * P),
         ("wo", P, p["vc"] * P)]
    if p["affine"]:
        w += [("gx", P, 1), ("bx", P, 1), ("gy", kv_rows, 1), ("by", kv_rows, 1)]
    if p["out_bias"]:
        w += [("bo", P, P)]
    p["weights"] = w
    return p


def narrow(name, **k):
    p = dict(kind="narrow", name=name, group=2, scale=8 ** -0.5, norm_eps=None, mask=None,
             ctx=None, affine=False, qkv_bias=False, out_bias=False, adds=("x",), store="x")
    p.update(k)
    w = [("wqkv", P, 3 * P), ("wo", P, P)]
    if p["qkv_bias"]:
        w += [("bqkv", P, 3)]
    if p["out_bias"]:
        w += [("bo", P, P)]
    if name == "L0_attn":
        w += [("ln_g", P, P), ("ln_b", P, P)]
    p["weights"] = w
    return p


def experts(name, chunks, **k):
    p = dict(kind="experts", name=name, group=4, chunks=chunks, func=ACT.Gelu, gated=False,
             norm_eps=None, rms_eps=None, affine=False, hidden_bias=False, out_bias=False,
             routing=None, shared=False, adds=("x",), store="x", ctx=None)
    p.update(k)
    sizes = [c for e in chunks for c in e]
    w = [("up", P, sum(sizes) * (2 if p["gated"] else 1)), ("down", P, len(sizes) * P)]
    if p["routing"]:
        w += [("gate", P, 8 + p["shared"])]
    if p["affine"]:
        w += [("gx", P, 1), ("bx", P, 1)]
    if p["rms_eps"]:
        w += [("gx", P, 1)]
    if p["hidden_bias"]:
        w += [("bh", P, len(sizes))]
    if p["out_bias"]:
        w += [("bo", P, P)]
    if p["store"] == "a":
        w += [("ln_g", P, P), ("ln_b", P, P)]
    p["weights"] = w
    return p


def single(name):
    return dict(kind="single", name=name, group=4, ctx="plain", adds=("x",), store="x",
                norm_eps=None, affine=False, out_bias=False,
                weights=[("wq", P, P), ("wk", CTX, P), ("wv", CTX, P), ("bq", P, 1), ("bk", P, 1),
                         ("bv", P, P)])


def cosine(name):
    return dict(kind="cosine", name=name, group=4, ctx=None, adds=("x",), store="x",
                norm_eps=None, affine=False, out_bias=False,
                weights=[("wq", P, P), ("wkv", P, 2 * P), ("bq", P, 1), ("bkv", P, 2 * P)])


THIRDS = [118, 117, 117]
PARTS = [
    narrow("L0_attn", mask="window"),
    attention("L0_self", scale=32 ** -0.5, norm_eps=LN_EPS, affine=True, post_mask=True,
              out_bias=True, adds=("a",), store="xo"),
    experts("L0_mlp1", [[P] * 4], norm_eps=LN_EPS, affine=True, hidden_bias=True, out_bias=True,
            adds=("a", "xo"), store="a"),
    attention("L0_cross", scale=32 ** -0.5, norm_eps=LN_EPS, affine=True, ctx="normed",
              out_bias=True, adds=("a",), store="xo"),
    experts("L0_mlp2", [[P] * 4], norm_eps=LN_EPS, affine=True, hidden_bias=True, out_bias=True,
            adds=("a", "xo", "x")),
    experts("L0_ffn", [[88, 88]] * 8 + [THIRDS], func=ACT.Silu, gated=True, routing="all",
            shared=True),
    narrow("L1_attn", norm_eps=1e-10, mask="causal", qkv_bias=True, out_bias=True, store="xo"),
    experts("L1_mlp", [[P] * 4], func=ACT.Gelu_apprx_tanh, norm_eps=1e-10, hidden_bias=True,
            out_bias=True, adds=("xo", "x")),
    attention("L1_cross", qc=8, vc=8, scale=64 ** -0.5, ctx="plain", out_bias=True),
    experts("L1_ffn", [THIRDS] * 8, func=ACT.Silu, gated=True, routing="top", rms_eps=1e-6,
            adds=("x", "x")),
    attention("L2_attn", qc=2, vc=8, taylor=True),
    single("L2_cross"),
    experts("L2_ffn", [[P] * 2] * 8, func=ACT.Silu, gated=True, routing="all"),
    cosine("L3_attn"),
    single("L3_cross"),
    experts("L3_ffn", [[P] * 2] * 8, routing="top"),
]
SOURCE = {"L0_self": "a", "L0_mlp1": "xo", "L0_cross": "a", "L0_mlp2": "xo", "L1_mlp": "xo"}

CONSTS = [("ident", P), ("lower", P), ("heads16", 16), ("heads8", 8), ("heads4", 4), ("heads2", 2),
          ("diagonal", P), ("iota", 8),
          ("cos_row", P), ("sin_row", P), ("cos_col", 1), ("sin_col", 1)]
CONSTS_BF = [("ident", P), ("causal", P), ("window", P)]


def columns(fields):
    at, place = 0, {}
    for f in fields:
        place[f[0]] = (at, f[-2] if len(f) == 3 else P, f[-1])
        at += f[-1]
    return place, at



def tail_steps(p):
    n = len(p["adds"]) + p["out_bias"] - 1
    if p["store"] != "xo":
        n += 3
        if p["store"] == "a" or p["name"] == "L0_attn":
            n += 2
        if p["name"] == "L0_attn":
            n += 3
    return n


def units(p):
    return max(p["qc"] // 2, 1)


def signal_counts(p):
    n = dict(z_ready=1, zt_ps=1, zt_ready=1, tail_read=1, tail_step=tail_steps(p), tail_done=1)
    if p["store"] != "xo":
        n.update(tail_var=1, tail_rstd=1)
        if p["name"] == "L0_attn":
            n.update(tail_var=2, tail_rstd=2)
    if p["norm_eps"] or p.get("rms_eps"):
        n.update(front_stats=1, front_aggr=1, front_var=1, front_rstd=1)
        if p.get("rms_eps"):
            n.update(front_sq=2)
    if p["ctx"]:
        n.update(ctx_in=16)
    if p["kind"] == "attention":
        u, o = units(p), p["vc"] // 4
        n.update(qk_ps=2 * u, qk_ev=2 * u, kb_ready=2 * u, s_ps=8, s_read=8, p_exp=8, p_sum=4,
                 p_rec=4, p_norm=4, t_ps=8, t_ev=8, pv_ps=2 * o, o_ev=2 * o, v_ps=2 * o,
                 v_ev=2 * o, o_ps=1)
        if p["taylor"]:
            n.update(s_mask=8, p_eps=4)
            del n["p_exp"]
        else:
            n.update(s_max=8)
        if p["post_mask"]:
            n.update(p_mul=4)
    elif p["kind"] == "narrow":
        n.update(qk_ps=2, qk_ev=2, kb_ready=4, s_ps=8, s_max=8, n_max=8, p_exp=8, p_rec=2, t_ps=8,
                 t_ev=8, pv_ps=2, o_norm=2, ot_ps=2, o_ev=2, v_ps=2, v_ev=2, o_ps=2)
    elif p["kind"] == "experts":
        chunks, ne = sum(map(len, p["chunks"])), len(p["chunks"])
        n.update(up_ps=chunks, act_ev=chunks, y_ps=ne)
        if p["gated"]:
            n.update(h_ready=chunks)
        if p["routing"]:
            n.update(gate_ps=1, route=11 + 2 * p["shared"], route_exp=1, acc=ne)
    elif p["kind"] == "single":
        n.update(q_ps=1, k_ps=1, q_ev=1, k_ev=1, v_ps=1, v_ev=1, s_ps=1, s_max=1, s_read=1,
                 p_exp=1, p_sum=1, p_rec=1, p_norm=1, t_ps=1, t_ev=1, pv_ps=1)
    elif p["kind"] == "cosine":
        n.update(kv_ps=2, kv_ev=2, kcs=1, q_ps=1, q_ev=1, qcs=1, o_ps=1, kvb_ps=1, kvb_ev=1)
    return n


class After:

    def __init__(self, base, per_step):
        self.base, self.n = base, per_step

    def __call__(self, i, k):
        return i * self.n + (self.base + k)


def bcast(ap, axis, count):
    ap = ap.unsqueeze(axis)
    shape = list(ap.shape)
    shape[axis] = count
    return ap.to_broadcast(shape)


def run_tailed(eng, steps, front, body, tail):
    front(0)
    body(0, False, True)
    with eng.Fori(1, steps - 1) as i:
        body(i, True, True)
    body(steps - 1, True, False)
    tail(steps - 1)


def run_steps(eng, steps, front, body):
    front(0)
    with eng.Fori(0, steps - 1) as i:
        body(i, True)
    body(steps - 1, False)



def build_program(nc, x, ctx, ctx_t, consts, consts_bf, weights, out, parts, batch):
    with ExitStack() as stack:
        def sb(name, shape, dt=F32):
            return stack.enter_context(nc.sbuf_tensor(name, shape, dt))

        state = {n: sb(f"{n}_state", [P, batch, P]) for n in ("x", "a", "xo")}
        sizes = [columns(p["weights"])[1] for p in parts]
        blocks = [sb(f"weights{b}", [P, max(sizes[b::2] + [1])]) for b in range(2)]
        const_place, const_cols = columns(CONSTS)
        const_bf_place, const_bf_cols = columns(CONSTS_BF)
        const_sb = sb("consts", [P, const_cols])
        const_bf_sb = sb("consts_bf", [P, const_bf_cols], BF16)

        def const(name):
            at, _, n = const_place[name]
            return const_sb[:, at:at + n]

        def const_bf(name):
            at, _, n = const_bf_place[name]
            return const_bf_sb[:, at:at + n]

        ident = const("ident")
        z = sb("z", [P, 4, P])
        z_ctx = sb("z_ctx", [P, 2, CTX])
        ctx_raw = sb("ctx_raw", [P, 2, CTX])
        z_t = sb("z_t", [P, BANK])
        y_t = sb("y_t", [P, BANK])
        stats = sb("stats", [P, 4, 6])
        meanvar = sb("meanvar", [P, 4, 2])
        var_eps = sb("var_eps", [P, 4])
        rstd = sb("rstd", [P, 4])
        res = sb("res", [P, 4, P])
        t_stats = sb("t_stats", [P, 4, 6])
        t_meanvar = sb("t_meanvar", [P, 4, 2])
        t_var_eps = sb("t_var_eps", [P, 4])
        t_rstd = sb("t_rstd", [P, 4])
        eps_col = {e: sb(f"eps{n}", [P, 1]) for n, e in enumerate((LN_EPS, 1e-10, 1e-6))}
        minus_half = sb("minus_half", [P, 1])
        gate_dve = sb("gate_dve", [P, GATES])
        gate_at = itertools.cycle(range(GATES))
        gate_pool = sb("gate_pool", [P, 2])
        tail_mark = sb("tail_mark", [P, 1])
        ARENA = 18 * 1024 + 256
        arena = sb("arena", [P, ARENA])

        psum = [stack.enter_context(nc.psum_tensor(f"bank{b}", [P, BANK], F32)) for b in range(8)]

        counts = [signal_counts(p) for p in parts]
        names = sorted({n for c in counts for n in c})
        sem = {n: stack.enter_context(nc.semaphore(n)) for n in names}
        weights_in = [stack.enter_context(nc.semaphore(f"weights_in{b}")) for b in range(2)]
        x_in = stack.enter_context(nc.semaphore("x_in"))
        consts_in = stack.enter_context(nc.semaphore("consts_in"))
        consts_cast = stack.enter_context(nc.semaphore("consts_cast"))
        out_done = stack.enter_context(nc.semaphore("out_done"))
        primed = stack.enter_context(nc.semaphore("primed"))
        bases = {n: int(n != "ctx_in") for n in names}
        afters = []
        for p, c in zip(parts, counts):
            afters.append({n: After(bases[n], k) for n, k in c.items()})
            for n, k in c.items():
                bases[n] += k * (batch // p["group"])

        def weight(l, name):
            at, rows, n = columns(parts[l]["weights"])[0][name]
            return blocks[l % 2][0:rows, at:at + n]

        def dve_gate(eng):
            at = next(gate_at)
            eng.memset(gate_dve[:, at:at + 1], 0.0)

        def pool_gate(eng):
            eng.tensor_tensor(gate_pool[:, 0:1], minus_half[:, :], minus_half[:, :], ALU.add)

        def all_tails(l):
            return afters[l]["tail_done"](batch // parts[l]["group"], 0)

        def part_start(eng, l):
            if l:
                eng.wait_ge(sem["tail_done"], all_tails(l - 1))
            else:
                eng.wait_ge(primed, 1)
                eng.wait_ge(consts_in, 32)
                eng.wait_ge(consts_cast, 1)
            eng.wait_ge(weights_in[l % 2], 16 * (l // 2 + 1))

        def group_of(l, i):
            g = parts[l]["group"]
            return bass.ds(i * g, g)

        block = stack.enter_context(nc.Block())

        @block.sync
        def _(eng):
            def load_weights(l):
                at = columns(parts[l]["weights"])[1]
                eng.dma_start(blocks[l % 2][:, 0:at], weights[l]).then_inc(weights_in[l % 2], 16)

            eng.dma_start(const_sb[:, :], consts).then_inc(consts_in, 16)
            eng.dma_start(arena[:, 0:const_bf_cols], consts_bf).then_inc(consts_in, 16)
            load_weights(0)
            eng.dma_start(state["x"][:, :, :], x.rearrange("b s c -> s b c")).then_inc(x_in, 16)
            for l, p in enumerate(parts):
                after, steps, g = afters[l], batch // p["group"], p["group"]
                if l:
                    eng.wait_ge(sem["tail_done"], all_tails(l - 1))
                if l + 1 < len(parts):
                    load_weights(l + 1)
                if p["ctx"]:
                    def load_ctx(j, first=False, p=p, after=after, g=g):
                        if not first:
                            if p["ctx"] == "normed":
                                eng.wait_ge(sem["z_ready"], after["z_ready"](j, 0))
                            else:
                                eng.wait_ge(sem["v_ps"], after["v_ps"](j, 0))
                        if p["ctx"] == "normed":
                            src = ctx[bass.ds(j * g, g), :, :].rearrange("b s c -> s b c")
                            eng.dma_start(ctx_raw[:, :, :], src).then_inc(sem["ctx_in"], 16)
                        else:
                            eng.dma_start(y_t[0:CTX, 0:g * P], ctx_t[:, bass.ds(j * (g * P), g * P)])\
                               .then_inc(sem["ctx_in"], 16)
                    load_ctx(0, True)
                    with eng.Fori(1, steps) as j:
                        load_ctx(j)
            eng.wait_ge(sem["tail_done"], all_tails(len(parts) - 1))
            eng.dma_start(out.rearrange("b s c -> s b c"), state["x"][:, :, :]).then_inc(out_done, 16)
            eng.wait_ge(out_done, 16)


        def dve_front_stats(eng, l, j):
            p, after = parts[l], afters[l]
            if not (p["norm_eps"] or p.get("rms_eps")):
                return
            src = state[SOURCE.get(p["name"], "x")]
            g = p["group"]
            for t in range(g):
                ins = eng.bn_stats(stats[:, t, :], src[:, j * g + t, :])
            if p["ctx"] == "normed":
                eng.wait_ge(sem["ctx_in"], after["ctx_in"](j, 16))
                for t in range(2):
                    ins = eng.bn_stats(stats[:, g + t, :], ctx_raw[:, t, :])
            ins.then_inc(sem["front_stats"], 1)
            n = g + (2 if p["ctx"] == "normed" else 0)
            eng.wait_ge(sem["front_stats"], after["front_stats"](j, 1))
            dve_gate(eng)
            for t in range(n):
                ins = eng.bn_aggr(meanvar[:, t, :], stats[:, t, :])
            ins.then_inc(sem["front_aggr"], 1)
            if p.get("rms_eps"):
                eng.wait_ge(sem["front_aggr"], after["front_aggr"](j, 1))
                eng.tensor_tensor(rstd[:, 0:g], meanvar[:, 0:g, 0], meanvar[:, 0:g, 0], ALU.mult)\
                   .then_inc(sem["front_sq"], 1)
                eng.wait_ge(sem["front_sq"], after["front_sq"](j, 1))
                eng.tensor_tensor(meanvar[:, 0:g, 1], meanvar[:, 0:g, 1], rstd[:, 0:g], ALU.add)\
                   .then_inc(sem["front_sq"], 1)

        def pool_front_rstd(eng, l, j):
            p, after = parts[l], afters[l]
            eps = p["norm_eps"] or p.get("rms_eps")
            if not eps:
                return
            n = p["group"] + (2 if p["ctx"] == "normed" else 0)
            if p.get("rms_eps"):
                eng.wait_ge(sem["front_sq"], after["front_sq"](j, 2))
            else:
                eng.wait_ge(sem["front_aggr"], after["front_aggr"](j, 1))
            eng.tensor_tensor(var_eps[:, 0:n], meanvar[:, 0:n, 1],
                              eps_col[eps][:, :].to_broadcast([P, n]), ALU.add)\
               .then_inc(sem["front_var"], 1)
            eng.wait_ge(sem["front_var"], after["front_var"](j, 1))
            eng.tensor_tensor(rstd[:, 0:n], var_eps[:, 0:n], minus_half[:, :].to_broadcast([P, n]),
                              ALU.pow).then_inc(sem["front_rstd"], 1)

        def dve_front_norm(eng, l, j):
            p, after = parts[l], afters[l]
            src = state[SOURCE.get(p["name"], "x")]
            g = p["group"]
            eng.wait_ge(sem["zt_ps"], after["zt_ps"](j, 0))
            if not (p["norm_eps"] or p.get("rms_eps")):
                dve_gate(eng)
                eng.tensor_copy(z[:, 0:g, :], src[:, group_of(l, j), :]).then_inc(sem["z_ready"], 1)
                return
            eng.wait_ge(sem["front_rstd"], after["front_rstd"](j, 1))
            dve_gate(eng)
            for t in range(g):
                if p.get("rms_eps"):
                    ins = eng.tensor_scalar(z[:, t, :], src[:, j * g + t, :], rstd[:, t:t + 1], None,
                                            ALU.mult)
                else:
                    ins = eng.tensor_scalar(z[:, t, :], src[:, j * g + t, :], meanvar[:, t, 0:1],
                                            rstd[:, t:t + 1], ALU.subtract, ALU.mult)
            if p["ctx"] == "normed":
                for t in range(2):
                    ins = eng.tensor_scalar(z_ctx[:, t, :], ctx_raw[:, t, :], meanvar[:, g + t, 0:1],
                                            rstd[:, g + t:g + t + 1], ALU.subtract, ALU.mult)
            ins.then_inc(sem["z_ready"], 1)

        def pe_transpose_front(eng, l, j, bank):
            p, after = parts[l], afters[l]
            eng.wait_ge(sem["z_ready"], after["z_ready"](j, 1))
            for t in range(p["group"]):
                ins = eng.transpose(psum[bank][:, t * P:(t + 1) * P], z[:, t, :], ident)
            if p["ctx"] == "normed":
                for t in range(2):
                    ins = eng.transpose(psum[bank][0:CTX, (2 + t) * P:(3 + t) * P], z_ctx[:, t, :], ident)
            ins.then_inc(sem["zt_ps"], 1)

        def act_front_out(eng, l, j, bank):
            p, after = parts[l], afters[l]
            n = p["group"] * P
            eng.wait_ge(sem["zt_ps"], after["zt_ps"](j, 1))
            if p.get("rms_eps"):
                eng.activation(z_t[:, 0:n], psum[bank][:, 0:n], ACT.Identity, scale=weight(l, "gx"))\
                   .then_inc(sem["zt_ready"], 1)
            elif not p["affine"]:
                eng.activation(z_t[:, 0:n], psum[bank][:, 0:n], ACT.Copy).then_inc(sem["zt_ready"], 1)
            else:
                ins = eng.activation(z_t[:, 0:n], psum[bank][:, 0:n], ACT.Identity,
                                     bias=weight(l, "bx"), scale=weight(l, "gx"))
                if p["kind"] == "attention":
                    rows, at = (CTX, n) if p["ctx"] else (P, 0)
                    ins = eng.activation(y_t[0:rows, 0:n], psum[bank][0:rows, at:at + n], ACT.Identity,
                                         bias=weight(l, "by"), scale=weight(l, "gy"))
                ins.then_inc(sem["zt_ready"], 1)


        def norm_step(l, r):
            return len(parts[l]["adds"]) + parts[l]["out_bias"] - 1 + 3 * r

        def dve_tail_add(eng, l, i, source):
            p, after = parts[l], afters[l]
            g, steps, now = p["group"], len(p["adds"]) + p["out_bias"], source
            for n in range(steps):
                dst = res[:, 0:g, :] if n < steps - 1 or p["store"] != "xo" else \
                    state["xo"][:, group_of(l, i), :]
                if n < len(p["adds"]):
                    other = state[p["adds"][n]][:, group_of(l, i), :]
                else:
                    other = bcast(weight(l, "bo"), 1, g)
                if n == 1:
                    eng.wait_ge(sem["tail_read"], after["tail_read"](i, 1))
                elif n:
                    eng.wait_ge(sem["tail_step"], after["tail_step"](i, n - 1))
                ins = eng.tensor_tensor(dst, now, other, ALU.add)
                ins.then_inc(sem["tail_step"] if n else sem["tail_read"], 1)
                now = res[:, 0:g, :]
            if p["store"] == "xo":
                if steps > 1:
                    eng.wait_ge(sem["tail_step"], after["tail_step"](i, steps - 1))
                else:
                    eng.wait_ge(sem["tail_read"], after["tail_read"](i, 1))
                eng.memset(tail_mark[:, :], 0.0).then_inc(sem["tail_done"], 1)

        def tail_source(l, i, r, t):
            return state["x"][:, i * parts[l]["group"] + t, :] if r else res[:, t, :]

        def dve_tail_stats(eng, l, i, r=0):
            p, after = parts[l], afters[l]
            if p["store"] == "xo":
                return
            k = norm_step(l, r)
            if k:
                eng.wait_ge(sem["tail_step"], after["tail_step"](i, k))
            else:
                eng.wait_ge(sem["tail_read"], after["tail_read"](i, 1))
            dve_gate(eng)
            for t in range(p["group"]):
                ins = eng.bn_stats(t_stats[:, t, :], tail_source(l, i, r, t))
            ins.then_inc(sem["tail_step"], 1)
            eng.wait_ge(sem["tail_step"], after["tail_step"](i, k + 1))
            dve_gate(eng)
            for t in range(p["group"]):
                ins = eng.bn_aggr(t_meanvar[:, t, :], t_stats[:, t, :])
            ins.then_inc(sem["tail_step"], 1)

        def pool_tail_rstd(eng, l, i, r=0):
            p, after = parts[l], afters[l]
            if p["store"] == "xo":
                return
            g = p["group"]
            eng.wait_ge(sem["tail_step"], after["tail_step"](i, norm_step(l, r) + 2))
            eng.tensor_tensor(t_var_eps[:, 0:g], t_meanvar[:, 0:g, 1],
                              eps_col[LN_EPS][:, :].to_broadcast([P, g]), ALU.add)\
               .then_inc(sem["tail_var"], 1)
            eng.wait_ge(sem["tail_var"], after["tail_var"](i, r + 1))
            eng.tensor_tensor(t_rstd[:, 0:g], t_var_eps[:, 0:g],
                              minus_half[:, :].to_broadcast([P, g]), ALU.pow)\
               .then_inc(sem["tail_rstd"], 1)

        def dve_tail_norm(eng, l, i, r=0):
            p, after = parts[l], afters[l]
            if p["store"] == "xo":
                return
            g, k = p["group"], norm_step(l, r) + 2
            in_place = r or p["store"] == "a"
            eng.wait_ge(sem["tail_rstd"], after["tail_rstd"](i, r + 1))
            dve_gate(eng)
            for t in range(g):
                dst = res[:, t, :] if in_place else state["x"][:, i * g + t, :]
                ins = eng.tensor_scalar(dst, tail_source(l, i, r, t), t_meanvar[:, t, 0:1],
                                        t_rstd[:, t:t + 1], ALU.subtract, ALU.mult)
            ins.then_inc(sem["tail_step"], 1)
            k += 1
            if in_place:
                eng.wait_ge(sem["tail_step"], after["tail_step"](i, k))
                eng.tensor_tensor(res[:, 0:g, :], res[:, 0:g, :], bcast(weight(l, "ln_g"), 1, g),
                                  ALU.mult).then_inc(sem["tail_step"], 1)
                k += 1
                eng.wait_ge(sem["tail_step"], after["tail_step"](i, k))
                eng.tensor_tensor(state["a"][:, group_of(l, i), :], res[:, 0:g, :],
                                  bcast(weight(l, "ln_b"), 1, g), ALU.add)\
                   .then_inc(sem["tail_step"], 1)
                k += 1
            if k == after["tail_step"].n:
                eng.wait_ge(sem["tail_step"], after["tail_step"](i, k))
                eng.memset(tail_mark[:, :], 0.0).then_inc(sem["tail_done"], 1)

        QK_BANKS = (4, 5, 6, 7)
        T_BANKS = (0, 1, 4, 5, 0, 1, 4, 5)

        class AttentionBuffers:
            def __init__(self, p):
                at = [0]

                def cut(n):
                    at[0] += n
                    assert at[0] <= ARENA
                    return arena[:, at[0] - n:at[0]]

                qc, vc = p["qc"], p["vc"]
                self.q = cut(qc * 2 * P).rearrange("p (c e t) -> p c e t", c=qc, e=2)
                self.k = cut(qc * 2 * P).rearrange("p (c e t) -> p c e t", c=qc, e=2)
                self.kb = cut(2 * HEADS * P).rearrange("p (e c r t) -> p e c r t", e=2, c=qc, t=P)
                self.v = cut(2 * vc * P).rearrange("p (e n) -> p e n", e=2)
                self.probs = cut(2 * HEADS * P).rearrange("p (e h t) -> p e h t", e=2, t=P)
                self.probs_t = cut(HEADS * P).rearrange("p (h t) -> p h t", t=P)
                self.o_t = cut(2 * vc * P).rearrange("p (e c t) -> p e c t", e=2, t=P)
                self.max = cut(2 * HEADS).rearrange("p (e h) -> p e h", e=2)
                self.sum = cut(2 * HEADS).rearrange("p (e h) -> p e h", e=2)
                self.rec = cut(2 * HEADS).rearrange("p (e h) -> p e h", e=2)

        def pe_attention(eng, l):
            p, after, b = parts[l], afters[l], AttentionBuffers(parts[l])
            u, o, cpu = units(p), p["vc"] // 4, min(p["qc"], 2)
            per_chunk = HEADS // p["qc"]
            kv_rows = CTX if p["ctx"] else P
            y = y_t if p["ctx"] or p["affine"] else z_t
            hv = P * p["vc"] // HEADS
            early = int(p["qc"] >= 4)
            wq, wk, wv, wo = (weight(l, n) for n in ("wq", "wk", "wv", "wo"))

            def project_qk(j, first, last):
                eng.wait_ge(sem["zt_ready"], after["zt_ready"](j, 1))
                if p["ctx"] == "plain":
                    eng.wait_ge(sem["ctx_in"], after["ctx_in"](j, 16))
                eng.wait_ge(sem["v_ev"], after["v_ev"](j, 0))
                for n in range(first, last):
                    for k, (w, src) in enumerate(((wk, y[0:kv_rows, 0:2 * P]), (wq, z_t[:, 0:2 * P]))):
                        if n >= 2:
                            eng.wait_ge(sem["qk_ev"], after["qk_ev"](j, 2 * n + k - 3))
                        bank = psum[QK_BANKS[(2 * n + k) % 4]]
                        for c in range(cpu):
                            at = (cpu * n + c) * P
                            ins = eng.matmul(bank[:, c * 2 * P:(c + 1) * 2 * P], w[:, at:at + P], src,
                                             start=True, stop=True)
                        ins.then_inc(sem["qk_ps"], 1)

            def project_v(j, e):
                for half in range(o):
                    eng.matmul(psum[4 + half][:, :], y[0:kv_rows, e * P:(e + 1) * P],
                               wv[:, half * BANK:(half + 1) * BANK], start=True, stop=True)\
                       .then_inc(sem["v_ps"], 1)

            def front(j):
                pe_transpose_front(eng, l, j, 7)
                project_qk(j, 0, u)
                eng.wait_ge(sem["qk_ev"], after["qk_ev"](j, 2 * u))
                project_v(j, 0)
                eng.wait_ge(sem["v_ev"], after["v_ev"](j, o))
                project_v(j, 1)

            def scores(i, e, g):
                if e == 0 and g == 0:
                    eng.wait_ge(sem["s_read"], after["s_read"](i, 0))
                    eng.wait_ge(sem["t_ev"], after["t_ev"](i, 0))
                if e == 0 and g == 3:
                    eng.wait_ge(sem["tail_read"], after["tail_read"](i, 0))
                if e == 1:
                    eng.wait_ge(sem["s_read"], after["s_read"](i, g + 1))
                n = g * p["qc"] // 4 // cpu
                eng.wait_ge(sem["qk_ev"], after["qk_ev"](i, 2 * n + 2))
                eng.wait_ge(sem["kb_ready"], after["kb_ready"](i, e * u + n + 1))
                together = min(per_chunk, 4)
                for c in range(4 // together):
                    h = 4 * g + c * together
                    first = h % per_chunk
                    ins = eng.matmul(psum[g][:, c * together * P:(c + 1) * together * P],
                                     b.q[:, h // per_chunk, e, :],
                                     b.kb[:, e, h // per_chunk, first:first + together, :],
                                     start=True, stop=True)
                ins.then_inc(sem["s_ps"], 1)

            def transposes(i, e, g, more):
                n = 4 * e + g
                eng.wait_ge(sem["p_norm"], after["p_norm"](i, 2 * e + g // 2 + 1))
                if T_BANKS[n] < 2:
                    eng.wait_ge(sem["s_read"], after["s_read"](i, 5 + T_BANKS[n]))
                if e == 1:
                    eng.wait_ge(sem["t_ev"], after["t_ev"](i, 4))
                    if more and T_BANKS[n] >= 4:
                        eng.wait_ge(sem["v_ev"], after["v_ev"](i + 1, o))
                for h in range(4):
                    ins = eng.transpose(psum[T_BANKS[n]][:, h * P:(h + 1) * P],
                                        b.probs[:, e, 4 * g + h, :], ident)
                ins.then_inc(sem["t_ps"], 1)

            def values(i, e, g):
                eng.wait_ge(sem["t_ev"], after["t_ev"](i, 4 * e + g + 1))
                n = e * o + g * o // 4
                if n >= 2 and g % (4 // o) == 0:
                    eng.wait_ge(sem["o_ev"], after["o_ev"](i, n - 1))
                for h in range(4 * g, 4 * g + 4):
                    row, chunk = h * hv % P, h * hv // P
                    ins = eng.matmul(psum[6 + n % 2][row:row + hv, chunk % 4 * P:(chunk % 4 + 1) * P],
                                     b.v[:, e, h * hv:(h + 1) * hv], b.probs_t[:, h, :],
                                     start=True, stop=True)
                if g % (4 // o) == 4 // o - 1:
                    ins.then_inc(sem["pv_ps"], 1)

            def output(i, e):
                eng.wait_ge(sem["o_ev"], after["o_ev"](i, (e + 1) * o))
                eng.wait_ge(sem["s_read"], after["s_read"](i, 8))
                for c in range(p["vc"]):
                    ins = eng.matmul(psum[3][:, e * P:(e + 1) * P], b.o_t[:, e, c, :],
                                     wo[:, c * P:(c + 1) * P], start=(c == 0),
                                     stop=(c == p["vc"] - 1))
                if e:
                    ins.then_inc(sem["o_ps"], 1)

            def body(i, more):
                for e in range(2):
                    for g in range(4):
                        scores(i, e, g)
                        if more and e == 1 and g == 0:
                            pe_transpose_front(eng, l, i + 1, 7)
                        if more and e == 1 and g == 2:
                            project_qk(i + 1, 0, early)
                if more:
                    project_qk(i + 1, early, u)
                for e in range(2):
                    transposes(i, e, 0, more)
                    transposes(i, e, 1, more)
                    if e == 0 and more:
                        eng.wait_ge(sem["qk_ev"], after["qk_ev"](i + 1, 2 * u))
                    elif e == 0:
                        eng.wait_ge(sem["v_ev"], after["v_ev"](i, 2 * o))
                    for g in range(4):
                        if g < 2:
                            transposes(i, e, g + 2, more)
                        values(i, e, g)
                    if more:
                        if e:
                            eng.wait_ge(sem["t_ev"], after["t_ev"](i, 8))
                        project_v(i + 1, e)
                    output(i, e)

            run_steps(eng, batch // 2, front, body)

        def act_attention(eng, l):
            p, after, b = parts[l], afters[l], AttentionBuffers(parts[l])
            u, o, cpu = units(p), p["vc"] // 4, min(p["qc"], 2)

            def qk_out(j, n):
                for k, whole in enumerate((b.k, b.q)):
                    eng.wait_ge(sem["qk_ps"], after["qk_ps"](j, 2 * n + k + 1))
                    src = psum[QK_BANKS[(2 * n + k) % 4]][:, 0:cpu * 2 * P]
                    src = src.rearrange("p (c e t) -> p c e t", c=cpu, e=2)
                    if k == 0:
                        eng.wait_ge(sem["kb_ready"], after["kb_ready"](j, 0))
                    eng.activation(whole[:, cpu * n:cpu * n + cpu, :, :], src, ACT.Copy)\
                       .then_inc(sem["qk_ev"], 1)

            def v_out(j, e):
                for half in range(o):
                    eng.wait_ge(sem["v_ps"], after["v_ps"](j, e * o + half + 1))
                    eng.activation(b.v[:, e, half * BANK:(half + 1) * BANK], psum[4 + half][:, :],
                                   ACT.Copy).then_inc(sem["v_ev"], 1)

            def front(j):
                act_front_out(eng, l, j, 7)
                for n in range(u):
                    qk_out(j, n)
                v_out(j, 0)
                v_out(j, 1)

            def outputs(i, e):
                for half in range(o):
                    n = e * o + half
                    eng.wait_ge(sem["pv_ps"], after["pv_ps"](i, n + 1))
                    dst = b.o_t[:, e, 4 * half:4 * half + 4, :]
                    src = psum[6 + n % 2][:, :].rearrange("p (c t) -> p c t", c=4)
                    eng.activation(dst, src, ACT.Copy).then_inc(sem["o_ev"], 1)

            def exps(i, e, g):
                dst = b.probs[:, e, 4 * g:4 * g + 4, :]
                if p["taylor"]:
                    eng.wait_ge(sem["s_ps"], after["s_ps"](i, 4 * e + g + 1))
                    eng.activation(dst, psum[g][:, :].rearrange("p (h t) -> p h t", h=4), ACT.Square,
                                   bias=1.0, scale=0.25).then_inc(sem["s_read"], 1)
                else:
                    eng.wait_ge(sem["s_read"], after["s_read"](i, 4 * e + g + 1))
                    eng.activation(dst, dst, ACT.Exp, scale=p["scale"]).then_inc(sem["p_exp"], 1)

            def transposed(i, e, g):
                n = 4 * e + g
                eng.wait_ge(sem["t_ps"], after["t_ps"](i, n + 1))
                eng.activation(b.probs_t[:, 4 * g:4 * g + 4, :],
                               psum[T_BANKS[n]][:, :].rearrange("p (h t) -> p h t", h=4),
                               ACT.Copy).then_inc(sem["t_ev"], 1)

            def body(i, more):
                for g in range(4):
                    if more and g == 3 and not p["taylor"]:
                        act_front_out(eng, l, i + 1, 7)
                    exps(i, 0, g)
                exps(i, 1, 0)
                if more and p["taylor"]:
                    act_front_out(eng, l, i + 1, 7)
                splits = (0, int(p["qc"] >= 4), (u + 2) // 2, u)
                for g in range(1, 4):
                    if more:
                        for n in range(splits[g - 1], splits[g]):
                            qk_out(i + 1, n)
                    if g == 3:
                        transposed(i, 0, 0)
                        transposed(i, 0, 1)
                    exps(i, 1, g)
                for e in range(2):
                    for g in range(4):
                        if e or g >= 2:
                            transposed(i, e, g)
                    outputs(i, e)
                    if more:
                        v_out(i + 1, e)

            run_steps(eng, batch // 2, front, body)

        def dve_attention(eng, l):
            p, after, b = parts[l], afters[l], AttentionBuffers(parts[l])

            def front(j):
                dve_front_stats(eng, l, j)
                dve_front_norm(eng, l, j)

            def shift(i, e, g):
                n = 4 * e + g
                eng.wait_ge(sem["s_ps"], after["s_ps"](i, n + 1))
                src = psum[g][:, :].rearrange("p (h t) -> p h t", h=4)
                m = b.max[:, e, 4 * g:4 * g + 4]
                eng.tensor_reduce(m, src, AX_X, ALU.max).then_inc(sem["s_max"], 1)
                eng.wait_ge(sem["s_max"], after["s_max"](i, n + 1))
                eng.tensor_tensor(b.probs[:, e, 4 * g:4 * g + 4, :], src, bcast(m, 2, P), ALU.subtract)\
                   .then_inc(sem["s_read"], 1)

            def taylor_mask(i, e, g):
                n = 4 * e + g
                eng.wait_ge(sem["s_read"], after["s_read"](i, n + 1))
                dst = b.probs[:, e, 4 * g:4 * g + 4, :]
                eng.scalar_tensor_tensor(out=dst, in0=dst, scalar=1.0, in1=bcast(const("lower"), 1, 4),
                                         op0=ALU.add, op1=ALU.mult).then_inc(sem["s_mask"], 1)

            first_pass = taylor_mask if p["taylor"] else shift

            def sums(i, e, half):
                n = 2 * e + half
                hs = slice(8 * half, 8 * half + 8)
                if p["taylor"]:
                    eng.wait_ge(sem["s_mask"], after["s_mask"](i, 4 * e + 2 * half + 2))
                else:
                    eng.wait_ge(sem["p_exp"], after["p_exp"](i, 4 * e + 2 * half + 2))
                eng.tensor_reduce(b.sum[:, e, hs], b.probs[:, e, hs, :], AX_X, ALU.add)\
                   .then_inc(sem["p_sum"], 1)
                eng.wait_ge(sem["p_sum"], after["p_sum"](i, n + 1))
                if p["taylor"]:
                    eng.tensor_scalar(b.max[:, e, hs], b.sum[:, e, hs], 2e-12, None, ALU.add)\
                       .then_inc(sem["p_eps"], 1)
                    eng.wait_ge(sem["p_eps"], after["p_eps"](i, n + 1))
                    eng.reciprocal(b.rec[:, e, hs], b.max[:, e, hs]).then_inc(sem["p_rec"], 1)
                else:
                    eng.reciprocal(b.rec[:, e, hs], b.sum[:, e, hs]).then_inc(sem["p_rec"], 1)

            def tail_add(i):
                eng.wait_ge(sem["o_ps"], after["o_ps"](i, 1))
                dve_tail_add(eng, l, i, psum[3][:, 0:2 * P].rearrange("p (e c) -> p e c", e=2))

            def tail(i):
                tail_add(i)
                dve_tail_stats(eng, l, i)
                dve_tail_norm(eng, l, i)

            def body(i, before, more):
                if more:
                    dve_front_stats(eng, l, i + 1)
                first_pass(i, 0, 0)
                if before:
                    tail_add(i - 1)
                if more:
                    dve_front_norm(eng, l, i + 1)
                first_pass(i, 0, 1)
                if before:
                    dve_tail_stats(eng, l, i - 1)
                first_pass(i, 0, 2)
                first_pass(i, 0, 3)
                if before:
                    dve_tail_norm(eng, l, i - 1)
                if p["taylor"] or p["post_mask"]:
                    sums(i, 0, 0)
                    first_pass(i, 1, 0)
                else:
                    first_pass(i, 1, 0)
                    sums(i, 0, 0)
                first_pass(i, 1, 1)
                sums(i, 0, 1)
                first_pass(i, 1, 2)
                sums(i, 1, 0)
                first_pass(i, 1, 3)
                sums(i, 1, 1)

            run_tailed(eng, batch // 2, front, body, tail)

        def pool_attention(eng, l):
            p, after, b = parts[l], afters[l], AttentionBuffers(parts[l])
            u, r, cpu = units(p), HEADS // p["qc"], min(p["qc"], 2)
            rows = const(f"heads{r}")

            def spread_k(j):
                for e in range(2):
                    for n in range(u):
                        eng.wait_ge(sem["qk_ev"], after["qk_ev"](j, 2 * n + 1))
                        for c in range(cpu * n, cpu * n + cpu):
                            ins = eng.tensor_tensor(b.kb[:, e, c, :, :], bcast(b.k[:, c, e, :], 1, r),
                                                    bcast(rows, 2, P), ALU.mult)
                        ins.then_inc(sem["kb_ready"], 1)

            def front(j):
                pool_front_rstd(eng, l, j)
                spread_k(j)

            def normalise(i, e, half):
                n = 2 * e + half
                hs = slice(8 * half, 8 * half + 8)
                probs = b.probs[:, e, hs, :]
                eng.wait_ge(sem["p_rec"], after["p_rec"](i, n + 1))
                done = sem["p_mul"] if p["post_mask"] else sem["p_norm"]
                eng.tensor_tensor(probs, probs, bcast(b.rec[:, e, hs], 2, P), ALU.mult)\
                   .then_inc(done, 1)
                if p["post_mask"]:
                    eng.wait_ge(sem["p_mul"], after["p_mul"](i, n + 1))
                    pool_gate(eng)
                    eng.affine_select(out=probs, in_=probs, compare_op=ALU.is_gt, fill=0.0, base=0,
                                      pattern=[[0, 8], [1, P]], channel_multiplier=-1)\
                       .then_inc(sem["p_norm"], 1)

            def body(i, before, more):
                if more:
                    pool_front_rstd(eng, l, i + 1)
                if before:
                    pool_tail_rstd(eng, l, i - 1)
                for e in range(2):
                    for half in range(2):
                        normalise(i, e, half)
                if more:
                    spread_k(i + 1)

            def tail(i):
                pool_tail_rstd(eng, l, i)

            run_tailed(eng, batch // 2, front, body, tail)

        SCORE_BANKS = (0, 1, 2, 0, 1, 2, 0, 1)

        class NarrowBuffers:
            def __init__(self):
                at = [0]

                def cut(n):
                    at[0] += n
                    return arena[:, at[0] - n:at[0]]

                self.kq = cut(2 * 2 * P).rearrange("p (e k t) -> p e k t", e=2, k=2)
                self.kb = cut(2 * HEADS * P).rearrange("p (e h t) -> p e h t", e=2, h=HEADS)
                self.v = cut(2 * P).rearrange("p (e n) -> p e n", e=2)
                self.probs = cut(2 * HEADS * P).rearrange("p (e h t) -> p e h t", e=2, t=P)
                self.probs_t = cut(HEADS * P).rearrange("p (h t) -> p h t", t=P)
                self.o = cut(2 * P).rearrange("p (e n) -> p e n", e=2)
                self.o_t = cut(2 * P).rearrange("p (e t) -> p e t", e=2)
                self.max, self.neg_max, self.sum, self.rec = (
                    cut(2 * HEADS).rearrange("p (e h) -> p e h", e=2) for _ in range(4))
                self.kq_ps = psum[6][:, 0:2 * P].rearrange("p (k t) -> p k t", k=2)
                self.out_ps = psum[6][:, 2 * P:4 * P].rearrange("p (e c) -> p e c", e=2)
                self.v_ps = psum[7][:, 0:P]
                self.o_ps = psum[3][:, 0:P]
                self.ot_ps = psum[7][:, 3 * P:4 * P]

        def pe_narrow(eng, l):
            p, after, b = parts[l], afters[l], NarrowBuffers()
            wqkv, wo = weight(l, "wqkv"), weight(l, "wo")

            def transpose_front(j):
                eng.wait_ge(sem["v_ev"], after["v_ev"](j, 0))
                pe_transpose_front(eng, l, j, 7)

            def project_qk(j, e):
                eng.wait_ge(sem["zt_ready"], after["zt_ready"](j, 1))
                eng.wait_ge(sem["qk_ev"], after["qk_ev"](j, e))
                for k, at in enumerate((P, 0)):
                    ins = eng.matmul(b.kq_ps[:, k, :], wqkv[:, at:at + P], z_t[:, e * P:(e + 1) * P],
                                     start=True, stop=True)
                ins.then_inc(sem["qk_ps"], 1)

            def project_v(j, e):
                eng.wait_ge(sem["v_ev"], after["v_ev"](j, e))
                eng.matmul(b.v_ps, z_t[:, e * P:(e + 1) * P], wqkv[:, 2 * P:3 * P], start=True,
                           stop=True).then_inc(sem["v_ps"], 1)

            def scores(j, e, g):
                eng.wait_ge(sem["qk_ev"], after["qk_ev"](j, e + 1))
                eng.wait_ge(sem["kb_ready"], after["kb_ready"](j, 2 * e + g // 2 + 1))
                bank = psum[SCORE_BANKS[4 * e + g]]
                eng.matmul(bank[:, :], const_bf("ident"), bcast(const_bf(p["mask"]), 1, 4),
                           start=True, stop=False)
                eng.matmul(bank[:, :], b.kq[:, e, 1, :], b.kb[:, e, 4 * g:4 * g + 4, :],
                           start=False, stop=True).then_inc(sem["s_ps"], 1)

            def transposes(i, e, g):
                if g < 2:
                    eng.wait_ge(sem["t_ev"], after["t_ev"](i, 4 * e))
                else:
                    eng.wait_ge(sem["t_ev"], after["t_ev"](i, 4 * e + g - 1))
                eng.wait_ge(sem["p_exp"], after["p_exp"](i, 4 * e + g + 1))
                for h in range(4):
                    ins = eng.transpose(psum[4 + g % 2][:, h * P:(h + 1) * P],
                                        b.probs[:, e, 4 * g + h, :], ident)
                ins.then_inc(sem["t_ps"], 1)

            def values(i, e, g):
                if g == 0:
                    eng.wait_ge(sem["o_norm"], after["o_norm"](i, e))
                    eng.wait_ge(sem["v_ev"], after["v_ev"](i, e + 1))
                eng.wait_ge(sem["t_ev"], after["t_ev"](i, 4 * e + g + 1))
                for h in range(4 * g, 4 * g + 4):
                    ins = eng.matmul(b.o_ps[:, h * 8:(h + 1) * 8], b.probs_t[:, h, :],
                                     b.v[:, e, h * 8:(h + 1) * 8], start=True, stop=True)
                if g == 3:
                    ins.then_inc(sem["pv_ps"], 1)

            def transpose_values(i, e):
                eng.wait_ge(sem["o_norm"], after["o_norm"](i, e + 1))
                eng.wait_ge(sem["o_ev"], after["o_ev"](i, e))
                eng.transpose(b.ot_ps, b.o[:, e, :], ident).then_inc(sem["ot_ps"], 1)

            def output(i, e):
                eng.wait_ge(sem["o_ev"], after["o_ev"](i, e + 1))
                eng.wait_ge(sem["tail_read"], after["tail_read"](i, 0))
                eng.matmul(b.out_ps[:, e, :], b.o_t[:, e, :], wo, start=True, stop=True)\
                   .then_inc(sem["o_ps"], 1)

            def front(j):
                transpose_front(j)
                project_qk(j, 0)
                project_qk(j, 1)
                project_v(j, 0)
                project_v(j, 1)
                for g in range(4):
                    if g == 3:
                        eng.wait_ge(sem["p_exp"], after["p_exp"](j, 1))
                    scores(j, 0, g)

            def body(i, before, more):
                for g in range(4):
                    eng.wait_ge(sem["p_exp"], after["p_exp"](i, g + 2))
                    scores(i, 1, g)
                    if g == 0 and before:
                        values(i - 1, 1, 3)
                        eng.wait_ge(sem["o_ev"], after["o_ev"](i - 1, 1))
                        project_v(i, 1)
                    if g == 1 and before:
                        eng.wait_ge(sem["v_ev"], after["v_ev"](i, 2))
                        transpose_values(i - 1, 1)
                    if g == 2 and more:
                        project_qk(i + 1, 0)
                    if g == 3 and before:
                        if more:
                            eng.wait_ge(sem["qk_ev"], after["qk_ev"](i + 1, 1))
                        output(i - 1, 1)
                    transposes(i, 0, g)
                    if g:
                        values(i, 0, g - 1)
                    if g == 1 and more:
                        eng.wait_ge(sem["o_ev"], after["o_ev"](i, 0))
                        transpose_front(i + 1)
                for g in range(4):
                    if more:
                        if g == 3:
                            eng.wait_ge(sem["p_exp"], after["p_exp"](i + 1, 1))
                        else:
                            eng.wait_ge(sem["p_exp"], after["p_exp"](i, (7, 8, 6)[g]))
                        scores(i + 1, 0, g)
                    if g == 0:
                        values(i, 0, 3)
                        if more:
                            project_v(i + 1, 0)
                    if g == 1:
                        if more:
                            eng.wait_ge(sem["v_ev"], after["v_ev"](i + 1, 1))
                        transpose_values(i, 0)
                    if g == 2:
                        if more:
                            eng.wait_ge(sem["qk_ev"], after["qk_ev"](i + 1, 2))
                        output(i, 0)
                    transposes(i, 1, g)
                    if g == 1 and more:
                        eng.wait_ge(sem["tail_read"], after["tail_read"](i, 0))
                        project_qk(i + 1, 1)
                    if g:
                        values(i, 1, g - 1)

            def tail(i):
                values(i, 1, 3)
                transpose_values(i, 1)
                output(i, 1)

            run_tailed(eng, batch // 2, front, body, tail)

        def act_narrow(eng, l):
            p, after, b = parts[l], afters[l], NarrowBuffers()

            def qk_out(j, e):
                eng.wait_ge(sem["qk_ps"], after["qk_ps"](j, e + 1))
                eng.wait_ge(sem["kb_ready"], after["kb_ready"](j, 2 * e))
                if p["qkv_bias"]:
                    eng.activation(b.kq[:, e, 0, :], b.kq_ps[:, 0, :], ACT.Identity,
                                   bias=weight(l, "bqkv")[:, 1:2])
                    eng.activation(b.kq[:, e, 1, :], b.kq_ps[:, 1, :], ACT.Identity,
                                   bias=weight(l, "bqkv")[:, 0:1]).then_inc(sem["qk_ev"], 1)
                else:
                    eng.activation(b.kq[:, e, :, :], b.kq_ps, ACT.Copy).then_inc(sem["qk_ev"], 1)

            def v_out(j, e):
                eng.wait_ge(sem["v_ps"], after["v_ps"](j, e + 1))
                eng.activation(b.v[:, e, :], b.v_ps, ACT.Copy).then_inc(sem["v_ev"], 1)

            def exps(j, e, g):
                eng.wait_ge(sem["n_max"], after["n_max"](j, 4 * e + g + 1))
                bank = psum[SCORE_BANKS[4 * e + g]]
                for h in range(4 * g, 4 * g + 4):
                    ins = eng.activation(b.probs[:, e, h, :], bank[:, h % 4 * P:(h % 4 + 1) * P],
                                         ACT.Exp, scale=p["scale"], bias=b.neg_max[:, e, h:h + 1],
                                         accum_out=b.sum[:, e, h:h + 1])
                ins.then_inc(sem["p_exp"], 1)

            def values_out(i, e):
                eng.wait_ge(sem["ot_ps"], after["ot_ps"](i, e + 1))
                if p["qkv_bias"]:
                    eng.activation(b.o_t[:, e, :], b.ot_ps, ACT.Identity,
                                   bias=weight(l, "bqkv")[:, 2:3]).then_inc(sem["o_ev"], 1)
                else:
                    eng.activation(b.o_t[:, e, :], b.ot_ps, ACT.Copy).then_inc(sem["o_ev"], 1)

            def front(j):
                act_front_out(eng, l, j, 7)
                qk_out(j, 0)
                qk_out(j, 1)
                v_out(j, 0)
                v_out(j, 1)
                for g in range(4):
                    exps(j, 0, g)

            def body(i, before, more):
                for g in range(4):
                    if g == 0 and before:
                        v_out(i, 1)
                    if g == 1 and before:
                        values_out(i - 1, 1)
                    if g == 2 and more:
                        qk_out(i + 1, 0)
                    exps(i, 1, g)
                    if g == 1 and more:
                        act_front_out(eng, l, i + 1, 7)
                for g in range(4):
                    if g == 0 and more:
                        v_out(i + 1, 0)
                    if g == 1:
                        values_out(i, 0)
                    if more:
                        exps(i + 1, 0, g)
                    if g == 1 and more:
                        qk_out(i + 1, 1)

            def tail(i):
                values_out(i, 1)

            run_tailed(eng, batch // 2, front, body, tail)

        def dve_narrow(eng, l):
            p, after, b = parts[l], afters[l], NarrowBuffers()
            twice = p["name"] == "L0_attn"

            def maxima(j, e, g):
                eng.wait_ge(sem["s_ps"], after["s_ps"](j, 4 * e + g + 1))
                hs = slice(4 * g, 4 * g + 4)
                src = psum[SCORE_BANKS[4 * e + g]][:, :].rearrange("p (h t) -> p h t", h=4)
                eng.tensor_reduce(b.max[:, e, hs], src, AX_X, ALU.max).then_inc(sem["s_max"], 1)
                eng.wait_ge(sem["s_max"], after["s_max"](j, 4 * e + g + 1))
                eng.tensor_scalar(b.neg_max[:, e, hs], b.max[:, e, hs], -p["scale"], None,
                                  ALU.mult).then_inc(sem["n_max"], 1)

            def transposed(i, e, g):
                eng.wait_ge(sem["t_ps"], after["t_ps"](i, 4 * e + g + 1))
                dve_gate(eng)
                eng.tensor_copy(b.probs_t[:, 4 * g:4 * g + 4, :],
                                psum[4 + g % 2][:, :].rearrange("p (h t) -> p h t", h=4))\
                   .then_inc(sem["t_ev"], 1)

            def reciprocals(i, e):
                eng.wait_ge(sem["p_exp"], after["p_exp"](i, 4 * e + 4))
                eng.reciprocal(b.rec[:, e, :], b.sum[:, e, :]).then_inc(sem["p_rec"], 1)

            def normalise(i, e):
                eng.wait_ge(sem["p_rec"], after["p_rec"](i, e + 1))
                eng.wait_ge(sem["pv_ps"], after["pv_ps"](i, e + 1))
                eng.tensor_tensor(b.o[:, e, :].rearrange("p (h d) -> p h d", h=HEADS),
                                  b.o_ps.rearrange("p (h d) -> p h d", h=HEADS),
                                  bcast(b.rec[:, e, :], 2, 8), ALU.mult).then_inc(sem["o_norm"], 1)

            def tail_add(i):
                eng.wait_ge(sem["o_ps"], after["o_ps"](i, 2))
                dve_tail_add(eng, l, i, b.out_ps)

            def front(j):
                dve_front_stats(eng, l, j)
                dve_front_norm(eng, l, j)
                for g in range(4):
                    maxima(j, 0, g)

            def body(i, before, more):
                if more:
                    dve_front_stats(eng, l, i + 1)
                for g in range(4):
                    maxima(i, 1, g)
                    if g == 0:
                        if before:
                            normalise(i - 1, 1)
                        if more:
                            dve_front_norm(eng, l, i + 1)
                        reciprocals(i, 0)
                    transposed(i, 0, g)
                    if g == 3 and before:
                        tail_add(i - 1)
                        dve_tail_stats(eng, l, i - 1)
                for g in range(4):
                    if more:
                        maxima(i + 1, 0, g)
                    if g == 0:
                        normalise(i, 0)
                        reciprocals(i, 1)
                    transposed(i, 1, g)
                    if g == 0 and before:
                        dve_tail_norm(eng, l, i - 1)
                    if g == 1 and before and twice:
                        dve_tail_stats(eng, l, i - 1, 1)
                    if g == 3 and before and twice:
                        dve_tail_norm(eng, l, i - 1, 1)

            def tail(i):
                normalise(i, 1)
                tail_add(i)
                dve_tail_stats(eng, l, i)
                dve_tail_norm(eng, l, i)
                if twice:
                    dve_tail_stats(eng, l, i, 1)
                    dve_tail_norm(eng, l, i, 1)

            run_tailed(eng, batch // 2, front, body, tail)

        def pool_narrow(eng, l):
            after, b = afters[l], NarrowBuffers()
            twice = parts[l]["name"] == "L0_attn"

            def spread_k(j, e):
                eng.wait_ge(sem["qk_ev"], after["qk_ev"](j, e + 1))
                for half in range(2):
                    hs = slice(8 * half, 8 * half + 8)
                    eng.tensor_tensor(b.kb[:, e, hs, :], bcast(b.kq[:, e, 0, :], 1, 8),
                                      bcast(const("heads16")[:, hs], 2, P), ALU.mult)\
                       .then_inc(sem["kb_ready"], 1)

            def front(j):
                pool_front_rstd(eng, l, j)
                spread_k(j, 0)
                spread_k(j, 1)

            def body(i, before, more):
                if more:
                    pool_front_rstd(eng, l, i + 1)
                    spread_k(i + 1, 0)
                if before:
                    pool_tail_rstd(eng, l, i - 1)
                if before and twice:
                    pool_tail_rstd(eng, l, i - 1, 1)
                if more:
                    spread_k(i + 1, 1)

            def tail(i):
                pool_tail_rstd(eng, l, i)
                if twice:
                    pool_tail_rstd(eng, l, i, 1)

            run_tailed(eng, batch // 2, front, body, tail)


        class ExpertBuffers:
            def __init__(self):
                at = [0]

                def cut(n):
                    at[0] += n
                    return arena[:, at[0] - n:at[0]]

                self.gate = cut(2 * BANK).rearrange("p (b n) -> p b n", b=2)
                self.h = cut(2 * 4 * BANK).rearrange("p (b c n) -> p b c n", b=2, c=4)
                self.acc = cut(4 * P).rearrange("p (t c) -> p t c", t=4)
                self.logits = cut(4 * 9).rearrange("p (t e) -> p t e", t=4)
                self.shifted = cut(4 * 9).rearrange("p (t e) -> p t e", t=4)
                self.exps = cut(4 * 9).rearrange("p (t e) -> p t e", t=4)
                self.top = cut(4 * 8).rearrange("p (t e) -> p t e", t=4)
                self.top_at = cut(4 * 8).rearrange("p (t e) -> p t e", t=4).bitcast(U32)
                self.index = cut(4 * 2).rearrange("p (t e) -> p t e", t=4)
                self.hot = cut(2 * 4 * 8).rearrange("p (k t e) -> p k t e", k=2, t=4)
                self.chosen = cut(4 * 8).rearrange("p (t e) -> p t e", t=4)
                self.picked = cut(4 * 8).rearrange("p (t e) -> p t e", t=4)
                self.den = cut(4 * 2).rearrange("p (t e) -> p t e", t=4)
                self.rden = cut(4 * 2).rearrange("p (t e) -> p t e", t=4)
                self.w = cut(4 * 9).rearrange("p (t e) -> p t e", t=4)

        def expert_chunks(p):
            found, n, at = [], 0, 0
            for e, pieces in enumerate(p["chunks"]):
                for c, size in enumerate(pieces):
                    found.append((e, c, n, size, at))
                    n += 1
                    at += size * (2 if p["gated"] else 1)
            return found

        def pe_experts(eng, l):
            p, after, b = parts[l], afters[l], ExpertBuffers()
            chunks, ne = expert_chunks(p), len(p["chunks"])
            up_w, down_w = weight(l, "up"), weight(l, "down")

            def front(j):
                pe_transpose_front(eng, l, j, 4)

            def wait_hidden(i, n):
                if p["gated"]:
                    eng.wait_ge(sem["h_ready"], after["h_ready"](i, n))
                else:
                    eng.wait_ge(sem["act_ev"], after["act_ev"](i, n))

            def up(i, e):
                for ex, _, n, size, at in chunks:
                    if ex != e:
                        continue
                    if p["gated"]:
                        wait_hidden(i, max(n - 1, 0))
                        for k in range(2):
                            ins = eng.matmul(psum[2 * (n % 2) + k][0:size, :],
                                             up_w[:, at + k * size:at + (k + 1) * size], z_t[:, :],
                                             start=True, stop=True)
                    else:
                        wait_hidden(i, max(n - 3, 0))
                        ins = eng.matmul(psum[n % 4][0:size, :], up_w[:, at:at + size], z_t[:, :],
                                         start=True, stop=True)
                    ins.then_inc(sem["up_ps"], 1)

            def down(i, e):
                mine = [c for c in chunks if c[0] == e]
                if p["routing"]:
                    eng.wait_ge(sem["acc"], after["acc"](i, max(e - 1, 0)))
                else:
                    eng.wait_ge(sem["tail_read"], after["tail_read"](i, 0))
                wait_hidden(i, mine[-1][2] + 1)
                for t in range(4):
                    for _, c, n, size, _ in mine:
                        ins = eng.matmul(psum[6 + e % 2][:, t * P:(t + 1) * P],
                                         b.h[0:size, e % 2, c, t * P:(t + 1) * P],
                                         down_w[0:size, n * P:(n + 1) * P], start=(c == 0),
                                         stop=(c == len(mine) - 1))
                ins.then_inc(sem["y_ps"], 1)

            def body(i, more):
                eng.wait_ge(sem["zt_ready"], after["zt_ready"](i, 1))
                if p["routing"]:
                    eng.wait_ge(sem["route"], after["route"](i, 0))
                    ng = 8 + p["shared"]
                    for t in range(4):
                        ins = eng.matmul(psum[5][:, t * ng:(t + 1) * ng], z_t[:, t * P:(t + 1) * P],
                                         weight(l, "gate"), start=True, stop=True)
                    ins.then_inc(sem["gate_ps"], 1)
                for e in range(ne):
                    up(i, e)
                    if e:
                        down(i, e - 1)
                if more:
                    front(i + 1)
                down(i, ne - 1)

            run_steps(eng, batch // 4, front, body)

        def act_experts(eng, l):
            p, after, b = parts[l], afters[l], ExpertBuffers()
            chunks, ne = expert_chunks(p), len(p["chunks"])

            def front(j):
                act_front_out(eng, l, j, 4)

            def hidden(i, e):
                for ex, c, n, size, _ in chunks:
                    if ex != e:
                        continue
                    eng.wait_ge(sem["up_ps"], after["up_ps"](i, n + 1))
                    if p["gated"]:
                        dst, src = b.gate[0:size, n % 2, :], psum[2 * (n % 2)][0:size, :]
                    else:
                        dst, src = b.h[0:size, e % 2, c, :], psum[n % 4][0:size, :]
                    if p["hidden_bias"]:
                        ins = eng.activation(dst, src, p["func"], bias=weight(l, "bh")[:, n:n + 1])
                    else:
                        ins = eng.activation(dst, src, p["func"])
                    ins.then_inc(sem["act_ev"], 1)

            def body(i, more):
                for e in range(ne):
                    hidden(i, e)
                    if e == 1 and p["routing"]:
                        eng.wait_ge(sem["route"], after["route"](i, 4))
                        ins = eng.activation(b.exps[:, :, 0:8], b.shifted[:, :, 0:8], ACT.Exp)
                        if p["shared"]:
                            ins = eng.activation(b.exps[:, :, 8:9], b.logits[:, :, 8:9], ACT.Exp,
                                                 scale=-1.0)
                        ins.then_inc(sem["route_exp"], 1)
                if more:
                    front(i + 1)

            run_steps(eng, batch // 4, front, body)

        def dve_experts(eng, l):
            p, after, b = parts[l], afters[l], ExpertBuffers()
            chunks, ne = expert_chunks(p), len(p["chunks"])
            ng = 8 + p["shared"]

            def front(j):
                dve_front_stats(eng, l, j)
                dve_front_norm(eng, l, j)

            def route_before(i):
                eng.wait_ge(sem["gate_ps"], after["gate_ps"](i, 1))
                eng.tensor_copy(b.logits[:, :, 0:ng], psum[5][:, 0:4 * ng].rearrange("p (t e) -> p t e", t=4))\
                   .then_inc(sem["route"], 1)
                eng.wait_ge(sem["route"], after["route"](i, 1))
                dve_gate(eng)
                for t in range(4):
                    ins = eng.max(b.top[:, t, :], b.logits[:, t, 0:8])
                ins.then_inc(sem["route"], 1)
                eng.wait_ge(sem["route"], after["route"](i, 2))
                dve_gate(eng)
                for t in range(4):
                    ins = eng.max_index(b.top_at[:, t, :], b.top[:, t, :], b.logits[:, t, 0:8])
                ins.then_inc(sem["route"], 1)
                eng.tensor_tensor(b.shifted[:, :, 0:8], b.logits[:, :, 0:8],
                                  b.top[:, :, 0:1].to_broadcast([P, 4, 8]), ALU.subtract)\
                   .then_inc(sem["route"], 1)
                eng.wait_ge(sem["route"], after["route"](i, 3))
                eng.tensor_copy(b.index[:, :, :], b.top_at[:, :, 0:2]).then_inc(sem["route"], 1)
                eng.wait_ge(sem["route"], after["route"](i, 5))
                for k in range(2):
                    ins = eng.tensor_tensor(b.hot[:, k, :, :], bcast(const("iota"), 1, 4),
                                            b.index[:, :, k:k + 1].to_broadcast([P, 4, 8]),
                                            ALU.is_equal)
                ins.then_inc(sem["route"], 1)
                eng.wait_ge(sem["route"], after["route"](i, 6))
                eng.tensor_tensor(b.chosen[:, :, :], b.hot[:, 0, :, :], b.hot[:, 1, :, :], ALU.add)\
                   .then_inc(sem["route"], 1)

            def route_after(i):
                k = 7
                eng.wait_ge(sem["route_exp"], after["route_exp"](i, 1))
                eng.wait_ge(sem["route"], after["route"](i, k))
                eng.tensor_tensor(b.picked[:, :, :], b.exps[:, :, 0:8], b.chosen[:, :, :], ALU.mult)\
                   .then_inc(sem["route"], 1)
                k += 1
                eng.wait_ge(sem["route"], after["route"](i, k))
                over = b.picked if p["routing"] == "top" else b.exps
                eng.tensor_reduce(b.den[:, :, 0], over[:, :, 0:8], AX_X, ALU.add).then_inc(sem["route"], 1)
                k += 1
                eng.wait_ge(sem["route"], after["route"](i, k))
                if p["shared"]:
                    eng.tensor_scalar(b.den[:, :, 1], b.exps[:, :, 8], 1.0, None, ALU.add)\
                       .then_inc(sem["route"], 1)
                    k += 1
                    eng.wait_ge(sem["route"], after["route"](i, k))
                nd = 1 + p["shared"]
                eng.reciprocal(b.rden[:, :, 0:nd], b.den[:, :, 0:nd]).then_inc(sem["route"], 1)
                k += 1
                eng.wait_ge(sem["route"], after["route"](i, k))
                eng.tensor_tensor(b.w[:, :, 0:8], b.picked[:, :, :],
                                  b.rden[:, :, 0:1].to_broadcast([P, 4, 8]), ALU.mult).then_inc(sem["route"], 1)
                k += 1
                if p["shared"]:
                    eng.tensor_copy(b.w[:, :, 8], b.rden[:, :, 1]).then_inc(sem["route"], 1)
                    k += 1
                eng.wait_ge(sem["route"], after["route"](i, k))
                dve_gate(eng)
                assert k == after["route"].n

            def hidden(i, e):
                for ex, c, n, size, _ in chunks:
                    if ex == e:
                        eng.wait_ge(sem["act_ev"], after["act_ev"](i, n + 1))
                        eng.tensor_tensor(b.h[0:size, e % 2, c, :], b.gate[0:size, n % 2, :],
                                          psum[2 * (n % 2) + 1][0:size, :], ALU.mult)\
                           .then_inc(sem["h_ready"], 1)

            def accumulate(i, e):
                eng.wait_ge(sem["y_ps"], after["y_ps"](i, e + 1))
                if e:
                    eng.wait_ge(sem["acc"], after["acc"](i, e))
                for t in range(4):
                    y, w = psum[6 + e % 2][:, t * P:(t + 1) * P], b.w[:, t, e:e + 1]
                    if e == 0:
                        ins = eng.tensor_scalar(b.acc[:, t, :], y, w, None, ALU.mult)
                    else:
                        ins = eng.scalar_tensor_tensor(out=b.acc[:, t, :], in0=y, scalar=w,
                                                       in1=b.acc[:, t, :], op0=ALU.mult, op1=ALU.add)
                ins.then_inc(sem["acc"], 1)

            def tail_add(i):
                if p["routing"]:
                    eng.wait_ge(sem["acc"], after["acc"](i, ne))
                    dve_tail_add(eng, l, i, b.acc[:, :, :])
                else:
                    eng.wait_ge(sem["y_ps"], after["y_ps"](i, 1))
                    dve_tail_add(eng, l, i, psum[6][:, :].rearrange("p (t c) -> p t c", t=4))

            def tail(i):
                tail_add(i)
                dve_tail_stats(eng, l, i)
                dve_tail_norm(eng, l, i)

            def mlp_body(i, before, more):
                if before:
                    tail_add(i - 1)
                if more:
                    dve_front_stats(eng, l, i + 1)
                if before:
                    dve_tail_stats(eng, l, i - 1)
                if more:
                    dve_front_norm(eng, l, i + 1)
                if before:
                    dve_tail_norm(eng, l, i - 1)

            def routed_body(i, before, more):
                route_before(i)
                for e in range(ne):
                    if p["gated"]:
                        hidden(i, e)
                    if e == 1 and before:
                        tail_add(i - 1)
                        dve_tail_stats(eng, l, i - 1)
                    if e == 2:
                        route_after(i)
                        accumulate(i, 0)
                        if before:
                            dve_tail_norm(eng, l, i - 1)
                    if e >= 2:
                        accumulate(i, e - 1)
                    if more and e == 3:
                        dve_front_stats(eng, l, i + 1)
                    if more and e == 4:
                        dve_front_norm(eng, l, i + 1)
                accumulate(i, ne - 1)

            run_tailed(eng, batch // 4, front, routed_body if p["routing"] else mlp_body, tail)

        def pool_norms(eng, l):
            def front(j):
                pool_front_rstd(eng, l, j)

            def tail(i):
                pool_tail_rstd(eng, l, i)

            def body(i, before, more):
                if more and not parts[l].get("routing"):
                    front(i + 1)
                if before:
                    tail(i - 1)
                if more and parts[l].get("routing"):
                    front(i + 1)

            run_tailed(eng, batch // 4, front, body, tail)


        class SingleBuffers:
            def __init__(self):
                self.q, self.k, self.v, self.probs, self.probs_t = (
                    arena[:, n * BANK:(n + 1) * BANK].rearrange("p (e t) -> p e t", e=4)
                    for n in range(5))
                self.max, self.sum, self.rec = (
                    arena[:, 5 * BANK + 4 * n:5 * BANK + 4 * n + 4] for n in range(3))

        def quads(bank):
            return psum[bank][:, :].rearrange("p (e t) -> p e t", e=4)

        def pe_single(eng, l):
            after, b = afters[l], SingleBuffers()

            def project_qk(j):
                pe_transpose_front(eng, l, j, 4)
                eng.wait_ge(sem["zt_ready"], after["zt_ready"](j, 1))
                eng.wait_ge(sem["q_ev"], after["q_ev"](j, 0))
                eng.matmul(psum[0][:, :], weight(l, "wq"), z_t[:, :], start=True, stop=True)\
                   .then_inc(sem["q_ps"], 1)
                eng.wait_ge(sem["ctx_in"], after["ctx_in"](j, 16))
                eng.wait_ge(sem["k_ev"], after["k_ev"](j, 0))
                eng.matmul(psum[1][:, :], weight(l, "wk"), y_t[0:CTX, :], start=True, stop=True)\
                   .then_inc(sem["k_ps"], 1)

            def project_v(j):
                eng.wait_ge(sem["v_ev"], after["v_ev"](j, 0))
                for e in range(4):
                    ins = eng.matmul(psum[2][:, e * P:(e + 1) * P], y_t[0:CTX, e * P:(e + 1) * P],
                                     weight(l, "wv"), start=True, stop=True)
                ins.then_inc(sem["v_ps"], 1)

            def front(j):
                project_qk(j)
                project_v(j)

            def body(i, more):
                eng.wait_ge(sem["q_ev"], after["q_ev"](i, 1))
                eng.wait_ge(sem["k_ev"], after["k_ev"](i, 1))
                eng.wait_ge(sem["s_read"], after["s_read"](i, 0))
                for e in range(4):
                    ins = eng.matmul(psum[3][:, e * P:(e + 1) * P], b.q[:, e, :], b.k[:, e, :],
                                     start=True, stop=True)
                ins.then_inc(sem["s_ps"], 1)
                if more:
                    project_qk(i + 1)
                eng.wait_ge(sem["p_norm"], after["p_norm"](i, 1))
                for e in range(4):
                    ins = eng.transpose(psum[5][:, e * P:(e + 1) * P], b.probs[:, e, :], ident)
                ins.then_inc(sem["t_ps"], 1)
                eng.wait_ge(sem["t_ev"], after["t_ev"](i, 1))
                eng.wait_ge(sem["v_ev"], after["v_ev"](i, 1))
                eng.wait_ge(sem["tail_read"], after["tail_read"](i, 0))
                for e in range(4):
                    ins = eng.matmul(psum[6][:, e * P:(e + 1) * P], b.probs_t[:, e, :], b.v[:, e, :],
                                     start=True, stop=True)
                ins.then_inc(sem["pv_ps"], 1)
                if more:
                    project_v(i + 1)

            run_steps(eng, batch // 4, front, body)

        def act_single(eng, l):
            after, b = afters[l], SingleBuffers()

            def front(j):
                act_front_out(eng, l, j, 4)
                eng.wait_ge(sem["q_ps"], after["q_ps"](j, 1))
                eng.activation(b.q, quads(0), ACT.Identity, bias=weight(l, "bq")).then_inc(sem["q_ev"], 1)

            def body(i, more):
                eng.wait_ge(sem["s_read"], after["s_read"](i, 1))
                eng.activation(b.probs, b.probs, ACT.Exp).then_inc(sem["p_exp"], 1)
                if more:
                    front(i + 1)
                eng.wait_ge(sem["t_ps"], after["t_ps"](i, 1))
                eng.activation(b.probs_t, quads(5), ACT.Copy).then_inc(sem["t_ev"], 1)

            run_steps(eng, batch // 4, front, body)

        def dve_single(eng, l):
            after, b = afters[l], SingleBuffers()

            def k_out(j):
                eng.wait_ge(sem["k_ps"], after["k_ps"](j, 1))
                eng.tensor_scalar(b.k, quads(1), weight(l, "bk"), None, ALU.add)\
                   .then_inc(sem["k_ev"], 1)

            def v_out(j):
                eng.wait_ge(sem["v_ps"], after["v_ps"](j, 1))
                eng.tensor_tensor(b.v, quads(2), bcast(weight(l, "bv"), 1, 4), ALU.add)\
                   .then_inc(sem["v_ev"], 1)

            def front(j):
                dve_front_norm(eng, l, j)
                k_out(j)
                v_out(j)

            def tail_add(i):
                eng.wait_ge(sem["pv_ps"], after["pv_ps"](i, 1))
                dve_tail_add(eng, l, i, quads(6))

            def tail(i):
                tail_add(i)
                dve_tail_stats(eng, l, i)
                dve_tail_norm(eng, l, i)

            def body(i, before, more):
                if more:
                    dve_front_norm(eng, l, i + 1)
                eng.wait_ge(sem["s_ps"], after["s_ps"](i, 1))
                eng.tensor_reduce(b.max, quads(3), AX_X, ALU.max).then_inc(sem["s_max"], 1)
                eng.wait_ge(sem["s_max"], after["s_max"](i, 1))
                eng.tensor_tensor(b.probs, quads(3), bcast(b.max, 2, P), ALU.subtract)\
                   .then_inc(sem["s_read"], 1)
                if before:
                    tail_add(i - 1)
                    dve_tail_stats(eng, l, i - 1)
                    v_out(i)
                eng.wait_ge(sem["p_exp"], after["p_exp"](i, 1))
                eng.tensor_reduce(b.sum, b.probs, AX_X, ALU.add).then_inc(sem["p_sum"], 1)
                eng.wait_ge(sem["p_sum"], after["p_sum"](i, 1))
                eng.reciprocal(b.rec, b.sum).then_inc(sem["p_rec"], 1)
                eng.wait_ge(sem["p_rec"], after["p_rec"](i, 1))
                eng.tensor_tensor(b.probs, b.probs, bcast(b.rec, 2, P), ALU.mult)\
                   .then_inc(sem["p_norm"], 1)
                if more:
                    k_out(i + 1)
                if before:
                    dve_tail_norm(eng, l, i - 1)

            run_tailed(eng, batch // 4, front, body, tail)


        class CosineBuffers:
            def __init__(self):
                def cut(n, m):
                    return arena[:, n * BANK:(n + m) * BANK]

                self.kv = cut(0, 2).rearrange("p (e n) -> p e n", e=4)
                self.q, self.q_cos, self.q_sin, self.k_cos, self.k_sin, self.kv_cos, self.kv_sin = (
                    cut(n, 1).rearrange("p (e t) -> p e t", e=4) for n in range(2, 9))

        def pe_cosine(eng, l):
            after, b = afters[l], CosineBuffers()

            def front(j):
                eng.wait_ge(sem["zt_ready"], after["zt_ready"](j, 1))
                eng.wait_ge(sem["kv_ev"], after["kv_ev"](j, 0))
                for pair in range(2):
                    for e in range(2 * pair, 2 * pair + 2):
                        ins = eng.matmul(psum[pair][:, e % 2 * 2 * P:(e % 2 + 1) * 2 * P],
                                         z_t[:, e * P:(e + 1) * P], weight(l, "wkv"), start=True,
                                         stop=True)
                    ins.then_inc(sem["kv_ps"], 1)
                eng.wait_ge(sem["q_ev"], after["q_ev"](j, 0))
                eng.matmul(psum[2][:, :], weight(l, "wq"), z_t[:, :], start=True, stop=True)\
                   .then_inc(sem["q_ps"], 1)

            def first(j):
                pe_transpose_front(eng, l, j, 4)
                front(j)

            def body(i, more):
                eng.wait_ge(sem["kcs"], after["kcs"](i, 1))
                eng.wait_ge(sem["kv_ev"], after["kv_ev"](i, 2))
                eng.wait_ge(sem["kvb_ev"], after["kvb_ev"](i, 0))
                for bank, k in ((3, b.k_cos), (5, b.k_sin)):
                    for e in range(4):
                        ins = eng.matmul(psum[bank][:, e * P:(e + 1) * P], k[:, e, :],
                                         b.kv[:, e, P:2 * P], start=True, stop=True)
                ins.then_inc(sem["kvb_ps"], 1)
                if more:
                    pe_transpose_front(eng, l, i + 1, 4)
                eng.wait_ge(sem["kvb_ev"], after["kvb_ev"](i, 1))
                eng.wait_ge(sem["qcs"], after["qcs"](i, 1))
                eng.wait_ge(sem["tail_read"], after["tail_read"](i, 0))
                for e in range(4):
                    eng.matmul(psum[6][:, e * P:(e + 1) * P], b.q_cos[:, e, :], b.kv_cos[:, e, :],
                               start=True, stop=False)
                    ins = eng.matmul(psum[6][:, e * P:(e + 1) * P], b.q_sin[:, e, :],
                                     b.kv_sin[:, e, :], start=False, stop=True)
                ins.then_inc(sem["o_ps"], 1)
                if more:
                    front(i + 1)

            run_steps(eng, batch // 4, first, body)

        def act_cosine(eng, l):
            after, b = afters[l], CosineBuffers()

            def q_out(j):
                eng.wait_ge(sem["q_ps"], after["q_ps"](j, 1))
                eng.wait_ge(sem["qcs"], after["qcs"](j, 0))
                eng.activation(b.q, quads(2), ACT.Relu, bias=weight(l, "bq")).then_inc(sem["q_ev"], 1)

            def front(j):
                act_front_out(eng, l, j, 4)
                q_out(j)

            def body(i, more):
                if more:
                    front(i + 1)

            run_steps(eng, batch // 4, front, body)

        def dve_cosine(eng, l):
            after, b = afters[l], CosineBuffers()

            def kv_out(j):
                bias = weight(l, "bkv")
                for pair in range(2):
                    eng.wait_ge(sem["kv_ps"], after["kv_ps"](j, pair + 1))
                    eng.tensor_tensor(b.kv[:, 2 * pair:2 * pair + 2, :],
                                      psum[pair][:, :].rearrange("p (e n) -> p e n", e=2),
                                      bcast(bias, 1, 2), ALU.add).then_inc(sem["kv_ev"], 1)
                eng.wait_ge(sem["kv_ev"], after["kv_ev"](j, 2))
                eng.tensor_scalar(b.k_cos, b.kv[:, :, 0:P], 0.0, const("cos_col"), ALU.max, ALU.mult)
                eng.tensor_scalar(b.k_sin, b.kv[:, :, 0:P], 0.0, const("sin_col"), ALU.max, ALU.mult)\
                   .then_inc(sem["kcs"], 1)

            def q_weights(j):
                eng.wait_ge(sem["q_ev"], after["q_ev"](j, 1))
                eng.tensor_tensor(b.q_cos, b.q, bcast(const("cos_row"), 1, 4), ALU.mult)
                eng.tensor_tensor(b.q_sin, b.q, bcast(const("sin_row"), 1, 4), ALU.mult)\
                   .then_inc(sem["qcs"], 1)

            def front(j):
                dve_front_norm(eng, l, j)
                kv_out(j)
                q_weights(j)

            def tail_add(i):
                eng.wait_ge(sem["o_ps"], after["o_ps"](i, 1))
                dve_tail_add(eng, l, i, quads(6))

            def tail(i):
                tail_add(i)
                dve_tail_stats(eng, l, i)
                dve_tail_norm(eng, l, i)

            def body(i, before, more):
                if before:
                    tail_add(i - 1)
                if more:
                    dve_front_norm(eng, l, i + 1)
                eng.wait_ge(sem["kvb_ps"], after["kvb_ps"](i, 1))
                diagonal = bcast(const("diagonal"), 1, 4)
                eng.tensor_tensor(b.kv_cos, quads(3), diagonal, ALU.mult)
                eng.tensor_tensor(b.kv_sin, quads(5), diagonal, ALU.mult).then_inc(sem["kvb_ev"], 1)
                if before:
                    dve_tail_stats(eng, l, i - 1)
                if more:
                    kv_out(i + 1)
                    q_weights(i + 1)
                if before:
                    dve_tail_norm(eng, l, i - 1)

            run_tailed(eng, batch // 4, front, body, tail)

        @block.tensor
        def _(eng):
            for l, p in enumerate(parts):
                part_start(eng, l)
                {"attention": pe_attention, "narrow": pe_narrow, "experts": pe_experts,
                 "single": pe_single, "cosine": pe_cosine}[p["kind"]](eng, l)

        @block.scalar
        def _(eng):
            for l, p in enumerate(parts):
                part_start(eng, l)
                {"attention": act_attention, "narrow": act_narrow, "experts": act_experts,
                 "single": act_single, "cosine": act_cosine}[p["kind"]](eng, l)

        @block.vector
        def _(eng):
            eng.wait_ge(consts_in, 32)
            eng.tensor_copy(const_bf_sb[:, :], arena[:, 0:const_bf_cols]).then_inc(consts_cast, 1)
            eng.wait_ge(x_in, 16)
            for l, p in enumerate(parts):
                part_start(eng, l)
                {"attention": dve_attention, "narrow": dve_narrow, "experts": dve_experts,
                 "single": dve_single, "cosine": dve_cosine}[p["kind"]](eng, l)

        @block.gpsimd
        def _(eng):
            for n, signal in sem.items():
                if n != "ctx_in":
                    eng.sem_inc(signal, 1)
            for e, col in eps_col.items():
                eng.memset(col[:, :], e)
            eng.memset(minus_half[:, :], -0.5).then_inc(primed, 1)
            for l, p in enumerate(parts):
                part_start(eng, l)
                {"attention": pool_attention, "narrow": pool_narrow}.get(p["kind"], pool_norms)(eng, l)



def const_arrays():
    row, col = np.arange(P)[:, None], np.arange(P)[None, :]
    theta = (np.float32(np.pi / 2) * np.arange(P, dtype=np.float32) / np.float32(P)).astype(np.float32)
    cos, sin = np.cos(theta).astype(np.float32), np.sin(theta).astype(np.float32)
    f = {"ident": row == col, "lower": col <= row, "heads16": row // 8 == np.arange(16),
         "heads8": row // 16 == np.arange(8), "heads4": row // 32 == np.arange(4),
         "heads2": row // 64 == np.arange(2), "diagonal": row // 8 == col // 8,
         "iota": np.broadcast_to(np.arange(8), (P, 8)),
         "cos_row": np.broadcast_to(cos, (P, P)), "sin_row": np.broadcast_to(sin, (P, P)),
         "cos_col": cos[:, None], "sin_col": sin[:, None]}
    causal = np.where(col <= row, 0.0, NEG)
    window = np.where((col <= row) & (col > row - 32), 0.0, NEG)
    g = {"ident": row == col, "causal": causal, "window": window}
    return (np.concatenate([np.asarray(f[n], np.float32) for n, _ in CONSTS], 1),
            np.concatenate([np.asarray(g[n], np.float32) for n, _ in CONSTS_BF], 1))


def weight_arrays(name, a):
    def rows(w):
        return w.reshape(-1, P, w.shape[1]).transpose(1, 0, 2).reshape(P, -1)

    def per_row(v):
        return v.reshape(-1, P).T

    def wide(v):
        return np.broadcast_to(v[None, :], (P, v.size))

    def col(v):
        return v[:, None]

    def projected(w):
        return w.transpose(1, 0, 2).reshape(w.shape[1], -1)

    def moe(gate_up, down, chunks):
        ups, downs = [], []
        for (g, u), d, sizes in zip(gate_up, down, chunks):
            at = 0
            for c in sizes:
                ups += [g[at:at + c].T] + ([u[at:at + c].T] if u is not None else [])
                downs.append(np.pad(d[:, at:at + c].T, ((0, P - c), (0, 0))))
                at += c
        return dict(up=np.concatenate(ups, 1), down=np.concatenate(downs, 1))

    chunks = {p["name"]: p.get("chunks") for p in PARTS}[name]
    if name == "L0_attn":
        return dict(wqkv=a["L0_attn_W_qkv"], wo=a["L0_attn_W_out"],
                    ln_g=wide(a["L0_xattn_ln1_g"]), ln_b=wide(a["L0_xattn_ln1_b"]))
    if name in ("L0_self", "L0_cross"):
        t = "L0_xattn_a1_" if name == "L0_self" else "L0_xattn_a2_"
        w = dict(wq=projected(a[t + "wq"]), wk=projected(a[t + "wk"]), wv=projected(a[t + "wv"]),
                 wo=rows(a[t + "li1_w"]), bo=wide(a[t + "li1_b"]), gx=col(a[t + "lnx_g"]),
                 bx=col(a[t + "lnx_b"]), gy=col(a[t + "lny_g"]), by=col(a[t + "lny_b"]))
        return w
    if name in ("L0_mlp1", "L0_mlp2"):
        t = "L0_xattn_a1_" if name == "L0_mlp1" else "L0_xattn_a2_"
        w = dict(up=a[t + "li2_w"], down=rows(a[t + "li3_w"]), bh=per_row(a[t + "li2_b"]),
                 bo=wide(a[t + "li3_b"]), gx=col(a[t + "ln3_g"]), bx=col(a[t + "ln3_b"]))
        if name == "L0_mlp1":
            w.update(ln_g=wide(a["L0_xattn_ln2_g"]), ln_b=wide(a["L0_xattn_ln2_b"]))
        return w
    if name == "L0_ffn":
        gu, inner = a["L0_ffn_experts_gate_up"], a["L0_ffn_experts_gate_up"].shape[1] // 2
        w = moe([(e[:inner], e[inner:]) for e in gu] + [(a["L0_ffn_shared_gate_w"], a["L0_ffn_shared_up_w"])],
                list(a["L0_ffn_experts_down"]) + [a["L0_ffn_shared_down_w"]], chunks)
        w["gate"] = np.concatenate([a["L0_ffn_gate_w"], a["L0_ffn_shared_expert_gate_w"]], 0).T
        return w
    if name == "L1_attn":
        return dict(wqkv=a["L1_attn_w_attn"].T, wo=a["L1_attn_w_proj"].T,
                    bqkv=per_row(a["L1_attn_b_attn"]), bo=wide(a["L1_attn_b_proj"]))
    if name == "L1_mlp":
        return dict(up=a["L1_attn_w_fc"].T, down=rows(a["L1_attn_w_mlp_proj"].T),
                    bh=per_row(a["L1_attn_b_fc"]), bo=wide(a["L1_attn_b_mlp_proj"]))
    if name == "L1_cross":
        return dict(wq=a["L1_xattn_Wq"], wk=a["L1_xattn_Wk"], wv=a["L1_xattn_Wv"], wo=rows(a["L1_xattn_Wo"]),
                    bo=wide(a["L1_xattn_bo"]))
    if name == "L1_ffn":
        w = moe(list(zip(a["L1_ffn_W1"], a["L1_ffn_W2"])), a["L1_ffn_W3"], chunks)
        return dict(w, gate=a["L1_ffn_gate_w"].T, gx=col(a["L1_ffn_rms_w"]))
    if name == "L2_attn":
        return dict(wq=a["L2_attn_Wq"].T, wk=a["L2_attn_Wk"].T,
                    wv=a["L2_attn_Wv"].T, wo=rows(a["L2_attn_Wo"].T))
    if name in ("L2_cross", "L3_cross"):
        t = name[:2] + "_xattn_"
        return dict(wq=a[t + "Wq"], wk=a[t + "Wk"], wv=a[t + "Wv"], bq=col(a[t + "bq"]),
                    bk=col(a[t + "bk"]), bv=wide(a[t + "bv"]))
    if name == "L2_ffn":
        inner = a["L2_ffn_w1"].shape[1] // 2
        w = moe([(e[:inner], e[inner:]) for e in a["L2_ffn_w1"]], a["L2_ffn_w2"], chunks)
        return dict(w, gate=a["L2_ffn_router_w"].T)
    if name == "L3_attn":
        return dict(wq=a["L3_attn_Wq"].T,
                    wkv=np.concatenate([a["L3_attn_Wk"].T, a["L3_attn_Wv"].T], 1),
                    bq=col(a["L3_attn_bq"]),
                    bkv=wide(np.concatenate([a["L3_attn_bk"], a["L3_attn_bv"]])))
    if name == "L3_ffn":
        w = moe([(e, None) for e in a["L3_ffn_w1"]], a["L3_ffn_w2"], chunks)
        return dict(w, gate=a["L3_ffn_router_w"].T)
    raise ValueError(name)


def weight_block(p, a):
    w = weight_arrays(p["name"], a)
    fields = []
    for name, r, c in p["weights"]:
        assert w[name].shape == (r, c), (p["name"], name, w[name].shape, r, c)
        fields.append(np.pad(w[name], ((0, P - r), (0, 0))))
    return np.ascontiguousarray(np.concatenate(fields, 1))


def kernel(**inputs):
    import concourse.bacc as bacc
    from concourse.bass_utils import run_bass_kernel_spmd

    a = {k: np.asarray(v) for k, v in inputs.items()}
    x, ctx = a["x"], a["ctx_512"]
    batch = x.shape[0]
    consts, consts_bf = const_arrays()
    arrays = {"in_x": np.ascontiguousarray(x), "in_ctx": np.ascontiguousarray(ctx),
              "in_ctx_t": np.ascontiguousarray(ctx.transpose(2, 0, 1).reshape(CTX, -1)),
              "in_consts": consts, "in_consts_bf": consts_bf}
    for p in PARTS:
        arrays[f"in_w_{p['name']}"] = weight_block(p, a)

    nc = bacc.Bacc("TRN2", target_bir_lowering=False, num_devices=1)
    dram = {n: nc.dram_tensor(n, v.shape, mybir.dt.from_np(v.dtype), kind="ExternalInput").ap()
            for n, v in arrays.items()}
    out = nc.dram_tensor("out", x.shape, F32, kind="ExternalOutput").ap()
    build_program(nc, dram["in_x"], dram["in_ctx"], dram["in_ctx_t"], dram["in_consts"],
                  dram["in_consts_bf"], [dram[f"in_w_{p['name']}"] for p in PARTS], out, PARTS, batch)
    return run_bass_kernel_spmd(nc, [arrays], core_ids=[0]).results[0]["out"]
```
